# Optimizing a Trainium2 kernel written in Bass

```python
import numpy as np
import jax
import jax.numpy as jnp

def _softmax(x, axis=-1):
    return jax.nn.softmax(x, axis=axis)

def _gelu(x):
    return jax.nn.gelu(x, approximate=True)

def _silu(x):
    return jax.nn.silu(x)

def _sigmoid(x):
    return jax.nn.sigmoid(x)

def _layernorm(x, axis=-1, eps=1e-05):
    m = jnp.mean(x, axis=axis, keepdims=True)
    v = jnp.var(x, axis=axis, keepdims=True)
    return (x - m) / jnp.sqrt(v + eps)

def _scatter_add(tgt, idx, src, axis=0):
    return tgt.at[idx].add(src)

def _segment_sum(src, seg, n):
    return jax.ops.segment_sum(src, seg, n)
kernel_name = 'mk_flamingo_gated_d4_seqx_r4_f0add8'

def setup_inputs(seed: int=0):
    np.random.seed(seed)
    _w = jnp.asarray

    def _rec_inputs():
        import jax
        import jax.numpy as jnp
        _rk = jax.random.key(seed)
        x = 7.22e-05 + 1 * jax.random.normal(jax.random.fold_in(_rk, 1), (8, 256, 256), jnp.float32)
        _lenS = 256 - jax.random.randint(jax.random.fold_in(_rk, 7), (8,), 0, max(1, 256 // 4) + 1, jnp.int32)
        _lenS2 = 77 - jax.random.randint(jax.random.fold_in(_rk, 8), (8,), 0, max(1, 77 // 4) + 1, jnp.int32)
        _ctx_768P = jax.random.normal(jax.random.fold_in(_rk, 11), (8, 16, 192), jnp.float32)
        _ctx_768c = jax.random.dirichlet(jax.random.fold_in(_rk, 511), 0.3 * jnp.ones((16,), jnp.float32), (8, 77))
        _ctx_768t = jnp.einsum('bsk,bkd->bsd', _ctx_768c, _ctx_768P)
        _ctx_768t = _ctx_768t * jax.lax.rsqrt(jnp.mean(jnp.square(_ctx_768t)) + 1e-12) * 0.953939
        ctx_768 = 3.88148e-05 + 0.999967 * (_ctx_768t + 0.3 * jax.random.normal(jax.random.fold_in(_rk, 611), (8, 77, 192), jnp.float32))
        _validS = jnp.arange(256)[None, :] < _lenS[:, None]
        _validS2 = jnp.arange(77)[None, :] < _lenS2[:, None]
        _causal = jnp.tril(jnp.ones((256, 256), dtype=bool))
        mask_BxS_bf1 = jnp.ones((8, 256), dtype=bool)
        mask_BxS2_bf1 = jnp.ones((8, 77), dtype=bool)
        _g = jax.random.normal(jax.random.fold_in(_rk, 9001), (2, 4), jnp.float32)
        _g = jnp.sign(_g) * jnp.maximum(jnp.abs(_g), 1.0) + (_g == 0) * 1.0
        g_xattn = _g[0]
        g_ffn = _g[1]
        return (x, ctx_768, mask_BxS_bf1, mask_BxS2_bf1, g_xattn, g_ffn)
    x, ctx_768, mask_BxS_bf1, mask_BxS2_bf1, g_xattn, g_ffn = _rec_inputs()

    def _L0_xattn_setup():
        import jax, jax.numpy as jnp
        import numpy as np
        B, T, DT, G, DV = (16, 128, 256, 144, 192)
        H, DH = (4, 32)
        INNER = H * DH
        HID = 4 * DT
        N_STATE = 64
        K_TOP = 32

        def layernorm(x, g, b, eps=1e-05):
            m = x.mean(-1, keepdims=True)
            v = x.var(-1, keepdims=True)
            return (x - m) * jax.lax.rsqrt(v + eps) * g + b

        def s4d(x, log_dt, A_re, A_im, C_re, C_im, D_skip):
            Bb, L, D = x.shape
            dt = jnp.exp(log_dt)
            A = A_re + 1j * A_im
            C = C_re + 1j * C_im
            dtA = dt[:, None] * A
            dC = C * (jnp.exp(dtA) - 1.0) / A
            powers = jnp.exp(dtA[:, :, None] * jnp.arange(L))
            K = 2.0 * jnp.einsum('dn,dnl->dl', dC, powers).real
            n = 2 * L
            Kf = jnp.fft.rfft(K, n=n, axis=-1)
            xf = jnp.fft.rfft(x, n=n, axis=1)
            y = jnp.fft.irfft(xf * Kf.T[None], n=n, axis=1)[:, :L]
            return y + x * D_skip
        key = jax.random.key(seed)
        ks = jax.random.split(key, 16)
        s = 0.02
        inp = {'x_text': jax.random.normal(ks[0], (B, T, DT), jnp.float32), 'x_vision': jax.random.normal(ks[1], (B, G, DV), jnp.float32), 'text_mask': jnp.ones((B, T), bool), 'vision_mask': jnp.ones((B, G), bool), 'Wq': jax.random.normal(ks[2], (DT, INNER), jnp.float32) * s, 'Wk': jax.random.normal(ks[3], (DV, INNER), jnp.float32) * s, 'Wv': jax.random.normal(ks[4], (DV, DT), jnp.float32) * s, 'W_film_in': jax.random.normal(ks[5], (DT, 2 * DT), jnp.float32) * s, 'b_film_in': jnp.zeros((2 * DT,), jnp.float32), 'W_film_out': jax.random.normal(ks[6], (DT, 2 * DT), jnp.float32) * s, 'b_film_out': jnp.zeros((2 * DT,), jnp.float32), 'g_norm_in': jnp.ones((DT,), jnp.float32), 'b_norm_in': jnp.zeros((DT,), jnp.float32), 'g_norm_out': jnp.ones((DT,), jnp.float32), 'b_norm_out': jnp.zeros((DT,), jnp.float32), 'g_ffn': jnp.ones((DT,), jnp.float32), 'b_ffn': jnp.zeros((DT,), jnp.float32), 'W1': jax.random.normal(ks[7], (DT, HID), jnp.float32) * s, 'b1': jnp.zeros((HID,), jnp.float32), 'W2': jax.random.normal(ks[8], (HID, DT), jnp.float32) * s, 'b2': jnp.zeros((DT,), jnp.float32), 'log_dt': jnp.log(0.001) + jax.random.uniform(ks[9], (DT,), jnp.float32) * (jnp.log(0.1) - jnp.log(0.001)), 'A_re': -0.5 * jnp.ones((DT, N_STATE), jnp.float32), 'A_im': jnp.tile(jnp.pi * jnp.arange(N_STATE, dtype=jnp.float32), (DT, 1)), 'C_re': jax.random.normal(ks[10], (DT, N_STATE), jnp.float32) * 0.5 ** 0.5, 'C_im': jax.random.normal(ks[11], (DT, N_STATE), jnp.float32) * 0.5 ** 0.5, 'D_skip': jax.random.normal(ks[12], (DT,), jnp.float32), 'mod_gate': jnp.array(0.5, jnp.float32)}
        return inp
    _L0_xattn_all = _L0_xattn_setup()
    _L0_xattn_in = {k: v for k, v in _L0_xattn_all.items() if k in ('Wq', 'Wk', 'Wv', 'W_film_in', 'b_film_in', 'W_film_out', 'b_film_out', 'g_norm_in', 'b_norm_in', 'g_norm_out', 'b_norm_out', 'g_ffn', 'b_ffn', 'W1', 'b1', 'W2', 'b2', 'log_dt', 'A_re', 'A_im', 'C_re', 'C_im', 'D_skip', 'mod_gate')}
    del _L0_xattn_all

    def _L0_ffn_setup():
        import jax, jax.numpy as jnp
        import numpy as np
        B, S, D, H, E, K = (4, 512, 256, 1024, 8, 2)
        CAPACITY_FACTOR = 1.5
        C = int(CAPACITY_FACTOR * B * S * K / E)
        key = jax.random.key(seed)
        ks = jax.random.split(key, 6)
        x = jax.random.normal(ks[0], (B, S, D), dtype=jnp.float32)
        w_router = jax.random.normal(ks[1], (D, E), dtype=jnp.float32) * 0.02
        w1 = jax.random.normal(ks[2], (E, D, H), dtype=jnp.float32) * 0.02
        b1 = jnp.zeros((E, H), dtype=jnp.float32)
        w2 = jax.random.normal(ks[3], (E, H, D), dtype=jnp.float32) * 0.02
        b2 = jnp.zeros((E, D), dtype=jnp.float32)
        return {'x': x, 'w_router': w_router, 'w1': w1, 'b1': b1, 'w2': w2, 'b2': b2}
    _L0_ffn_all = _L0_ffn_setup()
    _L0_ffn_in = {k: v for k, v in _L0_ffn_all.items() if k in ('w_router', 'w1', 'b1', 'w2', 'b2')}
    del _L0_ffn_all

    def _L1_xattn_setup():
        import jax, jax.numpy as jnp
        import numpy as np
        N_HEADS = 16
        D_HEAD = 64
        key = jax.random.key(seed)
        ks = jax.random.split(key, 7)
        B, SQ, SKV = (2, 512, 512)
        D_MODEL, D_COND, D_ATTN = (256, 192, N_HEADS * D_HEAD)
        return {'x': jax.random.normal(ks[0], (B, SQ, D_MODEL), jnp.float32), 'cond': jax.random.normal(ks[1], (B, SKV, D_COND), jnp.float32), 'w_q': jax.random.normal(ks[2], (D_MODEL, D_ATTN), jnp.float32) * D_MODEL ** (-0.5), 'w_k': jax.random.normal(ks[3], (D_COND, D_ATTN), jnp.float32) * D_COND ** (-0.5), 'w_v': jax.random.normal(ks[4], (D_COND, D_ATTN), jnp.float32) * D_COND ** (-0.5), 'w_out': jax.random.normal(ks[5], (D_ATTN, D_MODEL), jnp.float32) * D_ATTN ** (-0.5), 'b_out': jnp.zeros((D_MODEL,), jnp.float32)}
    _L1_xattn_all = _L1_xattn_setup()
    _L1_xattn_in = {k: v for k, v in _L1_xattn_all.items() if k in ('w_q', 'w_k', 'w_v', 'w_out', 'b_out')}
    del _L1_xattn_all

    def _L1_ffn_setup():
        import jax, jax.numpy as jnp
        import numpy as np
        from jax import lax
        D = 256
        H = 1024
        E = 8
        TOPK = 2
        key = jax.random.key(seed)
        ks = jax.random.split(key, 7)
        s = 0.02
        return {'x': jax.random.normal(ks[0], (2, 512, D), dtype=jnp.float32), 'W1': jax.random.normal(ks[1], (E, D, H), dtype=jnp.float32) * s, 'b1': jnp.zeros((E, H), dtype=jnp.float32), 'W2': jax.random.normal(ks[2], (E, H, D), dtype=jnp.float32) * s, 'b2': jnp.zeros((E, D), dtype=jnp.float32), 'Wr': jax.random.normal(ks[3], (D, E), dtype=jnp.float32) * s, 'br': jnp.zeros((E,), dtype=jnp.float32)}
    _L1_ffn_all = _L1_ffn_setup()
    _L1_ffn_in = {k: v for k, v in _L1_ffn_all.items() if k in ('W1', 'b1', 'W2', 'b2', 'Wr', 'br')}
    del _L1_ffn_all

    def _L2_xattn_setup():
        import jax, jax.numpy as jnp
        import numpy as np
        HEADS = 8
        DIM_HEAD = 128
        ATTN_MATRIX_SCALE = 1.5
        SCALE = DIM_HEAD ** (-0.5)

        def _split_heads(t):
            b, n, _ = t.shape
            t = t.reshape(b, n, HEADS, DIM_HEAD)
            return t.transpose(2, 0, 1, 3).reshape(HEADS, b * n, DIM_HEAD)
        key = jax.random.key(seed)
        ks = jax.random.split(key, 7)
        b, n, m = (2, 512, 512)
        qd, cd, inner = (256, 192, HEADS * DIM_HEAD)
        x = jax.random.normal(ks[0], (b, n, qd), dtype=jnp.float32)
        context = jax.random.normal(ks[1], (b, m, cd), dtype=jnp.float32)
        Wq = jax.random.normal(ks[2], (qd, inner), dtype=jnp.float32) * qd ** (-0.5)
        Wk = jax.random.normal(ks[3], (cd, inner), dtype=jnp.float32) * cd ** (-0.5)
        Wv = jax.random.normal(ks[4], (cd, inner), dtype=jnp.float32) * cd ** (-0.5)
        Wout = jax.random.normal(ks[5], (inner, qd), dtype=jnp.float32) * inner ** (-0.5)
        bout = jnp.zeros((qd,), dtype=jnp.float32)
        return {'x': x, 'context': context, 'Wq': Wq, 'Wk': Wk, 'Wv': Wv, 'Wout': Wout, 'bout': bout}
    _L2_xattn_all = _L2_xattn_setup()
    _L2_xattn_in = {k: v for k, v in _L2_xattn_all.items() if k in ('Wq', 'Wk', 'Wv', 'Wout', 'bout')}
    del _L2_xattn_all

    def _L2_ffn_setup():
        import jax, jax.numpy as jnp
        import numpy as np
        H = 256
        I = 704
        E = 8
        TOP_K = 2

        def _moe(hidden_states, router_w, gate_w, up_w, down_w):
            B, S, Hd = hidden_states.shape
            x = hidden_states.reshape(-1, Hd)
            logits = x @ router_w.T
            probs = jax.nn.softmax(logits.astype(jnp.float32), axis=-1)
            top_w, top_idx = jax.lax.top_k(probs, TOP_K)
            top_w = top_w.astype(x.dtype)
            onehot = jax.nn.one_hot(top_idx, E, dtype=x.dtype)
            w_te = jnp.einsum('tk,tke->te', top_w, onehot)
            g = jnp.einsum('th,eih->tei', x, gate_w)
            u = jnp.einsum('th,eih->tei', x, up_w)
            h = jax.nn.silu(g) * u
            y = jnp.einsum('tei,ehi,te->th', h, down_w, w_te)
            return y.reshape(B, S, Hd)
        key = jax.random.key(seed)
        ks = jax.random.split(key, 5)
        s = 0.02
        return {'hidden_states': jax.random.normal(ks[0], (2, 256, H), dtype=jnp.float32), 'router_w': jax.random.normal(ks[1], (E, H), dtype=jnp.float32) * s, 'gate_w': jax.random.normal(ks[2], (E, I, H), dtype=jnp.float32) * s, 'up_w': jax.random.normal(ks[3], (E, I, H), dtype=jnp.float32) * s, 'down_w': jax.random.normal(ks[4], (E, H, I), dtype=jnp.float32) * s}
    _L2_ffn_all = _L2_ffn_setup()
    _L2_ffn_in = {k: v for k, v in _L2_ffn_all.items() if k in ('router_w', 'gate_w', 'up_w', 'down_w')}
    del _L2_ffn_all

    def _L3_xattn_setup():
        import jax, jax.numpy as jnp
        import numpy as np
        HEADS = 8
        DIM_HEAD = 64
        SCALE = DIM_HEAD ** (-0.5)
        key = jax.random.key(seed)
        ks = jax.random.split(key, 7)
        B, Nq, Nc = (4, 512, 512)
        Dq, Dc = (256, 192)
        inner = HEADS * DIM_HEAD
        x = jax.random.normal(ks[0], (B, Nq, Dq), dtype=jnp.float32)
        context = jax.random.normal(ks[1], (B, Nc, Dc), dtype=jnp.float32)
        Wq = jax.random.normal(ks[2], (Dq, inner), dtype=jnp.float32) * Dq ** (-0.5)
        Wk = jax.random.normal(ks[3], (Dc, inner), dtype=jnp.float32) * Dc ** (-0.5)
        Wv = jax.random.normal(ks[4], (Dc, inner), dtype=jnp.float32) * Dc ** (-0.5)
        Wo = jax.random.normal(ks[5], (inner, Dq), dtype=jnp.float32) * inner ** (-0.5)
        bo = jax.random.normal(ks[6], (Dq,), dtype=jnp.float32) * 0.01
        return {'x': x, 'context': context, 'Wq': Wq, 'Wk': Wk, 'Wv': Wv, 'Wo': Wo, 'bo': bo}
    _L3_xattn_all = _L3_xattn_setup()
    _L3_xattn_in = {k: v for k, v in _L3_xattn_all.items() if k in ('Wq', 'Wk', 'Wv', 'Wo', 'bo')}
    del _L3_xattn_all

    def _L3_ffn_setup():
        import jax, jax.numpy as jnp
        import numpy as np
        DIM = 256
        MOE_HID = 128
        SHARED_HID = 512
        N_EXPERTS = 16
        TOP_K = 2
        NORM_TOPK_PROB = True
        key = jax.random.key(seed)
        ks = jax.random.split(key, 9)
        s = 0.02
        x = jax.random.normal(ks[0], (2, 256, DIM), dtype=jnp.float32)
        Wg = jax.random.normal(ks[1], (N_EXPERTS, DIM), dtype=jnp.float32) * s
        We_gate = jax.random.normal(ks[2], (N_EXPERTS, MOE_HID, DIM), dtype=jnp.float32) * s
        We_up = jax.random.normal(ks[3], (N_EXPERTS, MOE_HID, DIM), dtype=jnp.float32) * s
        We_down = jax.random.normal(ks[4], (N_EXPERTS, DIM, MOE_HID), dtype=jnp.float32) * s
        Ws_gate = jax.random.normal(ks[5], (SHARED_HID, DIM), dtype=jnp.float32) * s
        Ws_up = jax.random.normal(ks[6], (SHARED_HID, DIM), dtype=jnp.float32) * s
        Ws_down = jax.random.normal(ks[7], (DIM, SHARED_HID), dtype=jnp.float32) * s
        Wsg = jax.random.normal(ks[8], (1, DIM), dtype=jnp.float32) * s
        return {'x': x, 'Wg': Wg, 'We_gate': We_gate, 'We_up': We_up, 'We_down': We_down, 'Ws_gate': Ws_gate, 'Ws_up': Ws_up, 'Ws_down': Ws_down, 'Wsg': Wsg}
    _L3_ffn_all = _L3_ffn_setup()
    _L3_ffn_in = {k: v for k, v in _L3_ffn_all.items() if k in ('Wg', 'We_gate', 'We_up', 'We_down', 'Ws_gate', 'Ws_up', 'Ws_down', 'Wsg')}
    del _L3_ffn_all
    return {'x': x, 'ctx_768': ctx_768, 'mask_BxS_bf1': mask_BxS_bf1, 'mask_BxS2_bf1': mask_BxS2_bf1, 'g_xattn': g_xattn, 'g_ffn': g_ffn, 'L0_xattn_Wq': _L0_xattn_in['Wq'], 'L0_xattn_Wk': _L0_xattn_in['Wk'], 'L0_xattn_Wv': _L0_xattn_in['Wv'], 'L0_xattn_W_film_in': _L0_xattn_in['W_film_in'], 'L0_xattn_b_film_in': _L0_xattn_in['b_film_in'], 'L0_xattn_W_film_out': _L0_xattn_in['W_film_out'], 'L0_xattn_b_film_out': _L0_xattn_in['b_film_out'], 'L0_xattn_g_norm_in': _L0_xattn_in['g_norm_in'], 'L0_xattn_b_norm_in': _L0_xattn_in['b_norm_in'], 'L0_xattn_g_norm_out': _L0_xattn_in['g_norm_out'], 'L0_xattn_b_norm_out': _L0_xattn_in['b_norm_out'], 'L0_xattn_g_ffn': _L0_xattn_in['g_ffn'], 'L0_xattn_b_ffn': _L0_xattn_in['b_ffn'], 'L0_xattn_W1': _L0_xattn_in['W1'], 'L0_xattn_b1': _L0_xattn_in['b1'], 'L0_xattn_W2': _L0_xattn_in['W2'], 'L0_xattn_b2': _L0_xattn_in['b2'], 'L0_xattn_log_dt': _L0_xattn_in['log_dt'], 'L0_xattn_A_re': _L0_xattn_in['A_re'], 'L0_xattn_A_im': _L0_xattn_in['A_im'], 'L0_xattn_C_re': _L0_xattn_in['C_re'], 'L0_xattn_C_im': _L0_xattn_in['C_im'], 'L0_xattn_D_skip': _L0_xattn_in['D_skip'], 'L0_xattn_mod_gate': _L0_xattn_in['mod_gate'], 'L0_ffn_w_router': _L0_ffn_in['w_router'], 'L0_ffn_w1': _L0_ffn_in['w1'], 'L0_ffn_b1': _L0_ffn_in['b1'], 'L0_ffn_w2': _L0_ffn_in['w2'], 'L0_ffn_b2': _L0_ffn_in['b2'], 'L1_xattn_w_q': _L1_xattn_in['w_q'], 'L1_xattn_w_k': _L1_xattn_in['w_k'], 'L1_xattn_w_v': _L1_xattn_in['w_v'], 'L1_xattn_w_out': _L1_xattn_in['w_out'], 'L1_xattn_b_out': _L1_xattn_in['b_out'], 'L1_ffn_W1': _L1_ffn_in['W1'], 'L1_ffn_b1': _L1_ffn_in['b1'], 'L1_ffn_W2': _L1_ffn_in['W2'], 'L1_ffn_b2': _L1_ffn_in['b2'], 'L1_ffn_Wr': _L1_ffn_in['Wr'], 'L1_ffn_br': _L1_ffn_in['br'], 'L2_xattn_Wq': _L2_xattn_in['Wq'], 'L2_xattn_Wk': _L2_xattn_in['Wk'], 'L2_xattn_Wv': _L2_xattn_in['Wv'], 'L2_xattn_Wout': _L2_xattn_in['Wout'], 'L2_xattn_bout': _L2_xattn_in['bout'], 'L2_ffn_router_w': _L2_ffn_in['router_w'], 'L2_ffn_gate_w': _L2_ffn_in['gate_w'], 'L2_ffn_up_w': _L2_ffn_in['up_w'], 'L2_ffn_down_w': _L2_ffn_in['down_w'], 'L3_xattn_Wq': _L3_xattn_in['Wq'], 'L3_xattn_Wk': _L3_xattn_in['Wk'], 'L3_xattn_Wv': _L3_xattn_in['Wv'], 'L3_xattn_Wo': _L3_xattn_in['Wo'], 'L3_xattn_bo': _L3_xattn_in['bo'], 'L3_ffn_Wg': _L3_ffn_in['Wg'], 'L3_ffn_We_gate': _L3_ffn_in['We_gate'], 'L3_ffn_We_up': _L3_ffn_in['We_up'], 'L3_ffn_We_down': _L3_ffn_in['We_down'], 'L3_ffn_Ws_gate': _L3_ffn_in['Ws_gate'], 'L3_ffn_Ws_up': _L3_ffn_in['Ws_up'], 'L3_ffn_Ws_down': _L3_ffn_in['Ws_down'], 'L3_ffn_Wsg': _L3_ffn_in['Wsg']}

def reference(x, ctx_768, mask_BxS_bf1, mask_BxS2_bf1, g_xattn, g_ffn, L0_xattn_Wq, L0_xattn_Wk, L0_xattn_Wv, L0_xattn_W_film_in, L0_xattn_b_film_in, L0_xattn_W_film_out, L0_xattn_b_film_out, L0_xattn_g_norm_in, L0_xattn_b_norm_in, L0_xattn_g_norm_out, L0_xattn_b_norm_out, L0_xattn_g_ffn, L0_xattn_b_ffn, L0_xattn_W1, L0_xattn_b1, L0_xattn_W2, L0_xattn_b2, L0_xattn_log_dt, L0_xattn_A_re, L0_xattn_A_im, L0_xattn_C_re, L0_xattn_C_im, L0_xattn_D_skip, L0_xattn_mod_gate, L0_ffn_w_router, L0_ffn_w1, L0_ffn_b1, L0_ffn_w2, L0_ffn_b2, L1_xattn_w_q, L1_xattn_w_k, L1_xattn_w_v, L1_xattn_w_out, L1_xattn_b_out, L1_ffn_W1, L1_ffn_b1, L1_ffn_W2, L1_ffn_b2, L1_ffn_Wr, L1_ffn_br, L2_xattn_Wq, L2_xattn_Wk, L2_xattn_Wv, L2_xattn_Wout, L2_xattn_bout, L2_ffn_router_w, L2_ffn_gate_w, L2_ffn_up_w, L2_ffn_down_w, L3_xattn_Wq, L3_xattn_Wk, L3_xattn_Wv, L3_xattn_Wo, L3_xattn_bo, L3_ffn_Wg, L3_ffn_We_gate, L3_ffn_We_up, L3_ffn_We_down, L3_ffn_Ws_gate, L3_ffn_Ws_up, L3_ffn_Ws_down, L3_ffn_Wsg):
    import jax
    import jax.numpy as jnp

    def _L0_xattn_ref(x_text, x_vision, text_mask, vision_mask, Wq, Wk, Wv, W_film_in, b_film_in, W_film_out, b_film_out, g_norm_in, b_norm_in, g_norm_out, b_norm_out, g_ffn, b_ffn, W1, b1, W2, b2, log_dt, A_re, A_im, C_re, C_im, D_skip, mod_gate):
        import jax, jax.numpy as jnp
        import numpy as np
        B, T, DT, G, DV = (16, 128, 256, 144, 192)
        H, DH = (4, 32)
        INNER = H * DH
        HID = 4 * DT
        N_STATE = 64
        K_TOP = 32

        def layernorm(x, g, b, eps=1e-05):
            m = x.mean(-1, keepdims=True)
            v = x.var(-1, keepdims=True)
            return (x - m) * jax.lax.rsqrt(v + eps) * g + b

        def s4d(x, log_dt, A_re, A_im, C_re, C_im, D_skip):
            Bb, L, D = x.shape
            dt = jnp.exp(log_dt)
            A = A_re + 1j * A_im
            C = C_re + 1j * C_im
            dtA = dt[:, None] * A
            dC = C * (jnp.exp(dtA) - 1.0) / A
            powers = jnp.exp(dtA[:, :, None] * jnp.arange(L))
            K = 2.0 * jnp.einsum('dn,dnl->dl', dC, powers).real
            n = 2 * L
            Kf = jnp.fft.rfft(K, n=n, axis=-1)
            xf = jnp.fft.rfft(x, n=n, axis=1)
            y = jnp.fft.irfft(xf * Kf.T[None], n=n, axis=1)[:, :L]
            return y + x * D_skip
        Bb, Tt, D = x_text.shape
        Gg = x_vision.shape[1]
        Q = (x_text @ Wq).reshape(Bb, Tt, H, DH)
        K = (x_vision @ Wk).reshape(Bb, Gg, H, DH)
        scores = jnp.einsum('bthd,bghd->bhtg', Q, K) / np.sqrt(DH).astype(np.float32)
        scores = jnp.where(vision_mask[:, None, None, :], scores, -jnp.inf)
        topv, topi = jax.lax.top_k(scores, K_TOP)
        probs = jax.nn.softmax(topv, axis=-1)
        bi = jnp.arange(Bb)[:, None, None, None]
        hi = jnp.arange(H)[None, :, None, None]
        ti = jnp.arange(Tt)[None, None, :, None]
        attn = jnp.zeros_like(scores).at[bi, hi, ti, topi].set(probs)
        attn_mean = attn.mean(axis=1)
        V = x_vision @ Wv
        c_t = jnp.einsum('btg,bgd->btd', attn_mean, V)
        c_t = c_t * text_mask[..., None]
        x = layernorm(x_text, g_norm_in, b_norm_in)
        scale_in, shift_in = jnp.split(c_t @ W_film_in + b_film_in, 2, axis=-1)
        x = x * (1.0 + mod_gate * scale_in) + mod_gate * shift_in
        y = s4d(x, log_dt, A_re, A_im, C_re, C_im, D_skip)
        scale_out, shift_out = jnp.split(c_t @ W_film_out + b_film_out, 2, axis=-1)
        y = y * (1.0 + mod_gate * scale_out) + mod_gate * shift_out
        xt = x_text + y
        h = layernorm(xt, g_ffn, b_ffn)
        h = jax.nn.gelu(h @ W1 + b1, approximate=False) @ W2 + b2
        xt = xt + h
        return layernorm(xt, g_norm_out, b_norm_out)

    def _L0_ffn_ref(x, w_router, w1, b1, w2, b2):
        import jax, jax.numpy as jnp
        import numpy as np
        B, S, D, H, E, K = (4, 512, 256, 1024, 8, 2)
        CAPACITY_FACTOR = 1.5
        C = int(CAPACITY_FACTOR * B * S * K / E)
        Bs, Ss, Ds = x.shape
        N = Bs * Ss
        xf = x.reshape(N, Ds)
        logits = xf @ w_router
        probs = jax.nn.softmax(logits, axis=-1)
        gate, eidx = jax.lax.top_k(probs, K)
        gate = gate / jnp.sum(gate, axis=-1, keepdims=True)
        oh = jax.nn.one_hot(eidx, E, dtype=jnp.float32)
        ohf = oh.reshape(N * K, E)
        pos = jnp.cumsum(ohf, axis=0) - 1.0
        posk = jnp.sum(pos * ohf, axis=-1).reshape(N, K).astype(jnp.int32)
        keep = posk < C
        gate = gate * keep.astype(gate.dtype)
        e_flat = eidx.reshape(-1)
        p_flat = jnp.where(keep, posk, 0).reshape(-1)
        contrib = (xf[:, None, :] * keep[..., None].astype(xf.dtype)).reshape(N * K, Ds)
        expert_in = jnp.zeros((E, C, Ds), dtype=xf.dtype).at[e_flat, p_flat].add(contrib)
        h = jax.nn.relu(jnp.einsum('ecd,edh->ech', expert_in, w1) + b1[:, None, :])
        expert_out = jnp.einsum('ech,eho->eco', h, w2) + b2[:, None, :]
        tok = expert_out[e_flat, p_flat].reshape(N, K, -1)
        y = jnp.sum(tok * gate[..., None], axis=1)
        return y.reshape(Bs, Ss, -1)

    def _L1_xattn_ref(x, cond, w_q, w_k, w_v, w_out, b_out):
        import jax, jax.numpy as jnp
        import numpy as np
        N_HEADS = 16
        D_HEAD = 64
        B, SQ, _ = x.shape
        SKV = cond.shape[1]
        scale = D_HEAD ** (-0.5)
        q = (x @ w_q).reshape(B, SQ, N_HEADS, D_HEAD)
        k = (cond @ w_k).reshape(B, SKV, N_HEADS, D_HEAD)
        v = (cond @ w_v).reshape(B, SKV, N_HEADS, D_HEAD)
        attn = jnp.einsum('bqhd,bkhd->bhqk', q, k) * scale
        attn = jax.nn.softmax(attn, axis=-1)
        out = jnp.einsum('bhqk,bkhd->bqhd', attn, v).reshape(B, SQ, N_HEADS * D_HEAD)
        return out @ w_out + b_out

    def _L1_ffn_ref(x, W1, b1, W2, b2, Wr, br):
        import jax, jax.numpy as jnp
        import numpy as np
        from jax import lax
        D = 256
        H = 1024
        E = 8
        TOPK = 2
        B, S, _ = x.shape
        xf = x.reshape(-1, D)
        logits = xf @ Wr + br
        topv, _ = lax.top_k(logits, TOPK)
        thresh = topv[:, TOPK - 1:TOPK]
        masked = jnp.where(logits >= thresh, logits, -jnp.inf)
        weights = jax.nn.softmax(masked, axis=-1)
        h = jax.nn.gelu(jnp.einsum('td,edh->eth', xf, W1) + b1[:, None, :], approximate=False)
        expert_out = jnp.einsum('eth,ehd->etd', h, W2) + b2[:, None, :]
        out = jnp.einsum('etd,te->td', expert_out, weights)
        return out.reshape(B, S, D)

    def _L2_xattn_ref(x, context, Wq, Wk, Wv, Wout, bout):
        import jax, jax.numpy as jnp
        import numpy as np
        HEADS = 8
        DIM_HEAD = 128
        ATTN_MATRIX_SCALE = 1.5
        SCALE = DIM_HEAD ** (-0.5)

        def _split_heads(t):
            b, n, _ = t.shape
            t = t.reshape(b, n, HEADS, DIM_HEAD)
            return t.transpose(2, 0, 1, 3).reshape(HEADS, b * n, DIM_HEAD)
        b, n, _ = x.shape
        qh = _split_heads(jnp.einsum('bnq,qi->bni', x, Wq))
        kh = _split_heads(jnp.einsum('bmc,ci->bmi', context, Wk))
        vh = _split_heads(jnp.einsum('bmc,ci->bmi', context, Wv))
        sim = jnp.einsum('hid,hjd->hij', qh, kh) * SCALE
        mean = jnp.mean(sim, axis=-1, keepdims=True)
        sim = (sim - mean) * ATTN_MATRIX_SCALE + mean
        attn = jax.nn.softmax(sim, axis=-1)
        out = jnp.einsum('hij,hjd->hid', attn, vh)
        out = out.reshape(HEADS, b, n, DIM_HEAD).transpose(1, 2, 0, 3)
        out = out.reshape(b, n, HEADS * DIM_HEAD)
        return jnp.einsum('bni,iq->bnq', out, Wout) + bout

    def _L2_ffn_ref(hidden_states, router_w, gate_w, up_w, down_w):
        import jax, jax.numpy as jnp
        import numpy as np
        H = 256
        I = 704
        E = 8
        TOP_K = 2

        def _moe(hidden_states, router_w, gate_w, up_w, down_w):
            B, S, Hd = hidden_states.shape
            x = hidden_states.reshape(-1, Hd)
            logits = x @ router_w.T
            probs = jax.nn.softmax(logits.astype(jnp.float32), axis=-1)
            top_w, top_idx = jax.lax.top_k(probs, TOP_K)
            top_w = top_w.astype(x.dtype)
            onehot = jax.nn.one_hot(top_idx, E, dtype=x.dtype)
            w_te = jnp.einsum('tk,tke->te', top_w, onehot)
            g = jnp.einsum('th,eih->tei', x, gate_w)
            u = jnp.einsum('th,eih->tei', x, up_w)
            h = jax.nn.silu(g) * u
            y = jnp.einsum('tei,ehi,te->th', h, down_w, w_te)
            return y.reshape(B, S, Hd)
        return _moe(hidden_states, router_w, gate_w, up_w, down_w)

    def _L3_xattn_ref(x, context, Wq, Wk, Wv, Wo, bo):
        import jax, jax.numpy as jnp
        import numpy as np
        HEADS = 8
        DIM_HEAD = 64
        SCALE = DIM_HEAD ** (-0.5)
        B, Nq, _ = x.shape
        q = (x @ Wq).reshape(B, Nq, HEADS, DIM_HEAD)
        k = (context @ Wk).reshape(B, context.shape[1], HEADS, DIM_HEAD)
        v = (context @ Wv).reshape(B, context.shape[1], HEADS, DIM_HEAD)
        sim = jnp.einsum('bihd,bjhd->bhij', q, k) * SCALE
        attn = jax.nn.softmax(sim, axis=-1)
        out = jnp.einsum('bhij,bjhd->bihd', attn, v)
        out = out.reshape(B, Nq, HEADS * DIM_HEAD)
        return out @ Wo + bo

    def _L3_ffn_ref(x, Wg, We_gate, We_up, We_down, Ws_gate, Ws_up, Ws_down, Wsg):
        import jax, jax.numpy as jnp
        import numpy as np
        DIM = 256
        MOE_HID = 128
        SHARED_HID = 512
        N_EXPERTS = 16
        TOP_K = 2
        NORM_TOPK_PROB = True
        B, S, D = x.shape
        xt = x.reshape(-1, D)
        gates = jax.nn.softmax(xt @ Wg.T, axis=-1)
        scores, inds = jax.lax.top_k(gates, TOP_K)
        if NORM_TOPK_PROB:
            scores = scores / jnp.sum(scores, axis=-1, keepdims=True)
        g = jnp.einsum('td,ehd->teh', xt, We_gate)
        u = jnp.einsum('td,ehd->teh', xt, We_up)
        h = jax.nn.silu(g) * u
        y_all = jnp.einsum('teh,edh->ted', h, We_down)
        y_sel = jnp.take_along_axis(y_all, inds[:, :, None], axis=1)
        y = jnp.sum(y_sel * scores[:, :, None], axis=1)
        shared = jax.nn.silu(xt @ Ws_gate.T) * (xt @ Ws_up.T) @ Ws_down.T
        y = y + jax.nn.sigmoid(xt @ Wsg.T) * shared
        return y.reshape(B, S, D)
    x = x + jnp.tanh(g_xattn[0]) * _L0_xattn_ref(_layernorm(x, axis=-1), ctx_768, mask_BxS_bf1, mask_BxS2_bf1, L0_xattn_Wq, L0_xattn_Wk, L0_xattn_Wv, L0_xattn_W_film_in, L0_xattn_b_film_in, L0_xattn_W_film_out, L0_xattn_b_film_out, L0_xattn_g_norm_in, L0_xattn_b_norm_in, L0_xattn_g_norm_out, L0_xattn_b_norm_out, L0_xattn_g_ffn, L0_xattn_b_ffn, L0_xattn_W1, L0_xattn_b1, L0_xattn_W2, L0_xattn_b2, L0_xattn_log_dt, L0_xattn_A_re, L0_xattn_A_im, L0_xattn_C_re, L0_xattn_C_im, L0_xattn_D_skip, L0_xattn_mod_gate)
    x = x + jnp.tanh(g_ffn[0]) * _L0_ffn_ref(_layernorm(x, axis=-1), L0_ffn_w_router, L0_ffn_w1, L0_ffn_b1, L0_ffn_w2, L0_ffn_b2)
    x = x + jnp.tanh(g_xattn[1]) * _L1_xattn_ref(_layernorm(x, axis=-1), ctx_768, L1_xattn_w_q, L1_xattn_w_k, L1_xattn_w_v, L1_xattn_w_out, L1_xattn_b_out)
    x = x + jnp.tanh(g_ffn[1]) * _L1_ffn_ref(_layernorm(x, axis=-1), L1_ffn_W1, L1_ffn_b1, L1_ffn_W2, L1_ffn_b2, L1_ffn_Wr, L1_ffn_br)
    x = x + jnp.tanh(g_xattn[2]) * _L2_xattn_ref(_layernorm(x, axis=-1), ctx_768, L2_xattn_Wq, L2_xattn_Wk, L2_xattn_Wv, L2_xattn_Wout, L2_xattn_bout)
    x = x + jnp.tanh(g_ffn[2]) * _L2_ffn_ref(_layernorm(x, axis=-1), L2_ffn_router_w, L2_ffn_gate_w, L2_ffn_up_w, L2_ffn_down_w)
    x = x + jnp.tanh(g_xattn[3]) * _L3_xattn_ref(_layernorm(x, axis=-1), ctx_768, L3_xattn_Wq, L3_xattn_Wk, L3_xattn_Wv, L3_xattn_Wo, L3_xattn_bo)
    x = x + jnp.tanh(g_ffn[3]) * _L3_ffn_ref(_layernorm(x, axis=-1), L3_ffn_Wg, L3_ffn_We_gate, L3_ffn_We_up, L3_ffn_We_down, L3_ffn_Ws_gate, L3_ffn_Ws_up, L3_ffn_Ws_down, L3_ffn_Wsg)
    return x

_drawn_inputs = setup_inputs


def setup_inputs(seed=0):
    import zlib

    import numpy as np

    out = dict(_drawn_inputs(seed))
    spreads = {'L0_xattn_b_film_in': (0.0, 0.1),
     'L0_xattn_b_film_out': (0.0, 0.282),
     'L0_xattn_g_norm_in': (1.0, 0.2),
     'L0_xattn_b_norm_in': (0.0, 0.1),
     'L0_xattn_g_norm_out': (1.0, 0.2),
     'L0_xattn_b_norm_out': (0.0, 0.1),
     'L0_xattn_g_ffn': (1.0, 0.6),
     'L0_xattn_b_ffn': (0.0, 0.8),
     'L0_xattn_b1': (0.0, 0.8),
     'L0_xattn_b2': (0.0, 0.31),
     'L0_xattn_A_re': (-0.5, 0.2),
     'L0_ffn_b1': (0.0, 0.509),
     'L0_ffn_b2': (0.0, 0.1),
     'L1_xattn_b_out': (0.0, 0.1),
     'L1_ffn_b1': (0.0, 0.59),
     'L1_ffn_b2': (0.0, 0.1),
     'L1_ffn_br': (0.0, 0.281),
     'L2_xattn_bout': (0.0, 0.1)}
    factors = {'g_ffn': 8.0,
     'L0_xattn_Wq': 8.0,
     'L0_xattn_Wk': 8.0,
     'L0_xattn_Wv': 3.082,
     'L0_xattn_W_film_in': 3.551,
     'L0_xattn_W_film_out': 4.751,
     'L2_ffn_router_w': 8.0,
     'L2_ffn_gate_w': 8.0,
     'L2_ffn_up_w': 8.0,
     'L2_ffn_down_w': 8.0,
     'L3_xattn_bo': 25.146,
     'L3_ffn_Wg': 8.0,
     'L3_ffn_We_gate': 8.0,
     'L3_ffn_We_up': 8.0,
     'L3_ffn_We_down': 8.0,
     'L3_ffn_Ws_gate': 8.0,
     'L3_ffn_Ws_up': 8.0,
     'L3_ffn_Ws_down': 8.0,
     'L3_ffn_Wsg': 8.0}
    for name, (base, spread) in spreads.items():
        noise = np.random.default_rng([zlib.crc32(name.encode()), seed]).standard_normal(out[name].shape)
        drawn = base * np.exp(spread * noise) if base else spread * noise
        out[name] = jnp.asarray(drawn.astype(out[name].dtype))
    for name, factor in factors.items():
        out[name] = (out[name] * factor).astype(out[name].dtype)
    return out
```

```python
import math
from contextlib import ExitStack

import concourse.bass as bass
from concourse import mybir

F32 = mybir.dt.float32
F16 = mybir.dt.float16
U32 = mybir.dt.uint32
U8 = mybir.dt.uint8
ALU = mybir.AluOpType
ACT = mybir.ActivationFunctionType
X = mybir.AxisListType.X

P = 128
B, S, D = 8, 256, 256
NT = B * S // P
KD = D // P
G, DV = 77, 192
KC, CP = 2, DV // 2
GA = B * G
EPS = 1e-5
WSCALE = 64.0
INV = 1.0 / WSCALE
NEG = -1.0e30

SLOT = 4352
NS4, LAGS = 64, S
TWO_PI = 2.0 * math.pi
SIN_SCALE = -6.2831850
ROUND = 12582912.0
CAPACITY = int(1.5 * B * S * 2 / 8)
KROW = 384

R_GIN, R_BIN, R_GF, R_BF, R_GOUT, R_BOUT = range(6)
R_FI, R_FO, NR_ = 6, 8, 10
NROW = NR_ * D

C_TRI, C_IOTA, C_K16, C_MASK, C_PH, C_PHR, C_REV, NCST = 128, 256, 272, 288, 296, 300, 304, 432
ARENA = 20680

ROUTERS = [(0, 8), (16, 8), (32, 8), (48, 17)]
NRC = 48 + 34

J_X0, J_F0, J_E0, J_X1, J_E1, J_X2, J_E2, J_X3, J_SH, J_E3 = 0, 1, 2, 10, 12, 20, 22, 30, 31, 32


def build(nc, a, out):
    ctx = ExitStack()
    with ctx:
        def sb(name, shape, dt=F32):
            return ctx.enter_context(nc.sbuf_tensor(name, shape, dt))

        def sem(name):
            return ctx.enter_context(nc.semaphore(name))

        x = sb("x_resid", [P, NT, D])
        xT = sb("xT", [P, 2, KD, B * S], F16)
        raw = sb("w_raw", [P, 2, SLOT])
        wsp = sb("w_split", [P, 2, 2, SLOT], F16)
        ctxs = sb("ctx_split", [CP, 2, KC, GA], F16)
        rws = sb("router_split", [P, 2, NRC], F16)
        b1e = sb("b1_of_expert", [P, 8])
        b1c = sb("b1_cols", [P, 136])
        b2s = sb("b2_split", [33, 17, D], F16)
        ones = sb("ones16", [P, P], F16)
        tri = sb("tri16", [P, P], F16)
        rev = sb("rev16", [P, P], F16)
        cst = sb("consts", [P, NCST])
        ident, iota = cst[:, 0:P], cst[:, C_IOTA:C_IOTA + 16]
        sc = sb("scalars", [P, 17])
        tg = sb("tanh_gates", [P, 8])
        brow = sb("bout_rows", [P, 3, D])
        wgt = sb("expert_weights", [P, NT, 17])
        st6 = sb("bn_stats", [P, NT, 6])
        mean = sb("mean", [P, NT])
        rstd = sb("rstd", [P, NT])
        sm = sb("small", [P, 8, NT])
        xn = sb("xn", [P, 4, D])
        mk8 = sb("ctx_mask_u8", [P, GA], U8)
        tm8 = sb("text_mask_u8", [P, NT], U8)
        dsk = sb("skip", [P, D // 8])
        tmk = sb("text_mask", [P, NT])
        eps_t = sb("eps", [P, 1])
        spare = sb("credit_dummy", [1, 64])
        arena = sb("arena", [P, ARENA])

        ps = ctx.enter_context(nc.psum_tensor("ps", [P, 8, 512], F32))
        kdram = nc.dram_tensor("s4_kernel", [D, KROW, 2], F16, kind="Internal").ap()

        class Area:
            def __init__(self, at=0):
                self.at = at

            def f32(self, *dims):
                n = math.prod(dims)
                v = arena[:, self.at:self.at + n]
                self.at += n
                assert self.at <= ARENA, self.at
                return shaped(v, dims)

            def f16(self, *dims):
                n = math.prod(dims)
                v = arena[:, self.at:self.at + n // 2].bitcast(F16)
                self.at += n // 2
                assert self.at <= ARENA, self.at
                return shaped(v, dims)

        def shaped(v, dims):
            if len(dims) == 1:
                return v
            names = "abcde"[:len(dims)]
            return v.rearrange(f"p ({' '.join(names)}) -> p {' '.join(names)}",
                               **{n: d for n, d in zip(names, dims)})

        s_const = sem("const_loaded")
        s_x = sem("x_loaded")
        s_pool = sem("pool_consts_ready")
        s_cdone = sem("const_split_ready")
        s_raw = [sem("raw_loaded_0"), sem("raw_loaded_1")]
        s_w = sem("weights_split")
        s_wfree = sem("weights_used")
        s_pst = sem("pool_split_step")
        s_end = [sem(f"stage_end_{e}") for e in ("pe", "act", "dve")]
        s_out = sem("out_stored")
        credits = []

        def credit(name, n):
            s = sem(name)
            credits.append((s, n))
            return s

        block = ctx.enter_context(nc.Block())
        prog = {"pe": [], "act": [], "dve": []}
        pe, act, dve = nc.tensor, nc.scalar, nc.vector

        def barrier(eng, me, stage):
            eng.drain().then_inc(s_end[me], 1)
            for s in s_end:
                eng.wait_ge(s, stage + 1)

        def slot16(job):
            return wsp[:, job % 2]

        def mm3(out_ap, lhs, rhs, start, stop):
            pe.matmul(out_ap, lhs(0), rhs(0), start=start, stop=False)
            pe.matmul(out_ap, lhs(0), rhs(1), start=False, stop=False)
            return pe.matmul(out_ap, lhs(1), rhs(0), start=False, stop=stop)

        def bcast(v, n):
            return v.unsqueeze(1).to_broadcast([v.shape[0], n, v.shape[1]])

        def nothing(*args):
            pass

        carrier = {id(e): e.alloc_register("wait_carrier") for e in (pe, act, nc.gpsimd)}

        def settled(eng):
            eng.reg_add(carrier[id(eng)], carrier[id(eng)], 1)

        def start_carrier(eng):
            eng.reg_mov(carrier[id(eng)], 0)

        class Norm:
            stat_runs = 0
            tile_runs = 0
            var, std = sem("norm_var_ready"), sem("norm_std_ready")
            xn, full, hi = sem("norm_tile_ready"), sem("norm_tile_transposed"), sem("norm_hi_ready")
            free = credit("norm_bank_free", 4)

            def __init__(self, name, src, keep=None, affine=None):
                self.src, self.keep, self.affine = src, keep, affine
                self.rs = Norm.stat_runs
                Norm.stat_runs += 1
                self.rt = None

            def dve_stats(self):
                with dve.Fori(0, NT) as t:
                    dve.bn_stats(st6[:, t, :], self.src[:, t, :])
                dve.drain()
                dve.tensor_tensor(mean[:], st6[:, :, 1], st6[:, :, 4], ALU.add)
                dve.tensor_tensor(sm[:, 0], st6[:, :, 1], st6[:, :, 4], ALU.subtract)
                dve.tensor_tensor(sm[:, 1], st6[:, :, 2], st6[:, :, 5], ALU.add)
                dve.drain()
                dve.tensor_scalar(mean[:], mean[:], 0.5, None, ALU.mult)
                dve.tensor_tensor(sm[:, 0], sm[:, 0], sm[:, 0], ALU.mult)
                dve.tensor_scalar(sm[:, 1], sm[:, 1], 1.0 / D, None, ALU.mult)
                dve.drain()
                dve.scalar_tensor_tensor(sm[:, 2], sm[:, 0], 0.25, sm[:, 1], ALU.mult, ALU.add)\
                    .then_inc(self.var, 1)
                dve.wait_ge(self.std, self.rs + 1)
                dve.reciprocal(rstd[:], sm[:, 3])
                dve.drain()

            def act_stats(self):
                act.wait_ge(self.var, self.rs + 1)
                act.activation(sm[:, 3], sm[:, 2], ACT.Sqrt, bias=eps_t[:, 0:1]).then_inc(self.std, 1)

            def normalise(self, dst, t):
                return dve.tensor_scalar(dst, self.src[:, t, :], mean[:, bass.ds(t, 1)],
                                         rstd[:, bass.ds(t, 1)], ALU.subtract, ALU.mult)

            def dve_tiles(self):
                with dve.Fori(0, NT // 4) as i:
                    for k in range(4):
                        if self.keep is not None:
                            self.normalise(self.keep[:, 4 * i + k, :], 4 * i + k)
                        m = self.normalise(xn[:, k], 4 * i + k)
                        if self.affine is None:
                            m.then_inc(self.xn, 1)
                    if self.affine is not None:
                        g, b = self.affine
                        dve.drain()
                        dve.tensor_tensor(xn[:], xn[:], bcast(g, 4), ALU.mult)
                        dve.drain()
                        for k in range(4):
                            dve.tensor_tensor(xn[:, k], xn[:, k], b, ALU.add).then_inc(self.xn, 1)
                    for k in range(4):
                        t = 4 * i + k
                        dve.wait_ge(self.hi, self.rt + t + 1)
                        dve.tensor_tensor(xT[:, 1, :, bass.ds(t * P, P)], ps[:, k, 0:D].rearrange("p (c n) -> p c n", c=KD),
                                          xT[:, 0, :, bass.ds(t * P, P)], ALU.subtract).then_inc(self.free, 1)

            def pe_tiles(self):
                with pe.Fori(0, NT // 4) as i:
                    for k in range(4):
                        t = 4 * i + k
                        pe.wait_ge(self.xn, self.rt + t + 1)
                        pe.wait_ge(self.free, self.rt + t + 1)
                        for c in range(KD):
                            m = pe.transpose(ps[:, k, c * P:(c + 1) * P], xn[:, k, c * P:(c + 1) * P], ident)
                        m.then_inc(self.full, 1)

            def act_tiles(self):
                with act.Fori(0, NT // 4) as i:
                    for k in range(4):
                        t = 4 * i + k
                        act.wait_ge(self.full, self.rt + t + 1)
                        settled(act)
                        act.activation(xT[:, 0, :, bass.ds(t * P, P)], ps[:, k, 0:D].rearrange("p (c n) -> p c n", c=KD),
                                       ACT.Copy).then_inc(self.hi, 1)

        def norm_stage(n, stage):
            n.rt = Norm.tile_runs * NT
            Norm.tile_runs += 1
            prog["dve"] += [n.dve_stats, n.dve_tiles, lambda: barrier(dve, 2, stage)]
            prog["act"] += [n.act_stats, n.act_tiles, lambda: barrier(act, 1, stage)]
            prog["pe"] += [n.pe_tiles, lambda: barrier(pe, 0, stage)]

        class Route:
            def __init__(self, name, layer):
                self.layer = layer
                self.col, self.E = ROUTERS[layer]
                self.full = sem(name + "_logits_ready")
                self.arg = sem(name + "_exp_arg_ready")
                self.ex = sem(name + "_exp_ready")
                self.sel = sem(name + "_sel_ready")
                self.pos = sem(name + "_positions_ready")
                E = self.E
                ar = Area()
                self.L = ar.f32(NT, 17)
                self.mx = ar.f32(NT, 8)
                self.ix = ar.f32(NT, 8)
                self.ixf = ar.f32(NT, 2)
                self.io = ar.f32(16)
                self.e = ar.f32(NT, 17)
                self.s = ar.f32(NT, 16)
                self.t = ar.f32(NT, 16)
                self.h = ar.f16(NT, 16)
                self.den = ar.f32(NT)

            def pe_part(self):
                E, c0 = self.E, self.col
                with pe.Fori(0, NT) as t:
                    for c in range(KD):
                        m = mm3(ps[:, 0, bass.ds(t * E, E)], lambda h: xT[:, h, c, bass.ds(t * P, P)],
                                lambda h: rws[:, h, c0 + c * E:c0 + (c + 1) * E], c == 0, c == KD - 1)
                    m.then_inc(self.full, 1)
                if self.layer == 0:
                    pe.wait_ge(self.sel, 1)
                    pe.matmul(ps[:, 1, 0:NT * 8], tri[:], self.h[:, :, 0:8], start=True, stop=True)
                    for t in range(NT - 1):
                        rest = NT - 1 - t
                        src = self.h[:, t:t + 1, 0:8].to_broadcast([P, rest, 8])
                        m = pe.matmul(ps[:, 1, (t + 1) * 8:NT * 8], ones[:], src, start=False,
                                      stop=True, skip_group_check=True)
                    m.then_inc(self.pos, 1)

            def act_part(self):
                ne = 16 if self.layer == 3 else 8
                act.wait_ge(self.arg, 1)
                act.activation(self.e[:, :, 0:self.E], self.e[:, :, 0:self.E], ACT.Exp).then_inc(self.ex, 1)

            def dve_part(self):
                E, layer = self.E, self.layer
                ne = 16 if layer == 3 else 8
                L, e = self.L, self.e
                dve.wait_ge(self.full, NT)
                dve.tensor_scalar(L[:, :, 0:E], ps[:, 0, 0:NT * E].rearrange("p (t e) -> p t e", t=NT), INV, None, ALU.mult)
                dve.drain()
                if layer == 1:
                    dve.tensor_tensor(L[:, :, 0:E], L[:, :, 0:E], bcast(sc[:, 9:17], NT), ALU.add)
                    dve.drain()
                for t in range(NT):
                    dve.max(self.mx[:, t, :], L[:, t, 0:ne])
                dve.drain()
                m1 = self.mx[:, :, 0:1].to_broadcast([P, NT, ne])
                m2 = self.mx[:, :, 1:2].to_broadcast([P, NT, ne])
                dve.tensor_tensor(e[:, :, 0:ne], L[:, :, 0:ne], m1, ALU.subtract)
                if layer == 3:
                    dve.tensor_scalar(e[:, :, 16:17], L[:, :, 16:17], -1.0, None, ALU.mult)
                dve.drain().then_inc(self.arg, 1)
                s, t2 = self.s[:, :, 0:ne], self.t[:, :, 0:ne]
                if layer == 1:
                    dve.tensor_tensor(s, L[:, :, 0:ne], m2, ALU.is_ge)
                else:
                    for t in range(NT):
                        dve.max_index(self.ix[:, t, :].bitcast(U32), self.mx[:, t, :], L[:, t, 0:ne])
                    dve.drain()
                    dve.tensor_copy(self.ixf[:], self.ix[:, :, 0:2].bitcast(U32))
                    dve.drain()
                    io = bcast(iota[:, 0:ne], NT)
                    dve.tensor_tensor(s, io, self.ixf[:, :, 0:1].to_broadcast([P, NT, ne]), ALU.is_equal)
                    dve.tensor_tensor(t2, io, self.ixf[:, :, 1:2].to_broadcast([P, NT, ne]), ALU.is_equal)
                    dve.drain()
                    dve.tensor_tensor(s, s, t2, ALU.add)
                dve.drain()
                if layer == 0:
                    dve.tensor_copy(self.h[:, :, 0:8], s).then_inc(self.sel, 1)
                dve.wait_ge(self.ex, 1)
                den = self.den[:]
                if layer == 2:
                    dve.tensor_reduce(den, e[:, :, 0:ne], X, ALU.add)
                    dve.drain()
                dve.tensor_tensor(s, s, e[:, :, 0:ne], ALU.mult)
                dve.drain()
                if layer != 2:
                    dve.tensor_reduce(den, s, X, ALU.add)
                    dve.drain()
                dve.reciprocal(den, den)
                dve.drain()
                dve.tensor_scalar(den, den, tg[:, 4 + layer:5 + layer], INV, ALU.mult, ALU.mult)
                dve.drain()
                dve.tensor_tensor(wgt[:, :, 0:ne], s, den.unsqueeze(2).to_broadcast([P, NT, ne]), ALU.mult)
                if layer == 0:
                    dve.wait_ge(self.pos, 1)
                    dve.tensor_scalar(t2, ps[:, 1, 0:NT * 8].rearrange("p (t e) -> p t e", t=NT), float(CAPACITY), None, ALU.is_lt)
                    dve.drain()
                    dve.tensor_tensor(wgt[:, :, 0:8], wgt[:, :, 0:8], t2, ALU.mult)
                if layer == 3:
                    dve.tensor_scalar(e[:, :, 16:17], e[:, :, 16:17], 1.0, None, ALU.add)
                    dve.drain()
                    dve.reciprocal(e[:, :, 16:17], e[:, :, 16:17])
                    dve.drain()
                    dve.tensor_scalar(wgt[:, :, 16:17], e[:, :, 16:17], tg[:, 7:8], INV, ALU.mult, ALU.mult)
                dve.drain()

        TOK = 512
        NCH = B * S // TOK
        Q = TOK // P

        class Ffn:

            def __init__(self, name, job, pairs, cols, act_fn, up, down, gated, bias1, b2_row,
                         weight, dst, each=False, area=0, single=False):
                self.name, self.job, self.pairs, self.single = name, job, pairs, single
                self.cols, self.fn, self.up, self.down = cols, act_fn, up, down
                self.gated, self.bias1, self.b2_row = gated, bias1, b2_row
                self.weight, self.dst, self.each = weight, dst, each
                self.nh = len(cols)
                self.R = 2 if gated else 4
                self.lag = 1 if each else 2
                ar = Area(area)
                self.hf = ar.f32(self.R, TOK)
                self.hh = ar.f16(self.R, 2, TOK)
                self.s_up = sem(name + "_up_full")
                self.s_act = credit(name + "_act_done", self.R)
                self.s_upfree = credit(name + "_gate_product_done", self.R)
                self.s_hhi = sem(name + "_hi_ready")
                self.s_h = credit(name + "_hidden_ready", self.R)
                self.s_hfree = credit(name + "_down_done", self.R)
                self.s_yfree = credit(name + "_y_free", 2 if each else 1)

            def bank(self, j):
                return 2 * (j % 2) if self.gated else j % 4

            def schedule(self, fori, unit_up, unit_down, begin, end):
                nh, lag = self.nh, self.lag

                def steps(i0, off, cont_in, cont_out):
                    if not cont_in:
                        begin(i0, off)
                        for j in range(lag):
                            unit_up(i0, off, 0, j)
                    with fori(0, NCH - 1) as c:
                        for j in range(nh):
                            nx = j + lag
                            unit_up(i0, off, c, nx) if nx < nh else unit_up(i0, off, c + 1, nx - nh)
                            unit_down(i0, off, c, j)
                    for j in range(nh):
                        nx = j + lag
                        if nx < nh:
                            unit_up(i0, off, NCH - 1, nx)
                        elif cont_out:
                            if nx == nh:
                                begin(i0, off + 1)
                            unit_up(i0, off + 1, 0, nx - nh)
                        unit_down(i0, off, NCH - 1, j)
                    end(i0, off)

                if self.single:
                    steps(0, 0, False, False)
                else:
                    with fori(0, self.pairs) as i:
                        steps(2 * i, 0, False, True)
                        steps(2 * i, 1, True, False)

            def unit(self, i0, off, c, j):
                return ((i0 + off) * NCH + c) * self.nh + j

            def pe_part(self):
                def begin(i0, off):
                    pe.wait_ge(s_w, self.job + i0 + off + 1)

                def unit_up(i0, off, c, j):
                    w = wsp[:, (self.job + off) % 2]
                    n = self.unit(i0, off, c, j)
                    m = self.cols[j]
                    bk = self.bank(j)
                    pe.wait_ge(self.s_upfree if self.gated else self.s_act, n + 1)
                    if self.gated and m < P:
                        pe.matmul(ps[0:m, bk, 0:1], w[:, 0, 0:m], w[:, 0, 0:1], start=True, stop=True)
                    for g in range(2 if self.gated else 1):
                        for k in range(KD):
                            last = mm3(ps[0:m, bk + g, :],
                                       lambda h: self.up(w[:, h], g, k, j),
                                       lambda h: xT[:, h, k, bass.ds(c * TOK, TOK)], k == 0, k == KD - 1)
                    last.then_inc(self.s_up, 1)

                def unit_down(i0, off, c, j):
                    w = wsp[:, (self.job + off) % 2]
                    n = self.unit(i0, off, c, j)
                    step = (i0 + off) * NCH + c
                    m = self.cols[j]
                    r = j % self.R
                    pe.wait_ge(self.s_h, n + 1 + self.R)
                    first = self.each or j == 0
                    final = self.each or j == self.nh - 1
                    if first:
                        pe.wait_ge(self.s_yfree, (n if self.each else step) + 1)
                    for q in range(Q):
                        if self.each:
                            o = ps[:, 4 + 2 * (j % 2) + q // 2, (q % 2) * D:(q % 2 + 1) * D]
                        else:
                            o = ps[:, 4 + q, 0:D]
                        if first and self.b2_row is not None:
                            pe.matmul(o, ones[0:33, :], b2s[:, self.b2_row + i0 + off, :], start=True, stop=False)
                        last = mm3(o, lambda h: self.hh[0:m, r, h, q * P:(q + 1) * P],
                                   lambda h: self.down(w[0:m, h], j),
                                   first and self.b2_row is None, final)
                    last.then_inc(self.s_hfree, 1)

                def end(i0, off):
                    pe.drain().then_inc(s_wfree, 1)

                self.schedule(pe.Fori, unit_up, unit_down, begin, end)

            def act_part(self):
                def begin(i0, off):
                    if self.bias1 is not None:
                        act.drain()
                        act.copy(b1e[:], b1c[:, bass.ds(self.bias1 + (i0 + off) * self.nh, self.nh)])
                        act.drain()

                def unit_up(i0, off, c, j):
                    n = self.unit(i0, off, c, j)
                    m, r, bk = self.cols[j], j % self.R, self.bank(j)
                    act.wait_ge(self.s_up, n + 1)
                    act.wait_ge(self.s_h, n + 1)
                    settled(act)
                    kw = {}
                    if self.bias1 is not None:
                        kw["bias"] = b1e[:, j:j + 1]
                    act.activation(self.hf[0:m, r, :], ps[0:m, bk, :], self.fn, scale=INV, **kw)\
                        .then_inc(self.s_act, 1)

                self.schedule(act.Fori, unit_up, nothing, begin, nothing)

            def dve_part(self):
                def unit_up(i0, off, c, j):
                    n = self.unit(i0, off, c, j)
                    m, r, bk = self.cols[j], j % self.R, self.bank(j)
                    hf = self.hf[0:m, r, :]
                    dve.wait_ge(self.s_act, n + 1 + self.R)
                    if self.gated:
                        dve.scalar_tensor_tensor(hf, ps[0:m, bk + 1, :], INV, hf, ALU.mult, ALU.mult)\
                            .then_inc(self.s_upfree, 1)
                        dve.wait_ge(self.s_upfree, n + 1 + self.R)
                    dve.wait_ge(self.s_hfree, n + 1)
                    dve.tensor_copy(self.hh[0:m, r, 0, :], hf).then_inc(self.s_hhi, 1)
                    dve.wait_ge(self.s_hhi, n + 1)
                    dve.tensor_tensor(self.hh[0:m, r, 1, :], hf, self.hh[0:m, r, 0, :], ALU.subtract)\
                        .then_inc(self.s_h, 1)

                def unit_down(i0, off, c, j):
                    if not (self.each or j == self.nh - 1):
                        return
                    n = self.unit(i0, off, c, j)
                    dve.drain()
                    dve.wait_ge(self.s_hfree, n + 1 + self.R)
                    for q in range(Q):
                        t = c * Q + q
                        if self.each:
                            y = ps[:, 4 + 2 * (j % 2) + q // 2, (q % 2) * D:(q % 2 + 1) * D]
                        else:
                            y = ps[:, 4 + q, 0:D]
                        i = dve.scalar_tensor_tensor(self.dst[:, t, :], y, self.weight(t, i0 + off, j),
                                                     self.dst[:, t, :], ALU.mult, ALU.add)
                    i.then_inc(self.s_yfree, 1)

                self.schedule(dve.Fori, unit_up, unit_down, nothing, nothing)

        class Attn:
            def __init__(self, name, jobq, jobk, inner, dh, layer, merged):
                self.name, self.jobq, self.jobk = name, jobq, jobk
                self.inner, self.dh, self.layer, self.merged = inner, dh, layer, merged
                self.NC = inner // P
                self.hpc = P // dh
                self.H = inner // dh
                self.scale = dh ** -0.5
                ar = Area()
                self.q = ar.f16(2, self.NC, S)
                self.o = ar.f16(2, self.NC, S)
                if merged:
                    self.k = ar.f16(2, self.NC, GA)
                    self.v = ar.f16(2, 5, inner)
                    self.pr = ar.f32(3, 2, GA)
                    self.pT = ar.f16(2, 2, 5, S)
                    self.G = self.H
                    self.tuses = 3
                    self.kc = [P] * 4 + [GA - 4 * P]
                else:
                    self.k = ar.f16(2, self.NC, 2 * G)
                    self.v = ar.f16(2, inner)
                    self.pr = ar.f32(3, 2, 4, G)
                    self.pT = ar.f16(2, 2, 4, S)
                    self.G = self.NC // 2
                    self.tuses = 2
                self.mx = ar.f32(3, 2, 4)
                self.sm = ar.f32(3, 2, 4)
                n = name
                self.s_pf = sem(n + "_proj_full")
                self.s_ph = sem(n + "_proj_hi")
                self.s_pfree = credit(n + "_proj_free", 2)
                self.s_sf = sem(n + "_scores_full")
                self.s_sfree = credit(n + "_scores_free", 2 if merged else 4)
                self.s_ar = sem(n + "_exp_arg")
                self.s_ex = sem(n + "_exp_done")
                self.s_p = sem(n + "_probs_ready")
                self.s_tf = sem(n + "_trans_full")
                self.s_th = sem(n + "_trans_hi")
                self.s_tfree = credit(n + "_trans_free", 2)
                self.s_of = sem(n + "_out_done")
                self.s_z = sem(n + "_zero_ready")
                self.kv_uses = (2 * self.NC + 10) if merged else 0
                self.pb = (0 if merged else (self.NC // 4 + inner // 512)) + self.NC // 2
                self.uses = self.pb + self.NC // 2 + 2
                assert self.uses % 2 == 0 and self.kv_uses % 2 == 0

            def wq(self, h, k, c):
                w = wsp[:, self.jobq % 2, h]
                return w[:, k * self.inner + c * P:k * self.inner + (c + 1) * P]

            def wo(self, h, c):
                at = KD * self.inner + c * D
                return wsp[:, self.jobq % 2, h, at:at + D]

            def koff(self):
                return 2048 if self.jobk == self.jobq else 0

            def wk(self, h, k, c):
                at = self.koff() + k * self.inner + c * P
                return wsp[0:CP, self.jobk % 2, h, at:at + P]

            def wv(self, h, k, c0, n):
                at = self.koff() + KC * self.inner + k * self.inner + c0
                return wsp[0:CP, self.jobk % 2, h, at:at + n]

            def kv_entries(self, i):
                r = []
                if self.merged:
                    for c in range(self.NC):
                        for half in range(2):
                            n0 = half * (GA // 2)

                            def fill(bk, c=c, n0=n0):
                                for k in range(KC):
                                    m = mm3(ps[:, bk, 0:GA // 2], lambda h: self.wk(h, k, c),
                                            lambda h: ctxs[:, h, k, n0:n0 + GA // 2], k == 0, k == KC - 1)
                                return m
                            r.append((fill, [(lambda bk: ps[:, bk, 0:GA // 2],
                                              lambda h, c=c, n0=n0: self.k[:, h, c, n0:n0 + GA // 2], INV)]))
                    for kc, rows in enumerate(self.kc):
                        for half in range(2):
                            def fill(bk, kc=kc, rows=rows, half=half):
                                for k in range(KC):
                                    m = mm3(ps[0:rows, bk, :], lambda h: ctxs[:, h, k, kc * P:kc * P + rows],
                                            lambda h: self.wv(h, k, half * 512, 512), k == 0, k == KC - 1)
                                return m
                            r.append((fill, [(lambda bk, rows=rows: ps[0:rows, bk, :],
                                              lambda h, kc=kc, rows=rows, half=half:
                                              self.v[0:rows, h, kc, half * 512:(half + 1) * 512], INV)]))
                    return r
                for c0 in range(0, self.NC, 4):
                    def fill(bk, c0=c0):
                        for c in range(4):
                            for k in range(KC):
                                m = mm3(ps[:, bk, c * G:(c + 1) * G], lambda h: self.wk(h, k, c0 + c),
                                        lambda h: ctxs[:, h, k, bass.ds(i * G, G)], k == 0, k == KC - 1)
                        return m
                    dr = []
                    for b in range(self.hpc):
                        r0 = b * self.dh
                        dr.append((lambda bk, r0=r0: ps[r0:r0 + self.dh, bk, 0:4 * G].rearrange("p (c g) -> p c g", c=4),
                                   lambda h, r0=r0, b=b, c0=c0: self.k[r0:r0 + self.dh, h, c0:c0 + 4, b * G:(b + 1) * G], INV))
                    r.append((fill, dr))
                for half in range(self.inner // 512):
                    def fill(bk, half=half):
                        for k in range(KC):
                            m = mm3(ps[0:G, bk, :], lambda h: ctxs[:, h, k, bass.ds(i * G, G)],
                                    lambda h: self.wv(h, k, half * 512, 512), k == 0, k == KC - 1)
                        return m
                    r.append((fill, [(lambda bk: ps[0:G, bk, :],
                                      lambda h, half=half: self.v[0:G, h, half * 512:(half + 1) * 512], INV)]))
                return r

            def q_entries(self, i):
                r = []
                for c0 in range(0, self.NC, 2):
                    def fill(bk, c0=c0):
                        for c in range(2):
                            for k in range(KD):
                                m = mm3(ps[:, bk, c * S:(c + 1) * S], lambda h: self.wq(h, k, c0 + c),
                                        lambda h: xT[:, h, k, bass.ds(i * S, S)], k == 0, k == KD - 1)
                        return m
                    r.append((fill, [(lambda bk: ps[:, bk, :],
                                      lambda h, c0=c0: self.q[:, h, c0:c0 + 2, :].rearrange("p c n -> p (c n)"), INV)]))
                return r

            def walk(self, fori, eng):
                if self.merged:
                    for u, en in enumerate(self.kv_entries(0)):
                        eng.proj(u, u, en)
                with fori(0, B) as i:
                    base = i * self.uses + self.kv_uses
                    u = 0
                    for en in ([] if self.merged else self.kv_entries(i)) + self.q_entries(i):
                        eng.proj(base + u, self.kv_uses + u, en, i)
                        u += 1
                    for g in range(self.G + 2):
                        if g < self.G:
                            eng.scores(i, g)
                        if g >= 2:
                            eng.apply(i, g - 2)
                            if not self.merged or (g - 2) % 2 == 1:
                                eng.pv(i, g - 2, base + u, self.kv_uses + u)
                                u += 1
                            elif self.merged:
                                eng.pv_half(i, g - 2, base + u, self.kv_uses + u)
                    eng.out(i, base + u, self.kv_uses + u)
                    assert u + 2 == self.uses, (u + 2, self.uses)

            def bank67(self, u):
                return 6 + u % 2

        class AttnPE:
            def __init__(self, A):
                self.A = A

            def proj(self, n, u, en, i=None):
                A = self.A
                pe.wait_ge(A.s_pfree, n + 1)
                en[0](A.bank67(u)).then_inc(A.s_pf, 1)

            def scores(self, i, g):
                A = self.A
                if g == 0:
                    pe.wait_ge(A.s_pfree, i * A.uses + A.kv_uses + A.pb + 2)
                for t in range(2):
                    n = (i * A.G + g) * 2 + t
                    pe.wait_ge(A.s_sfree, n + 1)
                    if A.merged:
                        for half in range(2):
                            n0 = half * (GA // 2)
                            m = mm3(ps[:, 2 * t + half, 0:GA // 2],
                                    lambda h: A.q[:, h, g, t * P:(t + 1) * P],
                                    lambda h: A.k[:, h, g, n0:n0 + GA // 2], True, True)
                    else:
                        for c in range(2):
                            m = mm3(ps[:, 2 * (g % 2) + t, c * 2 * G:(c + 1) * 2 * G],
                                    lambda h: A.q[:, h, 2 * g + c, t * P:(t + 1) * P],
                                    lambda h: A.k[:, h, 2 * g + c, :], True, True)
                    m.then_inc(A.s_sf, 1)

            def apply(self, i, g):
                A = self.A
                pe.wait_ge(A.s_p, (i * A.G + g + 1) * 2)
                for tu in range(A.tuses):
                    n = (i * A.G + g) * A.tuses + tu
                    pe.wait_ge(A.s_tfree, n + 1)
                    bk = 4 + A.tbank(g, tu)
                    if A.merged:
                        for kc in range(2 * tu, min(2 * tu + 2, 5)):
                            rows = A.kc[kc]
                            for t in range(2):
                                at = (kc % 2) * S + t * P
                                m = pe.transpose(ps[0:rows, bk, at:at + P], A.pr[:, g % 3, t, kc * P:kc * P + rows], ident)
                    else:
                        for hd in range(2 * tu, 2 * tu + 2):
                            for t in range(2):
                                at = (hd % 2) * S + t * P
                                m = pe.transpose(ps[0:G, bk, at:at + P], A.pr[:, g % 3, t, hd, :], ident)
                    m.then_inc(A.s_tf, 1)

            def pv_head(self, g, bk, at):
                A = self.A
                for kc in range(5):
                    rows = A.kc[kc]
                    m = mm3(ps[:, bk, at:at + S], lambda h: A.v[0:rows, h, kc, g * P:(g + 1) * P],
                            lambda h: A.pT[0:rows, g % 2, h, kc, :], kc == 0, kc == 4)
                return m

            def wait_pT(self, i, g):
                A = self.A
                pe.wait_ge(A.s_tfree, (i * A.G + g + 1) * A.tuses + 2)

            def pv_half(self, i, g, n, u):
                A = self.A
                self.wait_pT(i, g)
                pe.wait_ge(A.s_pfree, n + 1)
                self.pv_head(g, A.bank67(u), 0)

            def pv(self, i, g, n, u):
                A = self.A
                self.wait_pT(i, g)
                pe.wait_ge(A.s_pfree, n + 1)
                bk = A.bank67(u)
                if A.merged:
                    m = self.pv_head(g, bk, S)
                else:
                    for c in range(2):
                        for b in range(2):
                            hd = 2 * c + b
                            col = (4 * g + hd) * A.dh
                            m = mm3(ps[b * 64:(b + 1) * 64, bk, c * S:(c + 1) * S],
                                    lambda h: A.v[0:G, h, col:col + A.dh],
                                    lambda h: A.pT[0:G, g % 2, h, hd, :], True, True)
                m.then_inc(A.s_pf, 1)

            def out(self, i, n, u):
                A = self.A
                for t in range(2):
                    pe.wait_ge(A.s_pfree, n + 2)
                    for c in range(A.NC):
                        m = mm3(ps[:, A.bank67(u + t), 0:D], lambda h: A.o[:, h, c, t * P:(t + 1) * P],
                                lambda h: A.wo(h, c), c == 0, c == A.NC - 1)
                    m.then_inc(A.s_pf, 1)

        class AttnACT:
            def __init__(self, A):
                self.A = A

            def hi(self, n, bk, drains):
                A = self.A
                act.wait_ge(A.s_pf, n + 1)
                for view, dst, scale in drains:
                    m = act.activation(dst(0), view(bk), ACT.Copy, scale=scale)
                m.then_inc(A.s_ph, 1)

            def proj(self, n, u, en, i=None):
                self.hi(n, self.A.bank67(u), en[1])

            def scores(self, i, g):
                A = self.A
                for t in range(2):
                    n = (i * A.G + g) * 2 + t
                    act.wait_ge(A.s_ar, n + 1)
                    if A.merged:
                        act.activation(A.pr[:, g % 3, t, :].rearrange("p (a n) -> p a n", a=2),
                                       ps[:, 2 * t:2 * t + 2, 0:GA // 2], ACT.Exp,
                                       scale=1.5 * A.scale, bias=A.mx[:, g % 3, t, 1:2],
                                       accum_out=A.sm[:, g % 3, t, 0:1])
                        act.drain().then_inc(A.s_ex, 1)
                    else:
                        v = A.pr[:, g % 3, t, :, :]
                        act.activation(v, v, ACT.Exp, scale=A.scale).then_inc(A.s_ex, 1)

            def apply(self, i, g):
                A = self.A
                for tu in range(A.tuses):
                    n = (i * A.G + g) * A.tuses + tu
                    act.wait_ge(A.s_tf, n + 1)
                    bk = 4 + A.tbank(g, tu)
                    act.activation(A.tdst(g, tu, 0), A.tsrc(bk, tu), ACT.Copy).then_inc(A.s_th, 1)

            def pv_half(self, i, g, n, u):
                pass

            def pv(self, i, g, n, u):
                self.hi(n, self.A.bank67(u), [self.A.odrain(g)])

            def out(self, i, n, u):
                pass

        class AttnDVE:
            def __init__(self, A):
                self.A = A

            def lo(self, n, m, bk, drains):
                A = self.A
                dve.wait_ge(A.s_ph, m + 1)
                for view, dst, scale in drains:
                    i = dve.scalar_tensor_tensor(dst(1), view(bk), scale, dst(0), ALU.mult, ALU.subtract)
                i.then_inc(A.s_pfree, 1)

            def count(self, i, u):
                A = self.A
                return (0 if i is None else i * (A.uses - 2)) + u

            def proj(self, n, u, en, i=None):
                self.lo(n, self.count(i, u), self.A.bank67(u), en[1])

            def scores(self, i, g):
                A = self.A
                r = g % 3
                for t in range(2):
                    n = (i * A.G + g) * 2 + t
                    dve.wait_ge(A.s_sf, n + 1)
                    if A.merged:
                        src = ps[:, 2 * t:2 * t + 2, 0:GA // 2]
                        dve.tensor_reduce(A.mx[:, r, t, 0:1], src, mybir.AxisListType.XY, ALU.max)
                        dve.drain()
                        dve.tensor_scalar(A.mx[:, r, t, 1:2], A.mx[:, r, t, 0:1], -1.5 * A.scale, None, ALU.mult)\
                            .then_inc(A.s_ar, 1)
                    else:
                        src = ps[:, 2 * (g % 2) + t, 0:4 * G].rearrange("p (h k) -> p h k", h=4)
                        dve.tensor_reduce(A.mx[:, r, t, :], src, X, ALU.max)
                        dve.drain()
                        dve.tensor_tensor(A.pr[:, r, t, :, :], src,
                                          A.mx[:, r, t, :].unsqueeze(2).to_broadcast([P, 4, G]), ALU.subtract)\
                            .then_inc(A.s_ar, 1)
                for t in range(2):
                    n = (i * A.G + g) * 2 + t
                    dve.wait_ge(A.s_ex, n + 1)
                    if A.merged:
                        dve.reciprocal(A.sm[:, r, t, 1:2], A.sm[:, r, t, 0:1]).then_inc(A.s_sfree, 1)
                        dve.drain()
                        dve.tensor_scalar(A.pr[:, r, t, :], A.pr[:, r, t, :], A.sm[:, r, t, 1:2], None, ALU.mult)\
                            .then_inc(A.s_p, 1)
                    else:
                        dve.tensor_reduce(A.sm[:, r, t, :], A.pr[:, r, t, :, :], X, ALU.add).then_inc(A.s_sfree, 1)
                        dve.drain()
                        dve.reciprocal(A.sm[:, r, t, :], A.sm[:, r, t, :])
                        dve.drain()
                        dve.tensor_tensor(A.pr[:, r, t, :, :], A.pr[:, r, t, :, :],
                                          A.sm[:, r, t, :].unsqueeze(2).to_broadcast([P, 4, G]), ALU.mult)\
                            .then_inc(A.s_p, 1)

            def apply(self, i, g):
                A = self.A
                for tu in range(A.tuses):
                    n = (i * A.G + g) * A.tuses + tu
                    dve.wait_ge(A.s_th, n + 1)
                    bk = 4 + A.tbank(g, tu)
                    dve.tensor_tensor(A.tdst(g, tu, 1), A.tsrc(bk, tu), A.tdst(g, tu, 0), ALU.subtract)\
                        .then_inc(A.s_tfree, 1)

            def pv_half(self, i, g, n, u):
                pass

            def pv(self, i, g, n, u):
                self.lo(n, self.count(i, u), self.A.bank67(u), [self.A.odrain(g)])

            def out(self, i, n, u):
                A = self.A
                for t in range(2):
                    dve.wait_ge(A.s_pf, n + t + 1)
                    dve.scalar_tensor_tensor(x[:, 2 * i + t, :], ps[:, A.bank67(u + t), 0:D],
                                             sm[:, 4, 0:1], x[:, 2 * i + t, :], ALU.mult, ALU.add)\
                        .then_inc(A.s_pfree, 1)

        def tbank(A):
            return lambda g, tu: (g * A.tuses + tu) % 2

        def tdst(A):
            def f(g, tu, h):
                if A.merged:
                    if tu == 2:
                        return A.pT[0:A.kc[4], g % 2, h, 4, :]
                    return A.pT[:, g % 2, h, 2 * tu:2 * tu + 2, :].rearrange("p c n -> p (c n)")
                return A.pT[0:G, g % 2, h, 2 * tu:2 * tu + 2, :].rearrange("p c n -> p (c n)")
            return f

        def tsrc(A):
            def f(bk, tu):
                if A.merged:
                    return ps[0:A.kc[4], bk, 0:S] if tu == 2 else ps[:, bk, :]
                return ps[0:G, bk, :]
            return f

        def odrain(A):
            def f(g):
                c0 = g - 1 if A.merged else 2 * g
                return (lambda bk: ps[:, bk, :],
                        lambda h: A.o[:, h, c0:c0 + 2, :].rearrange("p c n -> p (c n)"), 1.0)
            return f

        def attn_stage(A, stage):
            A.tbank, A.tdst, A.tsrc, A.odrain = tbank(A), tdst(A), tsrc(A), odrain(A)

            def pe_part():
                for j in sorted({A.jobq, A.jobk}):
                    pe.wait_ge(s_w, j + 1)
                if not A.merged:
                    pe.wait_ge(A.s_z, 1)
                A.walk(pe.Fori, AttnPE(A))
                pe.drain().then_inc(s_wfree, len({A.jobq, A.jobk}))
                barrier(pe, 0, stage)

            def act_part():
                if not A.merged:
                    act.wait_ge(A.s_z, 1)
                A.walk(act.Fori, AttnACT(A))
                barrier(act, 1, stage)

            def dve_part():
                if not A.merged:
                    dve.memset(A.k[:, :, :, :].rearrange("p h c n -> p (h c n)"), 0.0)
                dve.tensor_scalar(sm[:, 4, 0:1], tg[:, A.layer:A.layer + 1], INV, None, ALU.mult)
                dve.tensor_scalar(brow[:, A.layer - 1, :], brow[:, A.layer - 1, :], tg[:, A.layer:A.layer + 1], None, ALU.mult)
                dve.drain().then_inc(A.s_z, 1)
                with dve.Fori(0, NT) as t:
                    dve.tensor_tensor(x[:, t, :], x[:, t, :], brow[:, A.layer - 1, :], ALU.add)
                dve.drain()
                A.walk(dve.Fori, AttnDVE(A))
                barrier(dve, 2, stage)
            prog["pe"].append(pe_part)
            prog["act"].append(act_part)
            prog["dve"].append(dve_part)

        def small(n):
            return xT[:].rearrange("p a b c -> p (a b c)")[:, 2 * D * n:2 * D * (n + 1)].bitcast(F32)

        ARE, AIM, CRE, CIM, LDT = (small(n) for n in range(5))
        DT, IMC, T1, T2, T3, DCR, DCI, RE, T4, T5, T6 = (small(n) for n in range(5, 16))

        class KGen:
            def __init__(self):
                ar = Area()
                self.y = ar.f32(D, 16)
                self.e1 = ar.f32(D, 16)
                self.e2 = ar.f32(D, 16)
                self.v = ar.f32(D, 16)
                self.w = ar.f32(D, 16)
                self.kk = self.v[:, 0:32, :]
                self.kp = shaped(self.w.rearrange("p a b -> p (a b)")[:, 0:512].bitcast(F16), (32, 16, 2))
                self.zero = self.w.rearrange("p a b -> p (a b)")[:, 1024:1280].bitcast(F16)
                self.s_d = sem("kgen_dve")
                self.s_a = sem("kgen_act")
                self.s_t = sem("kgen_tables_ready")
                self.s_k = sem("kgen_sums_ready")
                self.s_st = sem("kgen_rows_ready")
                self.s_kd = sem("kernel_in_dram")

            ACTS = [("T1", "T1", "tanh", 1.0 / 16), ("T1", "T1", "tanh", 0.5), ("T2", "T2", "sin", 0),
                    ("T3", "T3", "sin", 0)]

            def act_part(self):
                n = [0]

                def step(dst, src, fn, **kw):
                    n[0] += 1
                    act.wait_ge(self.s_d, n[0])
                    act.activation(dst, src, fn, **kw)
                    act.drain().then_inc(self.s_a, 1)

                act.wait_ge(s_const, N_CONST)
                act.activation(tg[:], sc[:, 0:8], ACT.Tanh)
                step(T1, LDT, ACT.Tanh, scale=1.0 / 16)
                step(T1, RE, ACT.Tanh, scale=0.5)
                step(T2, T2, ACT.Sin, scale=SIN_SCALE)
                step(T3, T3, ACT.Sin, scale=SIN_SCALE)
                step(self.v, self.v, ACT.Sin, scale=SIN_SCALE, bias=cst[:, C_PHR:C_PHR + 1])
                step(self.w, self.w, ACT.Exp)
                step(self.v, self.v, ACT.Sin, scale=SIN_SCALE, bias=cst[:, C_PHR + 1:C_PHR + 2])
                step(self.w, self.w, ACT.Sin, scale=SIN_SCALE, bias=cst[:, C_PHR + 2:C_PHR + 3])
                step(self.w, self.w, ACT.Exp)

            def dve_part(self):
                n = [0]

                def tt(o, a_, b_, op):
                    dve.tensor_tensor(o, a_, b_, op)
                    dve.drain()

                def ts(o, a_, s1, s2, op0, op1):
                    dve.tensor_scalar(o, a_, s1, s2, op0, op1) if s2 is not None else dve.tensor_scalar(o, a_, s1, None, op0)
                    dve.drain()

                def ask(count=1):
                    dve.drain().then_inc(self.s_d, count)
                    n[0] += count
                    dve.wait_ge(self.s_a, n[0])

                def wrap(dst, y, ph):
                    ts(dst, y, ph, ROUND, ALU.add, ALU.add)
                    dve.scalar_tensor_tensor(dst, dst, ROUND, y, ALU.subtract, ALU.subtract)
                    dve.drain()

                dve.wait_ge(s_const, N_CONST)
                ask()
                ts(T2, T1, -1.0, 1.0, ALU.mult, ALU.add)
                ts(T3, T1, 1.0, None, ALU.add, None)
                dve.reciprocal(T2, T2)
                dve.drain()
                tt(T2, T2, T3, ALU.mult)
                for _ in range(3):
                    tt(T2, T2, T2, ALU.mult)
                tt(RE, T2, ARE, ALU.mult)
                tt(IMC, T2, AIM, ALU.mult)
                ts(IMC, IMC, 1.0 / TWO_PI, None, ALU.mult, None)
                ask()
                ts(T2, IMC, 0.5, None, ALU.mult, None)
                wrap(T4, T2, 0.0)
                wrap(T3, IMC, 0.0)
                dve.tensor_copy(T2, T4)
                ask(2)
                ts(T4, T1, -1.0, 1.0, ALU.mult, ALU.add)
                dve.reciprocal(T4, T4)
                dve.drain()
                tt(T1, T1, T4, ALU.mult)
                ts(T1, T1, 2.0, None, ALU.mult, None)
                tt(T2, T2, T2, ALU.mult)
                ts(T2, T2, 2.0, None, ALU.mult, None)
                ts(T4, T2, -1.0, 1.0, ALU.mult, ALU.add)
                tt(T4, T4, T1, ALU.mult)
                tt(T4, T4, T2, ALU.subtract)
                dve.scalar_tensor_tensor(T5, T1, 1.0, T3, ALU.add, ALU.mult)
                dve.drain()
                tt(T1, ARE, ARE, ALU.mult)
                tt(T2, AIM, AIM, ALU.mult)
                tt(T1, T1, T2, ALU.add)
                dve.reciprocal(T1, T1)
                dve.drain()
                ts(T1, T1, 2.0, None, ALU.mult, None)
                tt(T2, T4, ARE, ALU.mult)
                tt(T3, T5, AIM, ALU.mult)
                tt(T2, T2, T3, ALU.add)
                tt(T2, T2, T1, ALU.mult)
                tt(T3, T5, ARE, ALU.mult)
                tt(T6, T4, AIM, ALU.mult)
                tt(T3, T3, T6, ALU.subtract)
                tt(T3, T3, T1, ALU.mult)
                tt(DCR, CRE, T2, ALU.mult)
                tt(T6, CIM, T3, ALU.mult)
                tt(DCR, DCR, T6, ALU.subtract)
                tt(DCI, CRE, T3, ALU.mult)
                tt(T6, CIM, T2, ALU.mult)
                tt(DCI, DCI, T6, ALU.add)

                def over_k(o, v, at):
                    tt(o, v.unsqueeze(2).to_broadcast([P, D, 16]), bcast(cst[:, at:at + 16], D), ALU.mult)

                over_k(self.y, IMC, C_IOTA)
                wrap(self.v, self.y, cst[:, C_PH:C_PH + 1])
                over_k(self.w, RE, C_IOTA)
                ask(2)
                tt(self.e1, self.v, self.w, ALU.mult)
                over_k(self.y, IMC, C_K16)
                wrap(self.v, self.y, cst[:, C_PH + 1:C_PH + 2])
                wrap(self.w, self.y, cst[:, C_PH + 2:C_PH + 3])
                ask(2)
                tt(self.v, self.v, DCR.unsqueeze(2).to_broadcast([P, D, 16]), ALU.mult)
                tt(self.w, self.w, DCI.unsqueeze(2).to_broadcast([P, D, 16]), ALU.mult)
                tt(self.v, self.v, self.w, ALU.add)
                over_k(self.w, RE, C_K16)
                ask()
                dve.tensor_tensor(self.e2, self.v, self.w, ALU.mult)
                dve.drain().then_inc(self.s_t, 1)
                for bk in range(8):
                    dve.wait_ge(self.s_k, bk + 1)
                    m = self.y.rearrange("p a b -> p (a b)")[:, 512 * (bk % 4):512 * (bk % 4 + 1)]
                    m4 = shaped(m, (4, 8, 16))
                    mask = cst[:, C_MASK:C_MASK + 8].unsqueeze(1).unsqueeze(3).to_broadcast([P, 4, 8, 16])
                    dve.tensor_tensor(m4, shaped(ps[:, bk, :], (4, 8, 16)), mask, ALU.mult)
                    dve.drain()
                    dve.tensor_reduce(self.kk[:, 4 * bk:4 * bk + 4, :], m4.rearrange("p g d b -> p g b d"), X, ALU.add)
                dve.memset(self.zero, 0.0)
                dve.drain()
                dve.tensor_tensor(self.kk[:, :, 0], self.kk[:, :, 0], dsk[:], ALU.add)
                dve.drain()
                dve.tensor_copy(self.kp[:, :, :, 0], self.kk)
                dve.drain()
                dve.tensor_tensor(self.kp[:, :, :, 1], self.kk, self.kp[:, :, :, 0], ALU.subtract)
                dve.drain().then_inc(self.s_st, 1)

            def pe_part(self):
                pe.wait_ge(self.s_t, 1)
                for g in range(D // 8):
                    l = self.e2[:, 8 * g:8 * g + 8, :].rearrange("p d a -> p (d a)")
                    r = self.e1[:, 8 * g:8 * g + 8, :].rearrange("p d a -> p (d a)")
                    m = pe.matmul(ps[:, g // 4, (g % 4) * P:(g % 4 + 1) * P], l, r, start=True, stop=True)
                    if g % 4 == 3:
                        m.then_inc(self.s_k, 1)

            def store(self, sp):
                sp.wait_ge(self.s_st, 1)
                for half in range(2):
                    sp.dma_start(kdram[half * P:(half + 1) * P, 0:127, :].rearrange("d j c -> d (j c)"),
                                 self.zero[:, 0:254]).then_inc(self.s_kd, 16)
                for e in range(8):
                    sp.dma_start(kdram[:, 127:127 + S, :].rearrange("(g e) (a b) c -> e a g (b c)", e=8, b=16)[e],
                                 self.kp[16 * e:16 * e + 16].rearrange("p g b c -> p g (b c)")).then_inc(self.s_kd, 16)
                sp.wait_ge(self.s_kd, 160)

        L0 = Area()
        xtext = L0.f32(NT, D)
        u = L0.f16(2, NT, D)
        ystart = L0.at
        y = L0.f32(NT, D)
        rows = L0.f32(NROW)
        TG = 8
        tz = L0.f16(2, TG, S, 2)
        H0, DH0, KTOP = 4, 32, 32

        def row(n, w=D):
            return rows[:, n * D:n * D + w]

        class Attn0:
            def __init__(self):
                ar = Area(ystart)
                self.q = ar.f16(2, S)
                self.k = ar.f16(2, H0 * G)
                self.v = ar.f16(2, D)
                self.s = ar.f32(2, H0, G)
                self.w = ar.f32(2, H0, G)
                self.m1 = ar.f32(2, H0, 8)
                self.m2 = ar.f32(2, H0, 8)
                self.den = ar.f32(2, H0)
                self.am = ar.f32(2, G)
                self.amT = ar.f16(2, S)
                self.f = xn[:, 0:2, :].rearrange("p a b -> p (a b)")
                self.xl = xn[:, 2, :]
                self.uh = ar.f16(2, 2, D)
                self.mb = ar.f32(B, G)
                assert ar.at <= ystart + NT * D
                self.s_z = sem("a0_zero_ready")
                self.s_f = sem("a0_pe_done")
                self.s_hi = sem("a0_hi_done")
                self.s_lo = sem("a0_dve_done")
                self.s_arg = sem("a0_exp_arg")
                self.s_ex = sem("a0_exp_done")
                self.s_ff = sem("a0_film_full")
                self.s_fr = credit("a0_film_free", 2)
                self.s_u = sem("a0_u_ready")
                self.s_r = sem("a0_u_reversed")
                self.s_uc = credit("a0_u_copied", 2)

            def w0(self, at, n, rows_=P):
                return lambda h: wsp[0:rows_, J_X0 % 2, h, at:at + n]

            def pe_part(self):
                pe.wait_ge(s_w, J_X0 + 1)
                pe.wait_ge(self.s_z, 1)
                with pe.Fori(0, B) as i:
                    def cx(k):
                        return lambda h: ctxs[:, h, k, bass.ds(i * G, G)]
                    pe.wait_ge(self.s_fr, 2 * i + 2)
                    pe.wait_ge(self.s_uc, 2 * i + 2)
                    for k in range(KC):
                        mm3(ps[:, 0, 0:G], self.w0(2304 + k * P, P, CP), cx(k), k == 0, k == KC - 1)
                    for k in range(KC):
                        mm3(ps[0:G, 1, 0:D], cx(k), self.w0(2304 + 256 + k * D, D, CP), k == 0, k == KC - 1)
                    for k in range(KD):
                        m = mm3(ps[:, 2, 0:S], self.w0(k * P, P), lambda h: xT[:, h, k, bass.ds(i * S, S)],
                                k == 0, k == KD - 1)
                    m.then_inc(self.s_f, 1)
                    pe.wait_ge(self.s_lo, 4 * i + 1)
                    for t in range(2):
                        m = mm3(ps[:, 3 + t, 0:H0 * G], lambda h: self.q[:, h, t * P:(t + 1) * P],
                                lambda h: self.k[:, h, :], True, True)
                    m.then_inc(self.s_f, 1)
                    pe.wait_ge(self.s_lo, 4 * i + 2)
                    for t in range(2):
                        m = pe.transpose(ps[0:G, 5, t * P:(t + 1) * P], self.am[:, t, :], ident)
                    m.then_inc(self.s_f, 1)
                    pe.wait_ge(self.s_lo, 4 * i + 3)
                    for c in range(KD):
                        m = mm3(ps[:, 6, c * S:(c + 1) * S], lambda h: self.v[0:G, h, c * P:(c + 1) * P],
                                lambda h: self.amT[0:G, h, :], True, True)
                    m.then_inc(self.s_f, 1)
                    pe.wait_ge(self.s_lo, 4 * i + 4)
                    for t in range(2):
                        pe.wait_ge(self.s_fr, 2 * i + t + 1)
                        bk = 7 if t == 0 else 0
                        for k in range(KD):
                            m = mm3(ps[:, bk, :], lambda h: xT[:, h, k, bass.ds(i * S + t * P, P)],
                                    self.w0(256 + k * 2 * D, 2 * D), k == 0, k == KD - 1)
                        m.then_inc(self.s_ff, 1)
                    for t in range(2):
                        pe.wait_ge(self.s_u, 2 * i + t + 1)
                        pe.matmul(ps[:, 1 + t, :], rev[:], self.uh[:, t].rearrange("p h d -> p (h d)"),
                                  start=True, stop=True).then_inc(self.s_r, 1)

            def kblocks(self, h):
                return [(self.k[DH0 * b:DH0 * (b + 1), h, b * G:(b + 1) * G], ps[DH0 * b:DH0 * (b + 1), 0, 0:G])
                        for b in range(H0)]

            def act_part(self):
                act.wait_ge(self.s_z, 1)
                with act.Fori(0, B) as i:
                    act.wait_ge(self.s_f, 4 * i + 1)
                    for o, v in self.kblocks(0):
                        act.activation(o, v, ACT.Copy, scale=INV)
                    act.activation(self.v[0:G, 0, :], ps[0:G, 1, 0:D], ACT.Copy, scale=INV)
                    act.activation(self.q[:, 0, :], ps[:, 2, 0:S], ACT.Copy, scale=INV).then_inc(self.s_hi, 1)
                    act.wait_ge(self.s_arg, i + 1)
                    act.activation(self.s[:], self.s[:], ACT.Exp, scale=DH0 ** -0.5)
                    act.activation(self.w[:], self.w[:], ACT.Exp, scale=DH0 ** -0.5).then_inc(self.s_ex, 1)
                    act.wait_ge(self.s_f, 4 * i + 3)
                    act.activation(self.amT[0:G, 0, :], ps[0:G, 5, 0:S], ACT.Copy).then_inc(self.s_hi, 1)
                    act.wait_ge(self.s_f, 4 * i + 4)
                    settled(act)
                    act.activation(xT[:, 0, :, bass.ds(i * S, S)], shaped(ps[:, 6, :], (KD, S)), ACT.Copy)\
                        .then_inc(self.s_hi, 1)
                    for t in range(2):
                        act.wait_ge(self.s_r, 2 * i + t + 1)
                        settled(act)
                        act.activation(u[:, :, 2 * i + t, :], shaped(ps[:, 1 + t, :], (2, D)), ACT.Copy)\
                            .then_inc(self.s_uc, 1)

            def dve_part(self):
                dve.wait_ge(s_rows, N_ROWS)
                dve.tensor_copy(self.mb[:].rearrange("p a b -> p (a b)"), mk8[:])
                dve.tensor_copy(tmk[:], tm8[:])
                dve.memset(self.k[:].rearrange("p a b -> p (a b)"), 0.0)
                dve.drain()
                dve.tensor_scalar(self.mb[:], self.mb[:], -NEG, NEG, ALU.mult, ALU.add)
                dve.tensor_scalar(tmk[:], tmk[:], 1.0 / H0, None, ALU.mult)
                dve.tensor_scalar(row(R_FI, 4 * D), row(R_FI, 4 * D), sc[:, 8:9], None, ALU.mult)
                dve.drain()
                dve.tensor_scalar(row(R_FI), row(R_FI), 1.0, None, ALU.add)
                dve.tensor_scalar(row(R_FO), row(R_FO), 1.0, None, ALU.add)
                dve.tensor_scalar(sm[:, 4, 1:2], sc[:, 8:9], INV, None, ALU.mult)
                dve.drain().then_inc(self.s_z, 1)
                with dve.Fori(0, B) as i:
                    dve.wait_ge(self.s_hi, 3 * i + 1)
                    for (o, v), (oh, _) in zip(self.kblocks(1), self.kblocks(0)):
                        dve.scalar_tensor_tensor(o, v, INV, oh, ALU.mult, ALU.subtract)
                    dve.scalar_tensor_tensor(self.v[0:G, 1, :], ps[0:G, 1, 0:D], INV, self.v[0:G, 0, :], ALU.mult, ALU.subtract)
                    dve.scalar_tensor_tensor(self.q[:, 1, :], ps[:, 2, 0:S], INV, self.q[:, 0, :], ALU.mult, ALU.subtract)\
                        .then_inc(self.s_lo, 1)
                    dve.drain()
                    dve.wait_ge(self.s_f, 4 * i + 2)
                    for t in range(2):
                        dve.tensor_tensor(self.s[:, t], shaped(ps[:, 3 + t, 0:H0 * G], (H0, G)),
                                          self.mb[:, bass.ds(i, 1), :].to_broadcast([P, H0, G]), ALU.add)
                    dve.drain()
                    for r in range(KTOP // 8):
                        src = self.s if r == 0 else self.w
                        mx = self.m1 if r == 0 else self.m2
                        for t in range(2):
                            for h in range(H0):
                                dve.max(mx[:, t, h, :], src[:, t, h, :])
                        dve.drain()
                        for t in range(2):
                            for h in range(H0):
                                dve.match_replace(self.w[:, t, h, :], mx[:, t, h, :], src[:, t, h, :], NEG)
                        dve.drain()
                    mx = self.m1[:, :, :, 0:1].to_broadcast([P, 2, H0, G])
                    dve.tensor_tensor(self.s[:], self.s[:], mx, ALU.subtract)
                    dve.tensor_tensor(self.w[:], self.w[:], mx, ALU.subtract)
                    dve.drain().then_inc(self.s_arg, 1)
                    dve.wait_ge(self.s_ex, i + 1)
                    dve.tensor_tensor(self.s[:], self.s[:], self.w[:], ALU.subtract)
                    dve.drain()
                    dve.tensor_reduce(self.den[:], self.s[:], X, ALU.add)
                    dve.drain()
                    dve.reciprocal(self.den[:], self.den[:])
                    dve.drain()
                    for t in range(2):
                        dve.tensor_scalar(self.den[:, t, :], self.den[:, t, :], tmk[:, bass.ds(2 * i + t, 1)], None, ALU.mult)
                    dve.drain()
                    dve.tensor_tensor(self.s[:], self.s[:], self.den[:].unsqueeze(3).to_broadcast([P, 2, H0, G]), ALU.mult)
                    dve.drain()
                    dve.tensor_reduce(self.am[:], self.s[:].rearrange("p t h g -> p t g h"), X, ALU.add)
                    dve.drain().then_inc(self.s_lo, 1)
                    dve.wait_ge(self.s_hi, 3 * i + 2)
                    dve.tensor_tensor(self.amT[0:G, 1, :], ps[0:G, 5, 0:S], self.amT[0:G, 0, :], ALU.subtract)\
                        .then_inc(self.s_lo, 1)
                    dve.wait_ge(self.s_hi, 3 * i + 3)
                    dve.tensor_tensor(xT[:, 1, :, bass.ds(i * S, S)], shaped(ps[:, 6, :], (KD, S)),
                                      xT[:, 0, :, bass.ds(i * S, S)], ALU.subtract).then_inc(self.s_lo, 1)
                    for t in range(2):
                        tt_ = 2 * i + t
                        dve.drain()
                        dve.wait_ge(self.s_ff, tt_ + 1)
                        dve.tensor_scalar(self.xl, xtext[:, tt_, :], mean[:, bass.ds(tt_, 1)], rstd[:, bass.ds(tt_, 1)],
                                          ALU.subtract, ALU.mult)
                        dve.scalar_tensor_tensor(self.f, ps[:, 7 if t == 0 else 0, :], sm[:, 4, 1:2], row(R_FI, 2 * D),
                                                 ALU.mult, ALU.add).then_inc(self.s_fr, 1)
                        dve.drain()
                        dve.tensor_tensor(self.xl, self.xl, row(R_GIN), ALU.mult)
                        dve.drain()
                        dve.tensor_tensor(self.xl, self.xl, row(R_BIN), ALU.add)
                        dve.drain()
                        dve.tensor_tensor(self.xl, self.xl, self.f[:, 0:D], ALU.mult)
                        dve.drain()
                        dve.tensor_tensor(self.xl, self.xl, self.f[:, D:2 * D], ALU.add)
                        dve.drain()
                        dve.tensor_copy(self.uh[:, t, 0, :], self.xl)
                        dve.drain()
                        dve.tensor_tensor(self.uh[:, t, 1, :], self.xl, self.uh[:, t, 0, :], ALU.subtract)\
                            .then_inc(self.s_u, 1)

        class Conv:
            def __init__(self):
                self.s_t = [sem("toeplitz_loaded_0"), sem("toeplitz_loaded_1")]
                self.s_tfree = credit("toeplitz_used", 2)
                self.s_y = sem("conv_full")
                self.s_yfree = credit("conv_bank_free", 2)
                self.s_ff = sem("film_out_full")
                self.s_ffree = credit("film_out_free", 2)
                self.f = xn[:].rearrange("p a b -> p (a b)")[:, 0:2 * D]

            def sp_part(self, sp):
                with sp.Fori(0, D // TG // 2) as i:
                    for par in range(2):
                        g = 2 * i + par
                        sp.wait_ge(self.s_tfree, g + 1)
                        src = bass.AP(tensor=kdram.tensor, offset=g * (TG * KROW * 2),
                                      ap=[[2, P], [KROW * 2, TG], [1, 2 * S]])
                        sp.dma_start(tz[:, par].rearrange("p d l c -> p d (l c)"), src).then_inc(self.s_t[par], 16)

            def pe_part(self):
                with pe.Fori(0, D // TG // 2) as i:
                    for par in range(2):
                        g = 2 * i + par
                        pe.wait_ge(self.s_t[par], 16 * (i + 1))
                        pe.wait_ge(self.s_yfree, g + 1)
                        for k in range(TG):
                            d = g * TG + k
                            o = ps[:, par, k * NT:(k + 1) * NT]

                            def uu(h, a0=0, st=1):
                                return u[:, h, a0::st, bass.ds(d, 1)].rearrange("p t o -> p (t o)")

                            mm3(o, lambda h: tz[:, par, k, 0:P, h], lambda h: uu(h), True, True)
                            for a_, b_ in ((0, 0), (0, 1), (1, 0)):
                                m = pe.matmul(o[:, 1::2], tz[:, par, k, P:2 * P, a_], uu(b_, 0, 2), start=False,
                                              stop=True, skip_group_check=True)
                        m.then_inc(self.s_y, 1)
                        pe.drain().then_inc(self.s_tfree, 1)
                with pe.Fori(0, NT // 2) as i:
                    for par in range(2):
                        t = 2 * i + par
                        pe.wait_ge(self.s_ffree, t + 1)
                        for k in range(KD):
                            m = mm3(ps[:, 2 + par, :], lambda h: xT[:, h, k, bass.ds(t * P, P)],
                                    lambda h: wsp[:, J_X0 % 2, h, 1280 + k * 2 * D:1280 + (k + 1) * 2 * D], k == 0, k == KD - 1)
                        m.then_inc(self.s_ff, 1)
                pe.drain().then_inc(s_wfree, 1)

            def dve_part(self):
                with dve.Fori(0, D // TG // 2) as i:
                    for par in range(2):
                        g = 2 * i + par
                        dve.wait_ge(self.s_y, g + 1)
                        dve.tensor_copy(y[:, :, bass.ds(g * TG, TG)].rearrange("p t d -> p d t"),
                                        shaped(ps[:, par, 0:TG * NT], (TG, NT))).then_inc(self.s_yfree, 1)
                dve.drain()
                f = self.f
                with dve.Fori(0, NT // 2) as i:
                    for par in range(2):
                        t = 2 * i + par
                        dve.wait_ge(self.s_ff, t + 1)
                        dve.scalar_tensor_tensor(f, ps[:, 2 + par, :], sm[:, 4, 1:2], row(R_FO, 2 * D), ALU.mult, ALU.add)\
                            .then_inc(self.s_ffree, 1)
                        dve.drain()
                        dve.tensor_tensor(y[:, t, :], y[:, t, :], f[:, 0:D], ALU.mult)
                        dve.drain()
                        dve.tensor_tensor(y[:, t, :], y[:, t, :], f[:, D:2 * D], ALU.add)
                        dve.drain()
                        dve.tensor_tensor(y[:, t, :], y[:, t, :], xtext[:, t, :], ALU.add)
                        dve.drain()

        s_rows = sem("rows_loaded")
        N_CONST, N_ROWS = 16 * 9, 16
        stage = [0]

        def finish_stage():
            n = stage[0]
            prog["dve"].append(lambda: barrier(dve, 2, n))
            prog["act"].append(lambda: barrier(act, 1, n))
            prog["pe"].append(lambda: barrier(pe, 0, n))
            stage[0] += 1

        def norm(n):
            norm_stage(n, stage[0])
            stage[0] += 1

        kg = KGen()
        prog["dve"].append(kg.dve_part)
        prog["act"].append(kg.act_part)
        prog["pe"].append(kg.pe_part)
        prog["dve"].append(lambda: dve.wait_ge(kg.s_kd, 160))
        finish_stage()
        prog["dve"].append(lambda: dve.wait_ge(s_x, 16))
        prog["pe"].append(lambda: pe.wait_ge(s_cdone, 1))
        prog["act"].append(lambda: act.wait_ge(s_cdone, 1))
        norm(Norm("n0", x, keep=xtext))
        inner_stats = Norm("n0in", xtext)
        prog["dve"].append(inner_stats.dve_stats)
        prog["act"].append(inner_stats.act_stats)
        a0 = Attn0()
        prog["dve"].append(a0.dve_part)
        prog["act"].append(a0.act_part)
        prog["pe"].append(a0.pe_part)
        finish_stage()
        cv = Conv()
        prog["dve"].append(cv.dve_part)
        prog["pe"].append(cv.pe_part)
        finish_stage()
        norm(Norm("n0f", y, affine=(row(R_GF), row(R_BF))))
        no_weight = lambda t, e, j: INV
        mlp_up = lambda w, g, k, j: w[:, k * 1024 + j * P:k * 1024 + (j + 1) * P]
        mlp_down = lambda w, j: w[:, 2048 + j * D:2048 + (j + 1) * D]
        f0 = Ffn("mlp0", J_F0, 0, [P] * 8, ACT.Gelu, mlp_up, mlp_down, False, 0, 0, no_weight, y, single=True)
        prog["dve"].append(f0.dve_part)
        prog["act"].append(f0.act_part)
        prog["pe"].append(f0.pe_part)
        last0 = Norm("n0out", y)

        def out0():
            dve.drain()
            last0.dve_stats()
            with dve.Fori(0, NT) as t:
                last0.normalise(xn[:, 0], t)
                dve.drain()
                dve.tensor_tensor(xn[:, 0], xn[:, 0], row(R_GOUT), ALU.mult)
                dve.drain()
                dve.tensor_tensor(xn[:, 0], xn[:, 0], row(R_BOUT), ALU.add)
                dve.drain()
                dve.scalar_tensor_tensor(x[:, t, :], xn[:, 0], tg[:, 0:1], x[:, t, :], ALU.mult, ALU.add)
                dve.drain()
        prog["dve"].append(out0)
        prog["act"].append(last0.act_stats)
        finish_stage()

        def route(layer):
            r = Route(f"route{layer}", layer)
            prog["dve"].append(r.dve_part)
            prog["act"].append(r.act_part)
            prog["pe"].append(r.pe_part)
            finish_stage()

        def ffn(f):
            prog["dve"].append(f.dve_part)
            prog["act"].append(f.act_part)
            prog["pe"].append(f.pe_part)

        by_expert = lambda t, e, j: wgt[:, bass.ds(t, 1), bass.ds(e, 1)].rearrange("p a b -> p (a b)")
        norm(Norm("n0e", x))
        route(0)
        ffn(Ffn("moe0", J_E0, 4, [P] * 8, ACT.Relu, mlp_up, mlp_down, False, 8, 1, by_expert, x))
        finish_stage()

        norm(Norm("n1", x))
        attn_stage(Attn("a1", J_X1, J_X1 + 1, 1024, 64, 1, False), stage[0])
        stage[0] += 1
        norm(Norm("n1e", x))
        route(1)
        ffn(Ffn("moe1", J_E1, 4, [P] * 8, ACT.Gelu, mlp_up, mlp_down, False, 72, 9, by_expert, x))
        finish_stage()

        norm(Norm("n2", x))
        attn_stage(Attn("a2", J_X2, J_X2 + 1, 1024, 128, 2, True), stage[0])
        stage[0] += 1
        norm(Norm("n2e", x))
        route(2)
        cols2 = [P] * 5 + [64]
        up2 = lambda w, g, k, j: w[:, g * 1408 + k * 704 + j * P:g * 1408 + k * 704 + j * P + cols2[j]]
        down2 = lambda w, j: w[:, 2816 + j * D:2816 + (j + 1) * D]
        ffn(Ffn("moe2", J_E2, 4, cols2, ACT.Silu, up2, down2, True, None, None, by_expert, x))
        finish_stage()

        norm(Norm("n3", x))
        attn_stage(Attn("a3", J_X3, J_X3, 512, 64, 3, False), stage[0])
        stage[0] += 1
        norm(Norm("n3e", x))
        route(3)
        up3s = lambda w, g, k, j: w[:, g * 1024 + k * 512 + j * P:g * 1024 + k * 512 + (j + 1) * P]
        down3s = lambda w, j: w[:, 2048 + j * D:2048 + (j + 1) * D]
        shared = lambda t, e, j: wgt[:, bass.ds(t, 1), 16:17].rearrange("p a b -> p (a b)")
        ffn(Ffn("shared3", J_SH, 0, [P] * 4, ACT.Silu, up3s, down3s, True, None, None, shared, x, single=True))
        finish_stage()
        up3 = lambda w, g, k, j: w[:, 768 * j + g * D + k * P:768 * j + g * D + (k + 1) * P]
        down3 = lambda w, j: w[:, 768 * j + 512:768 * (j + 1)]
        by_pack = lambda t, e, j: wgt[:, bass.ds(t, 1), bass.ds(4 * e + j, 1)].rearrange("p a b -> p (a b)")
        ffn(Ffn("moe3", J_E3, 2, [P] * 4, ACT.Silu, up3, down3, True, None, None, by_pack, x, each=True))
        finish_stage()

        FULL = [("w", P, 0, 4096)]
        JOBS = [(J_X0, 1, [("wx0", P, 0, 2304), ("wx0c", CP, 2304, 768)]),
                (J_F0, 1, [("wf0", P, 0, 4096)]),
                (J_E0, 8, [("we0", P, 0, 4096)]),
                (J_X1, 1, [("wx1", P, 0, 4096)]),
                (J_X1 + 1, 1, [("wx1c", CP, 0, 4096)]),
                (J_E1, 8, [("we1", P, 0, 4096)]),
                (J_X2, 1, [("wx2", P, 0, 4096)]),
                (J_X2 + 1, 1, [("wx2c", CP, 0, 4096)]),
                (J_E2, 8, [("we2", P, 0, 4096), ("we2r", 64, 4096, 256)]),
                (J_X3, 1, [("wx3", P, 0, 2048), ("wx3c", CP, 2048, 2048)]),
                (J_SH, 1, [("ws3", P, 0, 3072)]),
                (J_E3, 4, [("we3", P, 0, 3072)])]

        landed = {0: 0, 1: 0}
        plan = []
        for j0, n, pieces in JOBS:
            base = dict(landed)
            plan.append((j0, n, pieces, base))
            for j in range(n):
                landed[(j0 + j) % 2] += 16 * len(pieces)

        def job_loop(fori, j0, n, body):
            if n == 1:
                body(j0, j0 % 2, 0, 0)
            else:
                with fori(0, n // 2) as i:
                    for off in range(2):
                        body(2 * i + (j0 + off), (j0 + off) % 2, 2 * i + off, i)

        tmpw = wsp[:, 1].rearrange("p h n -> p (h n)").bitcast(F32)
        ctxr = tmpw[0:CP, 0:KC * GA]
        rwr = tmpw[:, KC * GA:KC * GA + NRC]
        b2r = raw[0:33, 1, :]
        s_tmp = sem("temporaries_loaded")
        s_zero = sem("skip_cleared")

        @block.sync
        def _(sp):
            sp.dma_start(cst[:], a["cst"]).then_inc(s_const, 16)
            sp.dma_start(xT[:].rearrange("p a b c -> p (a b c)")[:, 0:8 * D].bitcast(F32), a["s4"]).then_inc(s_const, 16)
            sp.dma_start(LDT, a["ldt"].partition_broadcast(P)).then_inc(s_const, 16)
            sp.dma_start(sc[:], a["sc"].partition_broadcast(P)).then_inc(s_const, 16)
            sp.dma_start(mk8[:], a["cmask"].partition_broadcast(P)).then_inc(s_const, 16)
            sp.dma_start(tm8[:], a["tmask"]).then_inc(s_const, 16)
            sp.wait_ge(s_zero, 1)
            sp.dma_start(dsk[0:P:16, :], a["dskip"]).then_inc(s_const, 16)
            sp.dma_start(b1c[:], a["b1"]).then_inc(s_const, 16)
            sp.dma_start(brow[:].rearrange("p a b -> p (a b)"), a["brow"].partition_broadcast(P)).then_inc(s_const, 16)
            sp.dma_start(ctxr, a["ctx"]).then_inc(s_tmp, 16)
            sp.dma_start(rwr, a["wr"]).then_inc(s_tmp, 16)
            for r in (0, 32):
                sp.dma_start(b2r[r:r + 1], a["b2"]).then_inc(s_tmp, 16)
            sp.dma_start(x[:], a["x"]).then_inc(s_x, 16)

            def load(job, slot, e, seen, pieces, family):
                if not (isinstance(job, int) and job < 2):
                    sp.wait_ge(s_w, job - 1)
                elif job == 1:
                    sp.wait_ge(s_cdone, 1)
                for name, rows_, at, n in pieces:
                    src = a[name] if not family else a[name][bass.ds(e, 1)].rearrange("e p n -> (e p) n")
                    sp.dma_start(raw[0:rows_, slot, at:at + n], src).then_inc(s_raw[slot], 16)

            for j0, n, pieces, base in plan:
                if j0 == J_E0:
                    kg.store(sp)
                    for s in s_end:
                        sp.wait_ge(s, 1)
                    sp.dma_start(rows[:], a["rows"].partition_broadcast(P)).then_inc(s_rows, 16)
                    cv.sp_part(sp)
                job_loop(sp.Fori, j0, n, lambda j, s, e, seen: load(j, s, e, seen, pieces, n > 1))
            for s in s_end:
                sp.wait_ge(s, stage[0])
            sp.dma_start(out, x[:]).then_inc(s_out, 16)
            sp.wait_ge(s_out, 16)

        @block.gpsimd
        def _(pool):
            start_carrier(pool)
            pool.memset(dsk[:], 0.0).then_inc(s_zero, 1)
            for col, (s, n) in enumerate(credits):
                pool.memset(spare[:, col:col + 1], 0.0).then_inc(s, n)
            pool.memset(ones[:], 1.0)
            pool.memset(eps_t[:], EPS)
            pool.memset(b2s[:].rearrange("p a b -> p (a b)"), 0.0)
            pool.wait_ge(s_const, N_CONST)
            pool.tensor_copy(tri[:], cst[:, C_TRI:C_TRI + P])
            pool.tensor_copy(rev[:], cst[:, C_REV:C_REV + P])
            pool.wait_ge(s_tmp, 64)
            n_step = [0]

            def step(i):
                n_step[0] += 1
                i.then_inc(s_pst, 1)
                pool.wait_ge(s_pst, n_step[0])
            ch = [ctxs[:, h].rearrange("p k n -> p (k n)") for h in range(2)]
            step(pool.tensor_copy(ch[0], ctxr))
            pool.tensor_tensor(ch[1], ctxr, ch[0], ALU.subtract)
            step(pool.tensor_scalar(rwr, rwr, WSCALE, 1.0, ALU.mult, ALU.mult))
            step(pool.tensor_copy(rws[:, 0], rwr))
            pool.tensor_tensor(rws[:, 1], rwr, rws[:, 0], ALU.subtract)
            b2f = b2s[:].rearrange("p a b -> p (a b)")
            for r in (0, 32):
                step(pool.tensor_scalar(b2r[r:r + 1], b2r[r:r + 1], WSCALE, 1.0, ALU.mult, ALU.mult))
                step(pool.tensor_copy(b2f[r:r + 1], b2r[r:r + 1]))
            step(pool.tensor_tensor(b2f[32:33], b2r[32:33], b2f[32:33], ALU.subtract))
            pool.drain().then_inc(s_cdone, 1)
            steps_done = n_step[0]

            for j0, n, pieces, base in plan:
                def split(j, slot, e, seen):
                    pool.wait_ge(s_raw[slot], base[slot] + 16 * len(pieces) * (seen + 1))
                    if not (isinstance(j, int) and j < 2):
                        pool.wait_ge(s_wfree, j - 1)
                    pool.tensor_tensor(spare[:, 63:64], spare[:, 0:1], spare[:, 0:1], ALU.mult)
                    for _, rows_, at, w in pieces:
                        v = raw[0:rows_, slot, at:at + w]
                        hi, lo = (wsp[0:rows_, slot, h, at:at + w] for h in range(2))
                        pool.tensor_scalar(v, v, WSCALE, 1.0, ALU.mult, ALU.mult)
                        pool.drain()
                        pool.tensor_copy(hi, v)
                        pool.drain()
                        pool.tensor_tensor(lo, v, hi, ALU.subtract)
                    pool.drain().then_inc(s_w, 1)
                job_loop(pool.Fori, j0, n, split)

        @block.tensor
        def _(_pe):
            start_carrier(pe)
            for part in prog["pe"]:
                part()

        @block.scalar
        def _(_act):
            start_carrier(act)
            for part in prog["act"]:
                part()

        @block.vector
        def _(_dve):
            for part in prog["dve"]:
                part()


def kernel(**inputs):
    import numpy as np
    import concourse.bacc as bacc
    from concourse.bass_utils import run_bass_kernel_spmd as run

    g = {k: np.asarray(v) for k, v in inputs.items()}
    c = np.ascontiguousarray

    def kp(w, rows=P):
        k, n = w.shape
        return w.reshape(k // rows, rows, n).transpose(1, 0, 2).reshape(rows, -1)

    def cat(*parts):
        return c(np.concatenate(parts, axis=-1))

    cst = np.zeros((P, NCST), np.float32)
    r = np.arange(P)
    cst[:, 0:P] = np.eye(P)
    cst[:, C_TRI:C_TRI + P] = r[:, None] < r[None, :]
    cst[:, C_IOTA:C_IOTA + 16] = np.arange(16)
    cst[:, C_K16:C_K16 + 16] = 16 * np.arange(16)
    cst[:, C_MASK:C_MASK + 8] = (r[:, None] // 16) == np.arange(8)
    cst[:, C_REV:C_REV + P] = np.eye(P)[::-1]
    ph = np.where(r[:, None] < 64, [[0.25, 0.25, 0.5]], [[0.5, 0.0, 0.25]])
    cst[:, C_PH:C_PH + 3] = ph
    cst[:, C_PHR:C_PHR + 3] = ph * -SIN_SCALE
    a = {"cst": cst}
    a["x"] = c(g["x"].reshape(NT, P, D).transpose(1, 0, 2))
    a["ctx"] = c(kp(g["ctx_768"].reshape(GA, DV).T, CP))
    a["s4"] = c(np.tile(np.concatenate([g["L0_xattn_" + n].T for n in ("A_re", "A_im", "C_re", "C_im")], axis=1), (2, 1)))
    a["ldt"] = c(g["L0_xattn_log_dt"])
    a["sc"] = cat(g["g_xattn"], g["g_ffn"], g["L0_xattn_mod_gate"].reshape(1), g["L1_ffn_br"])
    a["cmask"] = c(g["mask_BxS2_bf1"].reshape(GA).view(np.uint8))
    a["tmask"] = c(g["mask_BxS_bf1"].reshape(NT, P).T.view(np.uint8))
    a["dskip"] = c(g["L0_xattn_D_skip"].reshape(D // 8, 8).T)
    a["b1"] = cat(g["L0_xattn_b1"].reshape(8, P).T, g["L0_ffn_b1"].reshape(64, P).T, g["L1_ffn_b1"].reshape(64, P).T)
    a["brow"] = cat(g["L1_xattn_b_out"], g["L2_xattn_bout"], g["L3_xattn_bo"])
    a["wr"] = cat(kp(g["L0_ffn_w_router"]), kp(g["L1_ffn_Wr"]), kp(g["L2_ffn_router_w"].T),
                  kp(np.concatenate([g["L3_ffn_Wg"].T, g["L3_ffn_Wsg"].T], axis=1)))
    a["b2"] = cat(g["L0_xattn_b2"].reshape(1, -1), g["L0_ffn_b2"].reshape(1, -1), g["L1_ffn_b2"].reshape(1, -1))
    L0x = lambda n: g["L0_xattn_" + n]
    a["rows"] = cat(*(L0x(n) for n in ("g_norm_in", "b_norm_in", "g_ffn", "b_ffn", "g_norm_out", "b_norm_out",
                                       "b_film_in", "b_film_out")))
    a["wx0"] = cat(kp(L0x("Wq")), kp(L0x("W_film_in")), kp(L0x("W_film_out")))
    a["wx0c"] = cat(kp(L0x("Wk"), CP), kp(L0x("Wv"), CP))
    a["wf0"] = cat(kp(L0x("W1")), kp(L0x("W2")))
    a["we0"] = c(np.stack([cat(kp(g["L0_ffn_w1"][e]), kp(g["L0_ffn_w2"][e])) for e in range(8)]))
    a["wx1"] = cat(kp(g["L1_xattn_w_q"]), kp(g["L1_xattn_w_out"]))
    a["wx1c"] = cat(kp(g["L1_xattn_w_k"], CP), kp(g["L1_xattn_w_v"], CP))
    a["we1"] = c(np.stack([cat(kp(g["L1_ffn_W1"][e]), kp(g["L1_ffn_W2"][e])) for e in range(8)]))
    a["wx2"] = cat(kp(g["L2_xattn_Wq"]), kp(g["L2_xattn_Wout"]))
    a["wx2c"] = cat(kp(g["L2_xattn_Wk"], CP), kp(g["L2_xattn_Wv"], CP))
    a["we2"] = c(np.stack([cat(kp(g["L2_ffn_gate_w"][e].T), kp(g["L2_ffn_up_w"][e].T),
                               kp(g["L2_ffn_down_w"][e].T[0:640])) for e in range(8)]))
    a["we2r"] = c(np.stack([g["L2_ffn_down_w"][e].T[640:704] for e in range(8)]))
    a["wx3"] = cat(kp(g["L3_xattn_Wq"]), kp(g["L3_xattn_Wo"]))
    a["wx3c"] = cat(kp(g["L3_xattn_Wk"], CP), kp(g["L3_xattn_Wv"], CP))
    a["ws3"] = cat(kp(g["L3_ffn_Ws_gate"].T), kp(g["L3_ffn_Ws_up"].T), kp(g["L3_ffn_Ws_down"].T))
    a["we3"] = c(np.stack([cat(*(v for e in range(4 * p, 4 * p + 4) for v in (
        kp(g["L3_ffn_We_gate"][e].T), kp(g["L3_ffn_We_up"][e].T), g["L3_ffn_We_down"][e].T))) for p in range(4)]))

    nc = bacc.Bacc("TRN2", target_bir_lowering=False, num_devices=1)
    aps = {n: nc.dram_tensor("in_" + n, v.shape, mybir.dt.from_np(v.dtype), kind="ExternalInput").ap()
           for n, v in a.items()}
    o = nc.dram_tensor("out_x", (P, NT, D), F32, kind="ExternalOutput").ap()
    build(nc, aps, o)
    res = run(nc, [{"in_" + n: v for n, v in a.items()}], core_ids=[0])
    return c(res.results[0]["out_x"].transpose(1, 0, 2).reshape(B, S, D))
```

```python
import math
from contextlib import ExitStack

import concourse.bass as bass
from concourse import mybir

F32 = mybir.dt.float32
F16 = mybir.dt.float16
U32 = mybir.dt.uint32
U8 = mybir.dt.uint8
ALU = mybir.AluOpType
ACT = mybir.ActivationFunctionType
X = mybir.AxisListType.X

P = 128
B, S, D = 8, 256, 256
NT = B * S // P
KD = D // P
G, DV = 77, 192
KC, CP = 2, DV // 2
GA = B * G
EPS = 1e-5
WSCALE = 64.0
INV = 1.0 / WSCALE
NEG = -1.0e30

SLOT = 4352
NS4, LAGS = 64, S
TWO_PI = 2.0 * math.pi
SIN_SCALE = -6.2831850
ROUND = 12582912.0
CAPACITY = int(1.5 * B * S * 2 / 8)
SLOTS = 8 * CAPACITY
KROW = 384

R_GIN, R_BIN, R_GF, R_BF, R_GOUT, R_BOUT = range(6)
R_FI, R_FO, NR_ = 6, 8, 10
NROW = NR_ * D

C_TRI, C_IOTA, C_K16, C_MASK, C_PH, C_PHR, C_REV, C_SPARE, NCST = 128, 256, 272, 288, 296, 300, 304, 432, 464
ARENA = 20664

ROUTERS = [(0, 8), (16, 8), (32, 8), (48, 17)]
NRC = 48 + 34

J_X0, J_F0, J_E0, J_X1, J_E1, J_X2, J_E2, J_X3, J_SH, J_E3 = 0, 1, 2, 10, 12, 20, 22, 30, 31, 32


def build(nc, a, out):
    ctx = ExitStack()
    with ctx:
        def sb(name, shape, dt=F32):
            return ctx.enter_context(nc.sbuf_tensor(name, shape, dt))

        def sem(name):
            return ctx.enter_context(nc.semaphore(name))

        x = sb("x_resid", [P, NT, D])
        xT = sb("xT", [P, 2, KD, B * S], F16)
        raw = sb("w_raw", [P, 2, SLOT])
        wsp = sb("w_split", [P, 2, 2, SLOT], F16)
        ctxs = sb("ctx_split", [CP, 2, KC, GA], F16)
        rws = sb("router_split", [P, 2, NRC], F16)
        b1e = sb("b1_of_expert", [P, 8])
        b1c = sb("b1_cols", [P, 136])
        b2s = sb("b2_split", [33, 17, D], F16)
        ones = sb("ones16", [P, P], F16)
        tri = sb("tri16", [P, P], F16)
        rev = sb("rev16", [P, P], F16)
        cst = sb("consts", [P, NCST])
        ident, iota = cst[:, 0:P], cst[:, C_IOTA:C_IOTA + 16]
        sc = sb("scalars", [P, 17])
        tg = sb("tanh_gates", [P, 8])
        brow = sb("bout_rows", [P, 3, D])
        wgt = sb("expert_weights", [P, NT, 17])
        st6 = sb("bn_stats", [P, NT, 6])
        mean = sb("mean", [P, NT])
        rstd = sb("rstd", [P, NT])
        sm = sb("small", [P, 8, NT])
        xn = sb("xn", [P, 4, D])
        mk8 = sb("ctx_mask_u8", [P, GA], U8)
        tm8 = sb("text_mask_u8", [P, NT], U8)
        dsk = sb("skip", [P, D // 8])
        tmk = sb("text_mask", [P, NT])
        eps_t = sb("eps", [P, 1])
        spare = sb("credit_dummy", [1, 64])
        arena = sb("arena", [P, ARENA])

        ps = ctx.enter_context(nc.psum_tensor("ps", [P, 8, 512], F32))
        kdram = nc.dram_tensor("s4_kernel", [D, KROW, 2], F16, kind="Internal").ap()

        xs = nc.dram_tensor("dispatched", [SLOTS + 2 * B * S, D], F32, kind="Internal").ap()
        ys = nc.dram_tensor("expert_rows", [SLOTS, D], F32, kind="Internal").ap()

        class Area:
            def __init__(self, at=0):
                self.at = at

            def f32(self, *dims):
                n = math.prod(dims)
                v = arena[:, self.at:self.at + n]
                self.at += n
                assert self.at <= ARENA, self.at
                return shaped(v, dims)

            def f16(self, *dims):
                n = math.prod(dims)
                v = arena[:, self.at:self.at + n // 2].bitcast(F16)
                self.at += n // 2
                assert self.at <= ARENA, self.at
                return shaped(v, dims)

        def shaped(v, dims):
            if len(dims) == 1:
                return v
            names = "abcde"[:len(dims)]
            return v.rearrange(f"p ({' '.join(names)}) -> p {' '.join(names)}",
                               **{n: d for n, d in zip(names, dims)})

        s_const = sem("const_loaded")
        s_x = sem("x_loaded")
        s_pool = sem("pool_consts_ready")
        s_cdone = sem("const_split_ready")
        s_raw = [sem("raw_loaded_0"), sem("raw_loaded_1")]
        s_w = sem("weights_split")
        s_wfree = sem("weights_used")
        s_pst = sem("pool_split_step")
        s_end = [sem(f"stage_end_{e}") for e in ("pe", "act", "dve")]
        s_out = sem("out_stored")
        credits = []

        def credit(name, n):
            s = sem(name)
            credits.append((s, n))
            return s

        block = ctx.enter_context(nc.Block())
        prog = {"pe": [], "act": [], "dve": []}
        pe, act, dve = nc.tensor, nc.scalar, nc.vector

        def barrier(eng, me, stage):
            eng.drain().then_inc(s_end[me], 1)
            for s in s_end:
                eng.wait_ge(s, stage + 1)

        def slot16(job):
            return wsp[:, job % 2]

        def mm3(out_ap, lhs, rhs, start, stop):
            pe.matmul(out_ap, lhs(0), rhs(0), start=start, stop=False)
            pe.matmul(out_ap, lhs(0), rhs(1), start=False, stop=False)
            return pe.matmul(out_ap, lhs(1), rhs(0), start=False, stop=stop)

        def bcast(v, n):
            return v.unsqueeze(1).to_broadcast([v.shape[0], n, v.shape[1]])

        def nothing(*args):
            pass

        carrier = {id(e): e.alloc_register("wait_carrier") for e in (pe, act, nc.gpsimd)}

        def settled(eng):
            eng.reg_add(carrier[id(eng)], carrier[id(eng)], 1)

        def start_carrier(eng):
            eng.reg_mov(carrier[id(eng)], 0)

        class Norm:
            stat_runs = 0
            tile_runs = 0
            var, std = sem("norm_var_ready"), sem("norm_std_ready")
            xn, full, hi = sem("norm_tile_ready"), sem("norm_tile_transposed"), sem("norm_hi_ready")
            free = credit("norm_bank_free", 4)

            def __init__(self, name, src, keep=None, affine=None):
                self.src, self.keep, self.affine = src, keep, affine
                self.rs = Norm.stat_runs
                Norm.stat_runs += 1
                self.rt = None

            def dve_stats(self):
                with dve.Fori(0, NT) as t:
                    dve.bn_stats(st6[:, t, :], self.src[:, t, :])
                dve.drain()
                dve.tensor_tensor(mean[:], st6[:, :, 1], st6[:, :, 4], ALU.add)
                dve.tensor_tensor(sm[:, 0], st6[:, :, 1], st6[:, :, 4], ALU.subtract)
                dve.tensor_tensor(sm[:, 1], st6[:, :, 2], st6[:, :, 5], ALU.add)
                dve.drain()
                dve.tensor_scalar(mean[:], mean[:], 0.5, None, ALU.mult)
                dve.tensor_tensor(sm[:, 0], sm[:, 0], sm[:, 0], ALU.mult)
                dve.tensor_scalar(sm[:, 1], sm[:, 1], 1.0 / D, None, ALU.mult)
                dve.drain()
                dve.scalar_tensor_tensor(sm[:, 2], sm[:, 0], 0.25, sm[:, 1], ALU.mult, ALU.add)\
                    .then_inc(self.var, 1)
                dve.wait_ge(self.std, self.rs + 1)
                dve.reciprocal(rstd[:], sm[:, 3])
                dve.drain()

            def act_stats(self):
                act.wait_ge(self.var, self.rs + 1)
                act.activation(sm[:, 3], sm[:, 2], ACT.Sqrt, bias=eps_t[:, 0:1]).then_inc(self.std, 1)

            def normalise(self, dst, t):
                return dve.tensor_scalar(dst, self.src[:, t, :], mean[:, bass.ds(t, 1)],
                                         rstd[:, bass.ds(t, 1)], ALU.subtract, ALU.mult)

            def dve_tiles(self):
                with dve.Fori(0, NT // 4) as i:
                    for k in range(4):
                        if self.keep is not None:
                            self.normalise(self.keep[:, 4 * i + k, :], 4 * i + k)
                        m = self.normalise(xn[:, k], 4 * i + k)
                        if self.affine is None:
                            m.then_inc(self.xn, 1)
                    if self.affine is not None:
                        g, b = self.affine
                        dve.drain()
                        dve.tensor_tensor(xn[:], xn[:], bcast(g, 4), ALU.mult)
                        dve.drain()
                        for k in range(4):
                            dve.tensor_tensor(xn[:, k], xn[:, k], b, ALU.add).then_inc(self.xn, 1)
                    for k in range(4):
                        t = 4 * i + k
                        dve.wait_ge(self.hi, self.rt + t + 1)
                        dve.tensor_tensor(xT[:, 1, :, bass.ds(t * P, P)], ps[:, k, 0:D].rearrange("p (c n) -> p c n", c=KD),
                                          xT[:, 0, :, bass.ds(t * P, P)], ALU.subtract).then_inc(self.free, 1)

            def pe_tiles(self):
                with pe.Fori(0, NT // 4) as i:
                    for k in range(4):
                        t = 4 * i + k
                        pe.wait_ge(self.xn, self.rt + t + 1)
                        pe.wait_ge(self.free, self.rt + t + 1)
                        for c in range(KD):
                            m = pe.transpose(ps[:, k, c * P:(c + 1) * P], xn[:, k, c * P:(c + 1) * P], ident)
                        m.then_inc(self.full, 1)

            def act_tiles(self):
                with act.Fori(0, NT // 4) as i:
                    for k in range(4):
                        t = 4 * i + k
                        act.wait_ge(self.full, self.rt + t + 1)
                        settled(act)
                        act.activation(xT[:, 0, :, bass.ds(t * P, P)], ps[:, k, 0:D].rearrange("p (c n) -> p c n", c=KD),
                                       ACT.Copy).then_inc(self.hi, 1)

        def norm_stage(n, stage):
            n.rt = Norm.tile_runs * NT
            Norm.tile_runs += 1
            prog["dve"] += [n.dve_stats, n.dve_tiles, lambda: barrier(dve, 2, stage)]
            prog["act"] += [n.act_stats, n.act_tiles, lambda: barrier(act, 1, stage)]
            prog["pe"] += [n.pe_tiles, lambda: barrier(pe, 0, stage)]

        ROUTE_END = 2560

        class Route:
            def __init__(self, name, layer):
                self.layer = layer
                self.col, self.E = ROUTERS[layer]
                self.full = sem(name + "_logits_ready")
                self.arg = sem(name + "_exp_arg_ready")
                self.ex = sem(name + "_exp_ready")
                self.sel = sem(name + "_sel_ready")
                self.pos = sem(name + "_positions_ready")
                E = self.E
                ar = Area()
                self.L = ar.f32(NT, 17)
                self.mx = ar.f32(NT, 8)
                self.ix = ar.f32(NT, 8)
                self.ixf = ar.f32(NT, 2)
                self.io = ar.f32(16)
                self.e = ar.f32(NT, 17)
                self.s = ar.f32(NT, 16)
                self.t = ar.f32(NT, 16)
                self.h = ar.f16(NT, 16)
                self.den = ar.f32(NT)
                if layer == 0:
                    self.oh = ar.f32(NT, 2, 8)
                    self.pr = ar.f32(NT, 2, 8)
                    self.slot = ar.f32(NT, 2)
                    self.kept = ar.f32(NT, 2)
                    self.to, self.fro = (ar.f32(NT, 2).bitcast(U32) for _ in range(2))
                    self.w2 = ar.f32(NT, 2)
                    self.s_ix = sem(name + "_slots_ready")
                    assert ar.at <= ROUTE_END

            def slots(self):
                pos = ps[:, 1, 0:NT * 8].rearrange("p (t e) -> p t e", t=NT).unsqueeze(2).to_broadcast([P, NT, 2, 8])
                w = wgt[:, :, 0:8].unsqueeze(2).to_broadcast([P, NT, 2, 8])
                io = iota[:, 0:8].unsqueeze(1).unsqueeze(1).to_broadcast([P, NT, 2, 8])
                spare_row = cst[:, C_SPARE:C_SPARE + 2 * NT].rearrange("p (t k) -> p t k", k=2)
                dve.tensor_tensor(self.oh, io, self.ixf[:].unsqueeze(3).to_broadcast([P, NT, 2, 8]), ALU.is_equal)
                dve.drain()
                dve.tensor_tensor(self.pr, self.oh, pos, ALU.mult)
                dve.tensor_tensor(self.oh, self.oh, w, ALU.mult)
                dve.drain()
                dve.tensor_reduce(self.slot, self.pr, X, ALU.add)
                dve.tensor_reduce(self.w2, self.oh, X, ALU.add)
                dve.drain()
                dve.tensor_scalar(self.kept, self.slot, float(CAPACITY), None, ALU.is_lt)
                dve.scalar_tensor_tensor(self.slot, self.ixf, float(CAPACITY), self.slot, ALU.mult, ALU.add)
                dve.drain()
                dve.tensor_tensor(self.pr[:, :, :, 0], self.slot, spare_row, ALU.subtract)
                dve.tensor_tensor(self.pr[:, :, :, 1], self.slot, self.kept, ALU.mult)
                dve.drain()
                dve.tensor_tensor(self.pr[:, :, :, 0], self.pr[:, :, :, 0], self.kept, ALU.mult)
                dve.tensor_copy(self.fro, self.pr[:, :, :, 1])
                dve.drain()
                dve.tensor_tensor(self.pr[:, :, :, 0], self.pr[:, :, :, 0], spare_row, ALU.add)
                dve.drain()
                dve.tensor_copy(self.to, self.pr[:, :, :, 0])
                dve.drain().then_inc(self.s_ix, 1)

            def pe_part(self):
                E, c0 = self.E, self.col
                with pe.Fori(0, NT) as t:
                    for c in range(KD):
                        m = mm3(ps[:, 0, bass.ds(t * E, E)], lambda h: xT[:, h, c, bass.ds(t * P, P)],
                                lambda h: rws[:, h, c0 + c * E:c0 + (c + 1) * E], c == 0, c == KD - 1)
                    m.then_inc(self.full, 1)
                if self.layer == 0:
                    pe.wait_ge(self.sel, 1)
                    pe.matmul(ps[:, 1, 0:NT * 8], tri[:], self.h[:, :, 0:8], start=True, stop=True)
                    for t in range(NT - 1):
                        rest = NT - 1 - t
                        src = self.h[:, t:t + 1, 0:8].to_broadcast([P, rest, 8])
                        m = pe.matmul(ps[:, 1, (t + 1) * 8:NT * 8], ones[:], src, start=False,
                                      stop=True, skip_group_check=True)
                    m.then_inc(self.pos, 1)

            def act_part(self):
                ne = 16 if self.layer == 3 else 8
                act.wait_ge(self.arg, 1)
                act.activation(self.e[:, :, 0:self.E], self.e[:, :, 0:self.E], ACT.Exp).then_inc(self.ex, 1)

            def dve_part(self):
                E, layer = self.E, self.layer
                ne = 16 if layer == 3 else 8
                L, e = self.L, self.e
                dve.wait_ge(self.full, NT)
                dve.tensor_scalar(L[:, :, 0:E], ps[:, 0, 0:NT * E].rearrange("p (t e) -> p t e", t=NT), INV, None, ALU.mult)
                dve.drain()
                if layer == 1:
                    dve.tensor_tensor(L[:, :, 0:E], L[:, :, 0:E], bcast(sc[:, 9:17], NT), ALU.add)
                    dve.drain()
                for t in range(NT):
                    dve.max(self.mx[:, t, :], L[:, t, 0:ne])
                dve.drain()
                m1 = self.mx[:, :, 0:1].to_broadcast([P, NT, ne])
                m2 = self.mx[:, :, 1:2].to_broadcast([P, NT, ne])
                dve.tensor_tensor(e[:, :, 0:ne], L[:, :, 0:ne], m1, ALU.subtract)
                if layer == 3:
                    dve.tensor_scalar(e[:, :, 16:17], L[:, :, 16:17], -1.0, None, ALU.mult)
                dve.drain().then_inc(self.arg, 1)
                s, t2 = self.s[:, :, 0:ne], self.t[:, :, 0:ne]
                if layer == 1:
                    dve.tensor_tensor(s, L[:, :, 0:ne], m2, ALU.is_ge)
                else:
                    for t in range(NT):
                        dve.max_index(self.ix[:, t, :].bitcast(U32), self.mx[:, t, :], L[:, t, 0:ne])
                    dve.drain()
                    dve.tensor_copy(self.ixf[:], self.ix[:, :, 0:2].bitcast(U32))
                    dve.drain()
                    io = bcast(iota[:, 0:ne], NT)
                    dve.tensor_tensor(s, io, self.ixf[:, :, 0:1].to_broadcast([P, NT, ne]), ALU.is_equal)
                    dve.tensor_tensor(t2, io, self.ixf[:, :, 1:2].to_broadcast([P, NT, ne]), ALU.is_equal)
                    dve.drain()
                    dve.tensor_tensor(s, s, t2, ALU.add)
                dve.drain()
                if layer == 0:
                    dve.tensor_copy(self.h[:, :, 0:8], s).then_inc(self.sel, 1)
                dve.wait_ge(self.ex, 1)
                den = self.den[:]
                if layer == 2:
                    dve.tensor_reduce(den, e[:, :, 0:ne], X, ALU.add)
                    dve.drain()
                dve.tensor_tensor(s, s, e[:, :, 0:ne], ALU.mult)
                dve.drain()
                if layer != 2:
                    dve.tensor_reduce(den, s, X, ALU.add)
                    dve.drain()
                dve.reciprocal(den, den)
                dve.drain()
                dve.tensor_scalar(den, den, tg[:, 4 + layer:5 + layer], INV, ALU.mult, ALU.mult)
                dve.drain()
                dve.tensor_tensor(wgt[:, :, 0:ne], s, den.unsqueeze(2).to_broadcast([P, NT, ne]), ALU.mult)
                if layer == 0:
                    dve.wait_ge(self.pos, 1)
                    dve.tensor_scalar(t2, ps[:, 1, 0:NT * 8].rearrange("p (t e) -> p t e", t=NT), float(CAPACITY), None, ALU.is_lt)
                    dve.drain()
                    dve.tensor_tensor(wgt[:, :, 0:8], wgt[:, :, 0:8], t2, ALU.mult)
                    dve.drain()
                    self.slots()
                if layer == 3:
                    dve.tensor_scalar(e[:, :, 16:17], e[:, :, 16:17], 1.0, None, ALU.add)
                    dve.drain()
                    dve.reciprocal(e[:, :, 16:17], e[:, :, 16:17])
                    dve.drain()
                    dve.tensor_scalar(wgt[:, :, 16:17], e[:, :, 16:17], tg[:, 7:8], INV, ALU.mult, ALU.mult)
                dve.drain()

        TOK = 512
        NCH = B * S // TOK
        Q = TOK // P

        class Ffn:

            def __init__(self, name, job, pairs, cols, act_fn, up, down, gated, bias1, b2_row,
                         weight, dst, each=False, area=0, single=False):
                self.name, self.job, self.pairs, self.single = name, job, pairs, single
                self.cols, self.fn, self.up, self.down = cols, act_fn, up, down
                self.gated, self.bias1, self.b2_row = gated, bias1, b2_row
                self.weight, self.dst, self.each = weight, dst, each
                self.nh = len(cols)
                self.R = 2 if gated else 4
                self.lag = 1 if each else 2
                ar = Area(area)
                self.hf = ar.f32(self.R, TOK)
                self.hh = ar.f16(self.R, 2, TOK)
                self.s_up = sem(name + "_up_full")
                self.s_act = credit(name + "_act_done", self.R)
                self.s_upfree = credit(name + "_gate_product_done", self.R)
                self.s_hhi = sem(name + "_hi_ready")
                self.s_h = credit(name + "_hidden_ready", self.R)
                self.s_hfree = credit(name + "_down_done", self.R)
                self.s_yfree = credit(name + "_y_free", 2 if each else 1)

            def bank(self, j):
                return 2 * (j % 2) if self.gated else j % 4

            def schedule(self, fori, unit_up, unit_down, begin, end):
                nh, lag = self.nh, self.lag

                def steps(i0, off, cont_in, cont_out):
                    if not cont_in:
                        begin(i0, off)
                        for j in range(lag):
                            unit_up(i0, off, 0, j)
                    with fori(0, NCH - 1) as c:
                        for j in range(nh):
                            nx = j + lag
                            unit_up(i0, off, c, nx) if nx < nh else unit_up(i0, off, c + 1, nx - nh)
                            unit_down(i0, off, c, j)
                    for j in range(nh):
                        nx = j + lag
                        if nx < nh:
                            unit_up(i0, off, NCH - 1, nx)
                        elif cont_out:
                            if nx == nh:
                                begin(i0, off + 1)
                            unit_up(i0, off + 1, 0, nx - nh)
                        unit_down(i0, off, NCH - 1, j)
                    end(i0, off)

                if self.single:
                    steps(0, 0, False, False)
                else:
                    with fori(0, self.pairs) as i:
                        steps(2 * i, 0, False, True)
                        steps(2 * i, 1, True, False)

            def unit(self, i0, off, c, j):
                return ((i0 + off) * NCH + c) * self.nh + j

            def pe_part(self):
                def begin(i0, off):
                    pe.wait_ge(s_w, self.job + i0 + off + 1)

                def unit_up(i0, off, c, j):
                    w = wsp[:, (self.job + off) % 2]
                    n = self.unit(i0, off, c, j)
                    m = self.cols[j]
                    bk = self.bank(j)
                    pe.wait_ge(self.s_upfree if self.gated else self.s_act, n + 1)
                    if self.gated and m < P:
                        pe.matmul(ps[0:m, bk, 0:1], w[:, 0, 0:m], w[:, 0, 0:1], start=True, stop=True)
                    for g in range(2 if self.gated else 1):
                        for k in range(KD):
                            last = mm3(ps[0:m, bk + g, :],
                                       lambda h: self.up(w[:, h], g, k, j),
                                       lambda h: xT[:, h, k, bass.ds(c * TOK, TOK)], k == 0, k == KD - 1)
                    last.then_inc(self.s_up, 1)

                def unit_down(i0, off, c, j):
                    w = wsp[:, (self.job + off) % 2]
                    n = self.unit(i0, off, c, j)
                    step = (i0 + off) * NCH + c
                    m = self.cols[j]
                    r = j % self.R
                    pe.wait_ge(self.s_h, n + 1 + self.R)
                    first = self.each or j == 0
                    final = self.each or j == self.nh - 1
                    if first:
                        pe.wait_ge(self.s_yfree, (n if self.each else step) + 1)
                    for q in range(Q):
                        if self.each:
                            o = ps[:, 4 + 2 * (j % 2) + q // 2, (q % 2) * D:(q % 2 + 1) * D]
                        else:
                            o = ps[:, 4 + q, 0:D]
                        if first and self.b2_row is not None:
                            pe.matmul(o, ones[0:33, :], b2s[:, self.b2_row + i0 + off, :], start=True, stop=False)
                        last = mm3(o, lambda h: self.hh[0:m, r, h, q * P:(q + 1) * P],
                                   lambda h: self.down(w[0:m, h], j),
                                   first and self.b2_row is None, final)
                    last.then_inc(self.s_hfree, 1)

                def end(i0, off):
                    pe.drain().then_inc(s_wfree, 1)

                self.schedule(pe.Fori, unit_up, unit_down, begin, end)

            def act_part(self):
                def begin(i0, off):
                    if self.bias1 is not None:
                        act.drain()
                        act.copy(b1e[:], b1c[:, bass.ds(self.bias1 + (i0 + off) * self.nh, self.nh)])
                        act.drain()

                def unit_up(i0, off, c, j):
                    n = self.unit(i0, off, c, j)
                    m, r, bk = self.cols[j], j % self.R, self.bank(j)
                    act.wait_ge(self.s_up, n + 1)
                    act.wait_ge(self.s_h, n + 1)
                    settled(act)
                    kw = {}
                    if self.bias1 is not None:
                        kw["bias"] = b1e[:, j:j + 1]
                    act.activation(self.hf[0:m, r, :], ps[0:m, bk, :], self.fn, scale=INV, **kw)\
                        .then_inc(self.s_act, 1)

                self.schedule(act.Fori, unit_up, nothing, begin, nothing)

            def dve_part(self):
                def unit_up(i0, off, c, j):
                    n = self.unit(i0, off, c, j)
                    m, r, bk = self.cols[j], j % self.R, self.bank(j)
                    hf = self.hf[0:m, r, :]
                    dve.wait_ge(self.s_act, n + 1 + self.R)
                    if self.gated:
                        dve.scalar_tensor_tensor(hf, ps[0:m, bk + 1, :], INV, hf, ALU.mult, ALU.mult)\
                            .then_inc(self.s_upfree, 1)
                        dve.wait_ge(self.s_upfree, n + 1 + self.R)
                    dve.wait_ge(self.s_hfree, n + 1)
                    dve.tensor_copy(self.hh[0:m, r, 0, :], hf).then_inc(self.s_hhi, 1)
                    dve.wait_ge(self.s_hhi, n + 1)
                    dve.tensor_tensor(self.hh[0:m, r, 1, :], hf, self.hh[0:m, r, 0, :], ALU.subtract)\
                        .then_inc(self.s_h, 1)

                def unit_down(i0, off, c, j):
                    if not (self.each or j == self.nh - 1):
                        return
                    n = self.unit(i0, off, c, j)
                    dve.drain()
                    dve.wait_ge(self.s_hfree, n + 1 + self.R)
                    for q in range(Q):
                        t = c * Q + q
                        if self.each:
                            y = ps[:, 4 + 2 * (j % 2) + q // 2, (q % 2) * D:(q % 2 + 1) * D]
                        else:
                            y = ps[:, 4 + q, 0:D]
                        i = dve.scalar_tensor_tensor(self.dst[:, t, :], y, self.weight(t, i0 + off, j),
                                                     self.dst[:, t, :], ALU.mult, ALU.add)
                    i.then_inc(self.s_yfree, 1)

                self.schedule(dve.Fori, unit_up, unit_down, nothing, nothing)

        class Dispatched:
            ROWS, NQ, NH, R, LAG = 384, 3, 8, 4, 2

            def __init__(self, name, job, act_fn, bias1, b2_row, route, at):
                self.name, self.job, self.fn, self.bias1, self.b2_row = name, job, act_fn, bias1, b2_row
                self.route = route
                ar = Area(at)
                self.rows = ar.f32(NT, D)
                self.hf = ar.f32(self.R, self.ROWS)
                self.hh = ar.f16(self.R, 2, self.ROWS)
                back = Area(at)
                self.yg = back.f32(2 * NT, D)
                ar.at = max(ar.at, back.at)
                self.xe = ar.f16(2, 2, KD, self.ROWS)
                self.xin = ar.f32(2, self.NQ, D)
                self.ysb = ar.f32(2, self.NQ, D)
                self.s_up = sem(name + "_up_full")
                self.s_act = credit(name + "_act_done", self.R)
                self.s_hhi = sem(name + "_hi_ready")
                self.s_h = credit(name + "_hidden_ready", self.R)
                self.s_hfree = credit(name + "_down_done", self.R)
                self.s_y = credit(name + "_y_copied", 1)
                self.s_in = [sem(name + f"_rows_loaded_{c}") for c in range(2)]
                self.s_tf = sem(name + "_rows_transposed")
                self.s_th = sem(name + "_xe_hi")
                self.s_tl = credit(name + "_xe_lo", 1)
                self.s_st = [credit(name + f"_rows_stored_{c}", 16) for c in range(2)]
                self.s_sc = sem(name + "_dispatched")
                self.s_ga = [sem(name + f"_gathered_{c}") for c in range(2)]

            def walk(self, fori, eng):
                def body(i0, last):
                    for k in range(4):
                        off, c = divmod(k, 2)
                        nxt = (i0,) + divmod(k + 1, 2) if k < 3 else (i0 + 2, 0, 0)
                        fin = last and k == 3
                        if not (last and k >= 2):
                            eng.load(*((i0, 1, k) if k < 2 else (i0 + 2, 0, k - 2)))
                        for j in range(self.NH):
                            nx = j + self.LAG
                            if nx < self.NH:
                                eng.up(i0, off, c, nx)
                            elif not fin:
                                if nx == self.NH and nxt[2] == 0:
                                    eng.begin(*nxt[0:2])
                                eng.up(*nxt, nx - self.NH)
                            eng.down(i0, off, c, j)
                            if j % 2 == 0 and j // 2 < self.NQ and not fin:
                                eng.turn(*nxt, j // 2)
                        if c == 1:
                            eng.end()
                eng.begin(0, 0)
                for c in range(2):
                    eng.load(0, 0, c)
                for q in range(self.NQ):
                    eng.turn(0, 0, 0, q)
                for j in range(self.LAG):
                    eng.up(0, 0, 0, j)
                with fori(0, 3) as i:
                    body(2 * i, False)
                body(6, True)

            def chunk(self, i0, off, c):
                return 2 * (i0 + off) + c

        class DispatchedPE:
            def __init__(self, F):
                self.F = F

            def begin(self, i0, off):
                pe.wait_ge(s_w, self.F.job + i0 + off + 1)

            def load(self, i0, off, c):
                pass

            def turn(self, i0, off, c, q):
                F = self.F
                n = F.chunk(i0, off, c)
                if q == 0:
                    pe.wait_ge(F.s_in[c], 16 * (i0 + off + 1))
                pe.wait_ge(F.s_tl, 3 * n + q + 1)
                for k in range(KD):
                    m = pe.transpose(ps[:, 7, k * P:(k + 1) * P], F.xin[:, c, q, k * P:(k + 1) * P], ident)
                m.then_inc(F.s_tf, 1)

            def up(self, i0, off, c, j):
                F = self.F
                n = F.chunk(i0, off, c)
                w = wsp[:, (F.job + off) % 2]
                if j == 0:
                    pe.wait_ge(F.s_tl, 3 * n + 3 + 1)
                pe.wait_ge(F.s_act, F.NH * n + j + 1)
                for k in range(KD):
                    m = mm3(ps[:, j % F.R, 0:F.ROWS],
                            lambda h: w[:, h, k * 1024 + j * P:k * 1024 + (j + 1) * P],
                            lambda h: F.xe[:, c, h, k, :], k == 0, k == KD - 1)
                m.then_inc(F.s_up, 1)

            def down(self, i0, off, c, j):
                F = self.F
                n = F.chunk(i0, off, c)
                w = wsp[:, (F.job + off) % 2]
                if j == 0:
                    pe.wait_ge(F.s_y, n + 1)
                pe.wait_ge(F.s_h, F.NH * n + j + 1 + F.R)
                for q in range(F.NQ):
                    o = ps[:, 4 + q, 0:D]
                    m = mm3(o, lambda h: F.hh[:, j % F.R, h, q * P:(q + 1) * P],
                            lambda h: w[:, h, 2048 + j * D:2048 + (j + 1) * D], j == 0, j == F.NH - 1)
                    if j == 0:
                        m = pe.matmul(o, ones[0:33, :], b2s[:, F.b2_row + i0 + off, :], start=False, stop=False)
                m.then_inc(F.s_hfree, 1)

            def end(self):
                pe.drain().then_inc(s_wfree, 1)

        class DispatchedACT:
            def __init__(self, F):
                self.F = F

            def begin(self, i0, off):
                act.drain()
                act.copy(b1e[:], b1c[:, bass.ds(self.F.bias1 + (i0 + off) * self.F.NH, self.F.NH)])
                act.drain()

            def load(self, i0, off, c):
                F = self.F
                n = F.chunk(i0, off, c)
                if isinstance(n, int) and n < 2:
                    act.wait_ge(F.s_sc, 16 * 2 * NT)
                else:
                    act.wait_ge(F.s_tf, 3 * n - 3)
                act.dma_start(F.xin[:, c], xs[bass.ds(n * F.ROWS, F.ROWS)].rearrange("(q p) d -> p q d", p=P))\
                    .then_inc(F.s_in[c], 16)

            def turn(self, i0, off, c, q):
                F = self.F
                act.wait_ge(F.s_tf, 3 * F.chunk(i0, off, c) + q + 1)
                act.activation(F.xe[:, c, 0, :, q * P:(q + 1) * P], shaped(ps[:, 7, 0:D], (KD, P)), ACT.Copy)\
                    .then_inc(F.s_th, 1)

            def up(self, i0, off, c, j):
                F = self.F
                n = F.NH * F.chunk(i0, off, c) + j
                act.wait_ge(F.s_up, n + 1)
                act.wait_ge(F.s_h, n + 1)
                act.activation(F.hf[:, j % F.R, :], ps[:, j % F.R, 0:F.ROWS], F.fn, scale=INV, bias=b1e[:, j:j + 1])\
                    .then_inc(F.s_act, 1)

            def down(self, i0, off, c, j):
                F = self.F
                n = F.chunk(i0, off, c)
                if j == F.NH - 1:
                    act.wait_ge(F.s_y, n + 2)
                    act.dma_start(ys[bass.ds(n * F.ROWS, F.ROWS)].rearrange("(q p) d -> p q d", p=P), F.ysb[:, c])\
                        .then_inc(F.s_st[c], 16)

            def end(self):
                pass

        class DispatchedDVE:
            def __init__(self, F):
                self.F = F

            def begin(self, i0, off):
                pass

            def load(self, i0, off, c):
                pass

            def turn(self, i0, off, c, q):
                F = self.F
                dve.wait_ge(F.s_th, 3 * F.chunk(i0, off, c) + q + 1)
                dve.tensor_tensor(F.xe[:, c, 1, :, q * P:(q + 1) * P], shaped(ps[:, 7, 0:D], (KD, P)),
                                  F.xe[:, c, 0, :, q * P:(q + 1) * P], ALU.subtract).then_inc(F.s_tl, 1)

            def up(self, i0, off, c, j):
                F = self.F
                n, r = F.NH * F.chunk(i0, off, c) + j, j % F.R
                dve.wait_ge(F.s_act, n + 1 + F.R)
                dve.wait_ge(F.s_hfree, n + 1)
                dve.tensor_copy(F.hh[:, r, 0, :], F.hf[:, r, :]).then_inc(F.s_hhi, 1)
                dve.wait_ge(F.s_hhi, n + 1)
                dve.tensor_tensor(F.hh[:, r, 1, :], F.hf[:, r, :], F.hh[:, r, 0, :], ALU.subtract).then_inc(F.s_h, 1)

            def down(self, i0, off, c, j):
                F = self.F
                n = F.chunk(i0, off, c)
                if j == F.NH - 1:
                    dve.wait_ge(F.s_hfree, F.NH * n + j + 1 + F.R)
                    dve.wait_ge(F.s_st[c], 16 * (i0 + off) + 16)
                    dve.tensor_copy(F.ysb[:, c], ps[:, 4:4 + F.NQ, 0:D]).then_inc(F.s_y, 1)

            def end(self):
                pass

            def combine(self):
                F = self.F
                for half in range(2):
                    dve.wait_ge(F.s_ga[half], 16 * NT)
                    for k in range(2):
                        for t in range(half * NT // 2, (half + 1) * NT // 2):
                            dve.scalar_tensor_tensor(x[:, t, :], F.yg[:, 2 * t + k, :], F.route.w2[:, t, k:k + 1], x[:, t, :],
                                                     ALU.mult, ALU.add)
                        dve.drain()

        class DispatchedPool:
            def __init__(self, F):
                self.F = F

            def scatter(self):
                F = self.F
                nc.gpsimd.wait_ge(F.route.s_ix, 1)
                nc.gpsimd.wait_ge(s_xz, 16)
                to = F.route.to.rearrange("p t k -> p (t k)")
                for n in range(2 * NT):
                    nc.gpsimd.indirect_dma_start(xs, bass.IndirectOffsetOnAxis(ap=to[:, n:n + 1], axis=0),
                                                 F.rows[:, n // 2, :], None).then_inc(F.s_sc, 16)

            def gather(self):
                F = self.F
                for c in range(2):
                    nc.gpsimd.wait_ge(F.s_st[c], 16 + 16 * 8)
                fro = F.route.fro.rearrange("p t k -> p (t k)")
                for n in range(2 * NT):
                    nc.gpsimd.indirect_dma_start(F.yg[:, n, :], None, ys,
                                                 bass.IndirectOffsetOnAxis(ap=fro[:, n:n + 1], axis=0))\
                        .then_inc(F.s_ga[n // NT], 16)

        class Attn:
            def __init__(self, name, jobq, jobk, inner, dh, layer, merged):
                self.name, self.jobq, self.jobk = name, jobq, jobk
                self.inner, self.dh, self.layer, self.merged = inner, dh, layer, merged
                self.NC = inner // P
                self.hpc = P // dh
                self.H = inner // dh
                self.scale = dh ** -0.5
                ar = Area()
                self.q = ar.f16(2, self.NC, S)
                self.o = ar.f16(2, self.NC, S)
                if merged:
                    self.k = ar.f16(2, self.NC, GA)
                    self.v = ar.f16(2, 5, inner)
                    self.pr = ar.f32(2, 2, GA)
                    self.pT = ar.f16(2, 2, 5, S)
                    self.G = self.H
                    self.tuses = 3
                    self.kc = [P] * 4 + [GA - 4 * P]
                else:
                    self.k = ar.f16(2, self.NC, 2 * G)
                    self.v = ar.f16(2, inner)
                    self.pr = ar.f32(2, 2, 4, G)
                    self.pT = ar.f16(2, 2, 4, S)
                    self.G = self.NC // 2
                    self.tuses = 2
                self.mx = ar.f32(2, 2, 4)
                self.sm = ar.f32(2, 2, 4)
                n = name
                self.s_pf = sem(n + "_proj_full")
                self.s_ph = sem(n + "_proj_hi")
                self.s_pfree = credit(n + "_proj_free", 2)
                self.s_sf = sem(n + "_scores_full")
                self.car, self.cex = (0, 2) if merged else (4, 0)
                self.s_ar = sem(n + "_exp_arg") if merged else credit(n + "_exp_arg", 4)
                self.s_ex = credit(n + "_exp_done", 2) if merged else sem(n + "_exp_done")
                self.s_p = sem(n + "_probs_ready")
                self.s_tf = sem(n + "_trans_full")
                self.s_th = sem(n + "_trans_hi")
                self.s_tfree = credit(n + "_trans_free", 2)
                self.s_of = sem(n + "_out_done")
                self.s_z = sem(n + "_zero_ready")
                self.plan()

            def events(self, T):
                G_, last = self.G, B * self.G
                b, g = divmod(T, G_)
                ev = []
                if 0 <= T - 1 < last:
                    ev.append(("norm",) + divmod(T - 1, G_))
                if T < last:
                    ev.append(("scores", b, g))
                if T >= 3 and T % G_ == 2 % G_:
                    ev += [("out", (T - 3) // G_, 0), ("out", (T - 3) // G_, 1)]
                if 0 <= T - 2 < last:
                    pb, pg = divmod(T - 2, G_)
                    ev.append(("pvhalf" if self.merged and pg % 2 == 0 else "pv", pb, pg))
                    if not self.merged and pg % 2 == 1 and pb + 1 < B:
                        ev.append(("v", pb + 1, pg // 2))
                if T < last and b + 1 < B:
                    if not self.merged:
                        ev.append(("q", b + 1, g))
                        if g % 2 == 1:
                            ev.append(("k", b + 1, g // 2))
                    elif g % 2 == 1:
                        ev.append(("q", b + 1, g // 2))
                if 0 <= T - 1 < last:
                    ev.append(("trans",) + divmod(T - 1, G_))
                return ev

            def plan(self):
                G_ = self.G
                if self.merged:
                    self.first = [("kv", 0, e) for e in range(2 * self.NC + 10)]
                else:
                    self.first = [("k", 0, e) for e in range(self.NC // 4)] + \
                                 [("v", 0, e) for e in range(self.inner // 512)]
                self.first += [("q", 0, e) for e in range(self.NC // 2)]
                self.tail = [e for T in range(B * G_, B * G_ + 3) for e in self.events(T)]
                bodies = [[e for T in range(b * G_, (b + 1) * G_) for e in self.events(T)] for b in range(B)]
                rel = [[(k, b - n, g) for k, b, g in body] for n, body in enumerate(bodies)]
                self.bodies = bodies
                self.h = next(h for h in range(B) if rel[h] == rel[B - 2])
                assert all(r == rel[self.h] for r in rel[self.h:B - 1])
                self.use, self.high = {}, {}
                for k, b, g in self.first + [e for x_ in bodies for e in x_] + self.tail:
                    if k in ("kv", "k", "v", "q", "out") or k == "pvhalf" or (k == "pv" and not self.merged):
                        key = (k, b, g) if k != "pvhalf" else ("pv", b, g + 1)
                        self.use[key] = len(self.use)
                        if k != "out":
                            self.high[key] = len(self.high)
                self.su = self.use["pv", 3, 1] - self.use["pv", 2, 1]
                self.sh = self.high["pv", 3, 1] - self.high["pv", 2, 1]
                assert self.su % 2 == 0

            def walk(self, fori, eng):
                for e in self.first:
                    eng.event(*e, 0)
                for body in self.bodies[:self.h]:
                    for e in body:
                        eng.event(*e, 0)
                with fori(0, B - 1 - self.h) as i:
                    for e in self.bodies[self.h]:
                        eng.event(*e, i)
                for e in self.bodies[B - 1] + self.tail:
                    eng.event(*e, 0)

            def u(self, key, i):
                return self.use[key] + self.su * i

            def bank67(self, key):
                return 6 + self.use[key] % 2

            def entry(self, k, b, e, i):
                if k == "q":
                    return self.q_entries(b + i)[e]
                kv = self.kv_entries(b + i)
                return kv[e] if k in ("kv", "k") else kv[self.NC // 4 + e]

            def wq(self, h, k, c):
                w = wsp[:, self.jobq % 2, h]
                return w[:, k * self.inner + c * P:k * self.inner + (c + 1) * P]

            def wo(self, h, c):
                at = KD * self.inner + c * D
                return wsp[:, self.jobq % 2, h, at:at + D]

            def koff(self):
                return 2048 if self.jobk == self.jobq else 0

            def wk(self, h, k, c):
                at = self.koff() + k * self.inner + c * P
                return wsp[0:CP, self.jobk % 2, h, at:at + P]

            def wv(self, h, k, c0, n):
                at = self.koff() + KC * self.inner + k * self.inner + c0
                return wsp[0:CP, self.jobk % 2, h, at:at + n]

            def kv_entries(self, i):
                r = []
                if self.merged:
                    for c in range(self.NC):
                        for half in range(2):
                            n0 = half * (GA // 2)

                            def fill(bk, c=c, n0=n0):
                                for k in range(KC):
                                    m = mm3(ps[:, bk, 0:GA // 2], lambda h: self.wk(h, k, c),
                                            lambda h: ctxs[:, h, k, n0:n0 + GA // 2], k == 0, k == KC - 1)
                                return m
                            r.append((fill, [(lambda bk: ps[:, bk, 0:GA // 2],
                                              lambda h, c=c, n0=n0: self.k[:, h, c, n0:n0 + GA // 2], INV)]))
                    for kc, rows in enumerate(self.kc):
                        for half in range(2):
                            def fill(bk, kc=kc, rows=rows, half=half):
                                for k in range(KC):
                                    m = mm3(ps[0:rows, bk, :], lambda h: ctxs[:, h, k, kc * P:kc * P + rows],
                                            lambda h: self.wv(h, k, half * 512, 512), k == 0, k == KC - 1)
                                return m
                            r.append((fill, [(lambda bk, rows=rows: ps[0:rows, bk, :],
                                              lambda h, kc=kc, rows=rows, half=half:
                                              self.v[0:rows, h, kc, half * 512:(half + 1) * 512], INV)]))
                    return r
                for c0 in range(0, self.NC, 4):
                    def fill(bk, c0=c0):
                        for c in range(4):
                            for k in range(KC):
                                m = mm3(ps[:, bk, c * G:(c + 1) * G], lambda h: self.wk(h, k, c0 + c),
                                        lambda h: ctxs[:, h, k, bass.ds(i * G, G)], k == 0, k == KC - 1)
                        return m
                    dr = []
                    for b in range(self.hpc):
                        r0 = b * self.dh
                        dr.append((lambda bk, r0=r0: ps[r0:r0 + self.dh, bk, 0:4 * G].rearrange("p (c g) -> p c g", c=4),
                                   lambda h, r0=r0, b=b, c0=c0: self.k[r0:r0 + self.dh, h, c0:c0 + 4, b * G:(b + 1) * G], INV))
                    r.append((fill, dr))
                for half in range(self.inner // 512):
                    def fill(bk, half=half):
                        for k in range(KC):
                            m = mm3(ps[0:G, bk, :], lambda h: ctxs[:, h, k, bass.ds(i * G, G)],
                                    lambda h: self.wv(h, k, half * 512, 512), k == 0, k == KC - 1)
                        return m
                    r.append((fill, [(lambda bk: ps[0:G, bk, :],
                                      lambda h, half=half: self.v[0:G, h, half * 512:(half + 1) * 512], INV)]))
                return r

            def q_entries(self, i):
                r = []
                for c0 in range(0, self.NC, 2):
                    def fill(bk, c0=c0):
                        for c in range(2):
                            for k in range(KD):
                                m = mm3(ps[:, bk, c * S:(c + 1) * S], lambda h: self.wq(h, k, c0 + c),
                                        lambda h: xT[:, h, k, bass.ds(i * S, S)], k == 0, k == KD - 1)
                        return m
                    r.append((fill, [(lambda bk: ps[:, bk, :],
                                      lambda h, c0=c0: self.q[:, h, c0:c0 + 2, :].rearrange("p c n -> p (c n)"), INV)]))
                return r

        class AttnPE:
            def __init__(self, A):
                self.A = A

            def event(self, k, b, g, i):
                A = self.A
                T = b * A.G + g + i * A.G
                if k in ("kv", "k", "v", "q"):
                    pe.wait_ge(A.s_pfree, A.u((k, b, g), i) + 1)
                    A.entry(k, b, g, i)[0](A.bank67((k, b, g))).then_inc(A.s_pf, 1)
                elif k == "scores":
                    need = A.use["q", b, g // 2 if A.merged else g]
                    if not A.merged:
                        need = max(need, A.use["k", b, g // 2])
                    pe.wait_ge(A.s_pfree, need + A.su * i + 3)
                    self.scores(T, g)
                elif k == "trans":
                    self.trans(T, g)
                elif k in ("pvhalf", "pv"):
                    key = ("pv", b, g + (k == "pvhalf"))
                    pe.wait_ge(A.s_tfree, (T + 1) * A.tuses + 2)
                    if k == "pvhalf" or not A.merged:
                        pe.wait_ge(A.s_pfree, A.u(key, i) + 1)
                    if not A.merged and g % 2 == 0:
                        pe.wait_ge(A.s_pfree, A.u(("v", b, g // 2), i) + 3)
                    self.pv(g, A.bank67(key), k)
                elif k == "out":
                    key = ("out", b, g)
                    pe.wait_ge(A.s_pfree, A.u(key, i) + 1)
                    if g == 0:
                        pe.wait_ge(A.s_pfree, A.u(("pv", b, A.G - 1), i) + 3)
                    for c in range(A.NC):
                        m = mm3(ps[:, A.bank67(key), 0:D], lambda h: A.o[:, h, c, g * P:(g + 1) * P],
                                lambda h: A.wo(h, c), c == 0, c == A.NC - 1)
                    m.then_inc(A.s_pf, 1)

            def scores(self, T, g):
                A = self.A
                for t in range(2):
                    pe.wait_ge(A.s_ex if A.merged else A.s_ar, 2 * T + t + 1)
                    if A.merged:
                        for half in range(2):
                            n0 = half * (GA // 2)
                            m = mm3(ps[:, 2 * t + half, 0:GA // 2],
                                    lambda h: A.q[:, h, g, t * P:(t + 1) * P],
                                    lambda h: A.k[:, h, g, n0:n0 + GA // 2], True, True)
                    else:
                        for c in range(2):
                            m = mm3(ps[:, 2 * (g % 2) + t, c * 2 * G:(c + 1) * 2 * G],
                                    lambda h: A.q[:, h, 2 * g + c, t * P:(t + 1) * P],
                                    lambda h: A.k[:, h, 2 * g + c, :], True, True)
                    m.then_inc(A.s_sf, 1)

            def trans(self, T, g):
                A = self.A
                pe.wait_ge(A.s_p, 2 * T + 2)
                for tu in range(A.tuses):
                    pe.wait_ge(A.s_tfree, T * A.tuses + tu + 1)
                    bk = 4 + A.tbank(g, tu)
                    if A.merged:
                        for kc in range(2 * tu, min(2 * tu + 2, 5)):
                            rows = A.kc[kc]
                            for t in range(2):
                                at = (kc % 2) * S + t * P
                                m = pe.transpose(ps[0:rows, bk, at:at + P], A.pr[:, g % 2, t, kc * P:kc * P + rows], ident)
                    else:
                        for hd in range(2 * tu, 2 * tu + 2):
                            for t in range(2):
                                at = (hd % 2) * S + t * P
                                m = pe.transpose(ps[0:G, bk, at:at + P], A.pr[:, g % 2, t, hd, :], ident)
                    m.then_inc(A.s_tf, 1)

            def pv(self, g, bk, k):
                A = self.A
                if A.merged:
                    at = 0 if k == "pvhalf" else S
                    for kc in range(5):
                        rows = A.kc[kc]
                        m = mm3(ps[:, bk, at:at + S], lambda h: A.v[0:rows, h, kc, g * P:(g + 1) * P],
                                lambda h: A.pT[0:rows, g % 2, h, kc, :], kc == 0, kc == 4)
                else:
                    for c in range(2):
                        for b in range(2):
                            hd = 2 * c + b
                            col = (4 * g + hd) * A.dh
                            m = mm3(ps[b * 64:(b + 1) * 64, bk, c * S:(c + 1) * S],
                                    lambda h: A.v[0:G, h, col:col + A.dh],
                                    lambda h: A.pT[0:G, g % 2, h, hd, :], True, True)
                if k == "pv":
                    m.then_inc(A.s_pf, 1)

        class AttnACT:
            def __init__(self, A):
                self.A = A

            def event(self, k, b, g, i):
                A = self.A
                T = b * A.G + g + i * A.G
                if k in ("kv", "k", "v", "q", "pv"):
                    key = (k, b, g)
                    act.wait_ge(A.s_pf, A.u(key, i) + 1)
                    for view, dst, scale in A.entry(k, b, g, i)[1] if k != "pv" else [A.odrain(g)]:
                        m = act.activation(dst(0), view(A.bank67(key)), ACT.Copy, scale=scale)
                    m.then_inc(A.s_ph, 1)
                elif k == "scores":
                    for t in range(2):
                        act.wait_ge(A.s_ar, 2 * T + t + 1 + A.car)
                        if A.merged:
                            act.activation(A.pr[:, g % 2, t, :].rearrange("p (a n) -> p a n", a=2),
                                           ps[:, 2 * t:2 * t + 2, 0:GA // 2], ACT.Exp,
                                           scale=1.5 * A.scale, bias=A.mx[:, g % 2, t, 1:2],
                                           accum_out=A.sm[:, g % 2, t, 0:1])
                            act.drain().then_inc(A.s_ex, 1)
                        else:
                            v = A.pr[:, g % 2, t, :, :]
                            act.activation(v, v, ACT.Exp, scale=A.scale).then_inc(A.s_ex, 1)
                elif k == "trans":
                    for tu in range(A.tuses):
                        act.wait_ge(A.s_tf, T * A.tuses + tu + 1)
                        bk = 4 + A.tbank(g, tu)
                        act.activation(A.tdst(g, tu, 0), A.tsrc(bk, tu), ACT.Copy).then_inc(A.s_th, 1)

        class AttnDVE:
            def __init__(self, A):
                self.A = A

            def event(self, k, b, g, i):
                A = self.A
                T = b * A.G + g + i * A.G
                if k in ("kv", "k", "v", "q", "pv"):
                    key = (k, b, g)
                    dve.wait_ge(A.s_ph, A.high[key] + A.sh * i + 1)
                    for view, dst, scale in A.entry(k, b, g, i)[1] if k != "pv" else [A.odrain(g)]:
                        m = dve.scalar_tensor_tensor(dst(1), view(A.bank67(key)), scale, dst(0), ALU.mult, ALU.subtract)
                    m.then_inc(A.s_pfree, 1)
                elif k == "norm":
                    self.norm(T, g % 2)
                elif k == "scores":
                    self.maxima(T, g, g % 2)
                elif k == "trans":
                    for tu in range(A.tuses):
                        dve.wait_ge(A.s_th, T * A.tuses + tu + 1)
                        bk = 4 + A.tbank(g, tu)
                        dve.tensor_tensor(A.tdst(g, tu, 1), A.tsrc(bk, tu), A.tdst(g, tu, 0), ALU.subtract)\
                            .then_inc(A.s_tfree, 1)
                elif k == "out":
                    dve.wait_ge(A.s_pf, A.u((k, b, g), i) + 1)
                    xo = x[:, 2 * (b + i) + g, :]
                    dve.scalar_tensor_tensor(xo, ps[:, A.bank67((k, b, g)), 0:D], sm[:, 4, 0:1], xo, ALU.mult, ALU.add)\
                        .then_inc(A.s_pfree, 1)

            def maxima(self, T, g, r):
                A = self.A
                for t in range(2):
                    dve.wait_ge(A.s_sf, 2 * T + t + 1)
                    if A.merged:
                        src = ps[:, 2 * t:2 * t + 2, 0:GA // 2]
                        dve.tensor_reduce(A.mx[:, r, t, 0:1], src, mybir.AxisListType.XY, ALU.max)
                    else:
                        src = ps[:, 2 * (g % 2) + t, 0:4 * G].rearrange("p (h k) -> p h k", h=4)
                        dve.tensor_reduce(A.mx[:, r, t, :], src, X, ALU.max)
                    dve.drain()
                    if A.merged:
                        dve.tensor_scalar(A.mx[:, r, t, 1:2], A.mx[:, r, t, 0:1], -1.5 * A.scale, None, ALU.mult)\
                            .then_inc(A.s_ar, 1)
                    else:
                        dve.tensor_tensor(A.pr[:, r, t, :, :], src,
                                          A.mx[:, r, t, :].unsqueeze(2).to_broadcast([P, 4, G]), ALU.subtract)\
                            .then_inc(A.s_ar, 1)

            def norm(self, T, r):
                A = self.A
                n = 2 * T + 2 + A.cex
                dve.wait_ge(A.s_ex, n)
                if A.merged:
                    dve.reciprocal(A.sm[:, r, :, 1:2], A.sm[:, r, :, 0:1])
                    dve.drain()
                    for t in range(2):
                        dve.tensor_scalar(A.pr[:, r, t, :], A.pr[:, r, t, :], A.sm[:, r, t, 1:2], None, ALU.mult)\
                            .then_inc(A.s_p, 1)
                else:
                    dve.tensor_reduce(A.sm[:, r, :, :], A.pr[:, r, :, :, :], X, ALU.add)
                    dve.drain()
                    dve.reciprocal(A.sm[:, r, :, :], A.sm[:, r, :, :])
                    dve.drain()
                    dve.tensor_tensor(A.pr[:, r].rearrange("p t h k -> p (t h) k"), A.pr[:, r].rearrange("p t h k -> p (t h) k"),
                                      A.sm[:, r].rearrange("p t h -> p (t h)").unsqueeze(2).to_broadcast([P, 8, G]),
                                      ALU.mult).then_inc(A.s_p, 2)

        def tbank(A):
            return lambda g, tu: (g * A.tuses + tu) % 2

        def tdst(A):
            def f(g, tu, h):
                if A.merged:
                    if tu == 2:
                        return A.pT[0:A.kc[4], g % 2, h, 4, :]
                    return A.pT[:, g % 2, h, 2 * tu:2 * tu + 2, :].rearrange("p c n -> p (c n)")
                return A.pT[0:G, g % 2, h, 2 * tu:2 * tu + 2, :].rearrange("p c n -> p (c n)")
            return f

        def tsrc(A):
            def f(bk, tu):
                if A.merged:
                    return ps[0:A.kc[4], bk, 0:S] if tu == 2 else ps[:, bk, :]
                return ps[0:G, bk, :]
            return f

        def odrain(A):
            def f(g):
                c0 = g - 1 if A.merged else 2 * g
                return (lambda bk: ps[:, bk, :],
                        lambda h: A.o[:, h, c0:c0 + 2, :].rearrange("p c n -> p (c n)"), 1.0)
            return f

        def attn_stage(A, stage):
            A.tbank, A.tdst, A.tsrc, A.odrain = tbank(A), tdst(A), tsrc(A), odrain(A)

            def pe_part():
                for j in sorted({A.jobq, A.jobk}):
                    pe.wait_ge(s_w, j + 1)
                if not A.merged:
                    pe.wait_ge(A.s_z, 1)
                A.walk(pe.Fori, AttnPE(A))
                pe.drain().then_inc(s_wfree, len({A.jobq, A.jobk}))
                barrier(pe, 0, stage)

            def act_part():
                if not A.merged:
                    act.wait_ge(A.s_z, 1)
                A.walk(act.Fori, AttnACT(A))
                barrier(act, 1, stage)

            def dve_part():
                if not A.merged:
                    dve.memset(A.k[:, :, :, :].rearrange("p h c n -> p (h c n)"), 0.0)
                dve.tensor_scalar(sm[:, 4, 0:1], tg[:, A.layer:A.layer + 1], INV, None, ALU.mult)
                dve.tensor_scalar(brow[:, A.layer - 1, :], brow[:, A.layer - 1, :], tg[:, A.layer:A.layer + 1], None, ALU.mult)
                dve.drain().then_inc(A.s_z, 1)
                with dve.Fori(0, NT) as t:
                    dve.tensor_tensor(x[:, t, :], x[:, t, :], brow[:, A.layer - 1, :], ALU.add)
                dve.drain()
                A.walk(dve.Fori, AttnDVE(A))
                barrier(dve, 2, stage)
            prog["pe"].append(pe_part)
            prog["act"].append(act_part)
            prog["dve"].append(dve_part)

        def small(n):
            return xT[:].rearrange("p a b c -> p (a b c)")[:, 2 * D * n:2 * D * (n + 1)].bitcast(F32)

        ARE, AIM, CRE, CIM, LDT = (small(n) for n in range(5))
        DT, IMC, T1, T2, T3, DCR, DCI, RE, T4, T5, T6 = (small(n) for n in range(5, 16))

        class KGen:
            def __init__(self):
                ar = Area()
                self.y = ar.f32(D, 16)
                self.e1 = ar.f32(D, 16)
                self.e2 = ar.f32(D, 16)
                self.v = ar.f32(D, 16)
                self.w = ar.f32(D, 16)
                self.kk = self.v[:, 0:32, :]
                self.kp = shaped(self.w.rearrange("p a b -> p (a b)")[:, 0:512].bitcast(F16), (32, 16, 2))
                self.zero = self.w.rearrange("p a b -> p (a b)")[:, 1024:1280].bitcast(F16)
                self.s_d = sem("kgen_dve")
                self.s_a = sem("kgen_act")
                self.s_t = sem("kgen_tables_ready")
                self.s_k = sem("kgen_sums_ready")
                self.s_st = sem("kgen_rows_ready")
                self.s_kd = sem("kernel_in_dram")

            ACTS = [("T1", "T1", "tanh", 1.0 / 16), ("T1", "T1", "tanh", 0.5), ("T2", "T2", "sin", 0),
                    ("T3", "T3", "sin", 0)]

            def act_part(self):
                n = [0]

                def step(dst, src, fn, **kw):
                    n[0] += 1
                    act.wait_ge(self.s_d, n[0])
                    act.activation(dst, src, fn, **kw)
                    act.drain().then_inc(self.s_a, 1)

                act.wait_ge(s_const, N_CONST)
                act.activation(tg[:], sc[:, 0:8], ACT.Tanh)
                step(T1, LDT, ACT.Tanh, scale=1.0 / 16)
                step(T1, RE, ACT.Tanh, scale=0.5)
                step(T2, T2, ACT.Sin, scale=SIN_SCALE)
                step(T3, T3, ACT.Sin, scale=SIN_SCALE)
                step(self.v, self.v, ACT.Sin, scale=SIN_SCALE, bias=cst[:, C_PHR:C_PHR + 1])
                step(self.w, self.w, ACT.Exp)
                step(self.v, self.v, ACT.Sin, scale=SIN_SCALE, bias=cst[:, C_PHR + 1:C_PHR + 2])
                step(self.w, self.w, ACT.Sin, scale=SIN_SCALE, bias=cst[:, C_PHR + 2:C_PHR + 3])
                step(self.w, self.w, ACT.Exp)

            def dve_part(self):
                n = [0]

                def tt(o, a_, b_, op):
                    dve.tensor_tensor(o, a_, b_, op)
                    dve.drain()

                def ts(o, a_, s1, s2, op0, op1):
                    dve.tensor_scalar(o, a_, s1, s2, op0, op1) if s2 is not None else dve.tensor_scalar(o, a_, s1, None, op0)
                    dve.drain()

                def ask(count=1):
                    dve.drain().then_inc(self.s_d, count)
                    n[0] += count
                    dve.wait_ge(self.s_a, n[0])

                def wrap(dst, y, ph):
                    ts(dst, y, ph, ROUND, ALU.add, ALU.add)
                    dve.scalar_tensor_tensor(dst, dst, ROUND, y, ALU.subtract, ALU.subtract)
                    dve.drain()

                dve.wait_ge(s_const, N_CONST)
                ask()
                ts(T2, T1, -1.0, 1.0, ALU.mult, ALU.add)
                ts(T3, T1, 1.0, None, ALU.add, None)
                dve.reciprocal(T2, T2)
                dve.drain()
                tt(T2, T2, T3, ALU.mult)
                for _ in range(3):
                    tt(T2, T2, T2, ALU.mult)
                tt(RE, T2, ARE, ALU.mult)
                tt(IMC, T2, AIM, ALU.mult)
                ts(IMC, IMC, 1.0 / TWO_PI, None, ALU.mult, None)
                ask()
                ts(T2, IMC, 0.5, None, ALU.mult, None)
                wrap(T4, T2, 0.0)
                wrap(T3, IMC, 0.0)
                dve.tensor_copy(T2, T4)
                ask(2)
                ts(T4, T1, -1.0, 1.0, ALU.mult, ALU.add)
                dve.reciprocal(T4, T4)
                dve.drain()
                tt(T1, T1, T4, ALU.mult)
                ts(T1, T1, 2.0, None, ALU.mult, None)
                tt(T2, T2, T2, ALU.mult)
                ts(T2, T2, 2.0, None, ALU.mult, None)
                ts(T4, T2, -1.0, 1.0, ALU.mult, ALU.add)
                tt(T4, T4, T1, ALU.mult)
                tt(T4, T4, T2, ALU.subtract)
                dve.scalar_tensor_tensor(T5, T1, 1.0, T3, ALU.add, ALU.mult)
                dve.drain()
                tt(T1, ARE, ARE, ALU.mult)
                tt(T2, AIM, AIM, ALU.mult)
                tt(T1, T1, T2, ALU.add)
                dve.reciprocal(T1, T1)
                dve.drain()
                ts(T1, T1, 2.0, None, ALU.mult, None)
                tt(T2, T4, ARE, ALU.mult)
                tt(T3, T5, AIM, ALU.mult)
                tt(T2, T2, T3, ALU.add)
                tt(T2, T2, T1, ALU.mult)
                tt(T3, T5, ARE, ALU.mult)
                tt(T6, T4, AIM, ALU.mult)
                tt(T3, T3, T6, ALU.subtract)
                tt(T3, T3, T1, ALU.mult)
                tt(DCR, CRE, T2, ALU.mult)
                tt(T6, CIM, T3, ALU.mult)
                tt(DCR, DCR, T6, ALU.subtract)
                tt(DCI, CRE, T3, ALU.mult)
                tt(T6, CIM, T2, ALU.mult)
                tt(DCI, DCI, T6, ALU.add)

                def over_k(o, v, at):
                    tt(o, v.unsqueeze(2).to_broadcast([P, D, 16]), bcast(cst[:, at:at + 16], D), ALU.mult)

                over_k(self.y, IMC, C_IOTA)
                wrap(self.v, self.y, cst[:, C_PH:C_PH + 1])
                over_k(self.w, RE, C_IOTA)
                ask(2)
                tt(self.e1, self.v, self.w, ALU.mult)
                over_k(self.y, IMC, C_K16)
                wrap(self.v, self.y, cst[:, C_PH + 1:C_PH + 2])
                wrap(self.w, self.y, cst[:, C_PH + 2:C_PH + 3])
                ask(2)
                tt(self.v, self.v, DCR.unsqueeze(2).to_broadcast([P, D, 16]), ALU.mult)
                tt(self.w, self.w, DCI.unsqueeze(2).to_broadcast([P, D, 16]), ALU.mult)
                tt(self.v, self.v, self.w, ALU.add)
                over_k(self.w, RE, C_K16)
                ask()
                dve.tensor_tensor(self.e2, self.v, self.w, ALU.mult)
                dve.drain().then_inc(self.s_t, 1)
                for bk in range(8):
                    dve.wait_ge(self.s_k, bk + 1)
                    m = self.y.rearrange("p a b -> p (a b)")[:, 512 * (bk % 4):512 * (bk % 4 + 1)]
                    m4 = shaped(m, (4, 8, 16))
                    mask = cst[:, C_MASK:C_MASK + 8].unsqueeze(1).unsqueeze(3).to_broadcast([P, 4, 8, 16])
                    dve.tensor_tensor(m4, shaped(ps[:, bk, :], (4, 8, 16)), mask, ALU.mult)
                    dve.drain()
                    dve.tensor_reduce(self.kk[:, 4 * bk:4 * bk + 4, :], m4.rearrange("p g d b -> p g b d"), X, ALU.add)
                dve.memset(self.zero, 0.0)
                dve.drain()
                dve.tensor_tensor(self.kk[:, :, 0], self.kk[:, :, 0], dsk[:], ALU.add)
                dve.drain()
                dve.tensor_copy(self.kp[:, :, :, 0], self.kk)
                dve.drain()
                dve.tensor_tensor(self.kp[:, :, :, 1], self.kk, self.kp[:, :, :, 0], ALU.subtract)
                dve.drain().then_inc(self.s_st, 1)

            def pe_part(self):
                pe.wait_ge(self.s_t, 1)
                for g in range(D // 8):
                    l = self.e2[:, 8 * g:8 * g + 8, :].rearrange("p d a -> p (d a)")
                    r = self.e1[:, 8 * g:8 * g + 8, :].rearrange("p d a -> p (d a)")
                    m = pe.matmul(ps[:, g // 4, (g % 4) * P:(g % 4 + 1) * P], l, r, start=True, stop=True)
                    if g % 4 == 3:
                        m.then_inc(self.s_k, 1)

            def store(self, sp):
                sp.wait_ge(self.s_st, 1)
                for half in range(2):
                    sp.dma_start(kdram[half * P:(half + 1) * P, 0:127, :].rearrange("d j c -> d (j c)"),
                                 self.zero[:, 0:254]).then_inc(self.s_kd, 16)
                for e in range(8):
                    sp.dma_start(kdram[:, 127:127 + S, :].rearrange("(g e) (a b) c -> e a g (b c)", e=8, b=16)[e],
                                 self.kp[16 * e:16 * e + 16].rearrange("p g b c -> p g (b c)")).then_inc(self.s_kd, 16)
                sp.dma_start(xs[0:SLOTS].rearrange("(p n) d -> p n d", p=P),
                             self.zero.bitcast(F32).unsqueeze(1).to_broadcast([P, SLOTS // P, D])).then_inc(s_xz, 16)
                sp.wait_ge(self.s_kd, 160)

        L0 = Area()
        xtext = L0.f32(NT, D)
        u = L0.f16(2, NT, D)
        ystart = L0.at
        y = L0.f32(NT, D)
        rows = L0.f32(NROW)
        TG = 8
        tz = L0.f16(2, TG, S, 2)
        H0, DH0, KTOP = 4, 32, 32

        def row(n, w=D):
            return rows[:, n * D:n * D + w]

        class Attn0:
            def __init__(self):
                ar = Area(ystart)
                self.q = ar.f16(2, S)
                self.k = ar.f16(2, H0 * G)
                self.v = ar.f16(2, D)
                self.s = ar.f32(2, H0, G)
                self.w = ar.f32(2, H0, G)
                self.m1 = ar.f32(2, H0, 8)
                self.m2 = ar.f32(2, H0, 8)
                self.den = ar.f32(2, H0)
                self.am = ar.f32(2, G)
                self.amT = ar.f16(2, S)
                self.f = xn[:, 0:2, :].rearrange("p a b -> p (a b)")
                self.xl = xn[:, 2, :]
                self.uh = ar.f16(2, 2, D)
                self.mb = ar.f32(B, G)
                assert ar.at <= ystart + NT * D
                self.s_z = sem("a0_zero_ready")
                self.s_f = sem("a0_pe_done")
                self.s_hi = sem("a0_hi_done")
                self.s_lo = sem("a0_dve_done")
                self.s_arg = sem("a0_exp_arg")
                self.s_ex = sem("a0_exp_done")
                self.s_ff = sem("a0_film_full")
                self.s_fr = credit("a0_film_free", 2)
                self.s_u = sem("a0_u_ready")
                self.s_r = sem("a0_u_reversed")
                self.s_uc = credit("a0_u_copied", 2)

            def w0(self, at, n, rows_=P):
                return lambda h: wsp[0:rows_, J_X0 % 2, h, at:at + n]

            def pe_part(self):
                pe.wait_ge(s_w, J_X0 + 1)
                pe.wait_ge(self.s_z, 1)
                with pe.Fori(0, B) as i:
                    def cx(k):
                        return lambda h: ctxs[:, h, k, bass.ds(i * G, G)]
                    pe.wait_ge(self.s_fr, 2 * i + 2)
                    pe.wait_ge(self.s_uc, 2 * i + 2)
                    for k in range(KC):
                        mm3(ps[:, 0, 0:G], self.w0(2304 + k * P, P, CP), cx(k), k == 0, k == KC - 1)
                    for k in range(KC):
                        mm3(ps[0:G, 1, 0:D], cx(k), self.w0(2304 + 256 + k * D, D, CP), k == 0, k == KC - 1)
                    for k in range(KD):
                        m = mm3(ps[:, 2, 0:S], self.w0(k * P, P), lambda h: xT[:, h, k, bass.ds(i * S, S)],
                                k == 0, k == KD - 1)
                    m.then_inc(self.s_f, 1)
                    pe.wait_ge(self.s_lo, 4 * i + 1)
                    for t in range(2):
                        m = mm3(ps[:, 3 + t, 0:H0 * G], lambda h: self.q[:, h, t * P:(t + 1) * P],
                                lambda h: self.k[:, h, :], True, True)
                    m.then_inc(self.s_f, 1)
                    pe.wait_ge(self.s_lo, 4 * i + 2)
                    for t in range(2):
                        m = pe.transpose(ps[0:G, 5, t * P:(t + 1) * P], self.am[:, t, :], ident)
                    m.then_inc(self.s_f, 1)
                    pe.wait_ge(self.s_lo, 4 * i + 3)
                    for c in range(KD):
                        m = mm3(ps[:, 6, c * S:(c + 1) * S], lambda h: self.v[0:G, h, c * P:(c + 1) * P],
                                lambda h: self.amT[0:G, h, :], True, True)
                    m.then_inc(self.s_f, 1)
                    pe.wait_ge(self.s_lo, 4 * i + 4)
                    for t in range(2):
                        pe.wait_ge(self.s_fr, 2 * i + t + 1)
                        bk = 7 if t == 0 else 0
                        for k in range(KD):
                            m = mm3(ps[:, bk, :], lambda h: xT[:, h, k, bass.ds(i * S + t * P, P)],
                                    self.w0(256 + k * 2 * D, 2 * D), k == 0, k == KD - 1)
                        m.then_inc(self.s_ff, 1)
                    for t in range(2):
                        pe.wait_ge(self.s_u, 2 * i + t + 1)
                        pe.matmul(ps[:, 1 + t, :], rev[:], self.uh[:, t].rearrange("p h d -> p (h d)"),
                                  start=True, stop=True).then_inc(self.s_r, 1)

            def kblocks(self, h):
                return [(self.k[DH0 * b:DH0 * (b + 1), h, b * G:(b + 1) * G], ps[DH0 * b:DH0 * (b + 1), 0, 0:G])
                        for b in range(H0)]

            def act_part(self):
                act.wait_ge(self.s_z, 1)
                with act.Fori(0, B) as i:
                    act.wait_ge(self.s_f, 4 * i + 1)
                    for o, v in self.kblocks(0):
                        act.activation(o, v, ACT.Copy, scale=INV)
                    act.activation(self.v[0:G, 0, :], ps[0:G, 1, 0:D], ACT.Copy, scale=INV)
                    act.activation(self.q[:, 0, :], ps[:, 2, 0:S], ACT.Copy, scale=INV).then_inc(self.s_hi, 1)
                    act.wait_ge(self.s_arg, i + 1)
                    act.activation(self.s[:], self.s[:], ACT.Exp, scale=DH0 ** -0.5)
                    act.activation(self.w[:], self.w[:], ACT.Exp, scale=DH0 ** -0.5).then_inc(self.s_ex, 1)
                    act.wait_ge(self.s_f, 4 * i + 3)
                    act.activation(self.amT[0:G, 0, :], ps[0:G, 5, 0:S], ACT.Copy).then_inc(self.s_hi, 1)
                    act.wait_ge(self.s_f, 4 * i + 4)
                    settled(act)
                    act.activation(xT[:, 0, :, bass.ds(i * S, S)], shaped(ps[:, 6, :], (KD, S)), ACT.Copy)\
                        .then_inc(self.s_hi, 1)
                    for t in range(2):
                        act.wait_ge(self.s_r, 2 * i + t + 1)
                        settled(act)
                        act.activation(u[:, :, 2 * i + t, :], shaped(ps[:, 1 + t, :], (2, D)), ACT.Copy)\
                            .then_inc(self.s_uc, 1)

            def dve_part(self):
                dve.wait_ge(s_rows, N_ROWS)
                dve.tensor_copy(self.mb[:].rearrange("p a b -> p (a b)"), mk8[:])
                dve.tensor_copy(tmk[:], tm8[:])
                dve.memset(self.k[:].rearrange("p a b -> p (a b)"), 0.0)
                dve.drain()
                dve.tensor_scalar(self.mb[:], self.mb[:], -NEG, NEG, ALU.mult, ALU.add)
                dve.tensor_scalar(tmk[:], tmk[:], 1.0 / H0, None, ALU.mult)
                dve.tensor_scalar(row(R_FI, 4 * D), row(R_FI, 4 * D), sc[:, 8:9], None, ALU.mult)
                dve.drain()
                dve.tensor_scalar(row(R_FI), row(R_FI), 1.0, None, ALU.add)
                dve.tensor_scalar(row(R_FO), row(R_FO), 1.0, None, ALU.add)
                dve.tensor_scalar(sm[:, 4, 1:2], sc[:, 8:9], INV, None, ALU.mult)
                dve.drain().then_inc(self.s_z, 1)
                with dve.Fori(0, B) as i:
                    dve.wait_ge(self.s_hi, 3 * i + 1)
                    for (o, v), (oh, _) in zip(self.kblocks(1), self.kblocks(0)):
                        dve.scalar_tensor_tensor(o, v, INV, oh, ALU.mult, ALU.subtract)
                    dve.scalar_tensor_tensor(self.v[0:G, 1, :], ps[0:G, 1, 0:D], INV, self.v[0:G, 0, :], ALU.mult, ALU.subtract)
                    dve.scalar_tensor_tensor(self.q[:, 1, :], ps[:, 2, 0:S], INV, self.q[:, 0, :], ALU.mult, ALU.subtract)\
                        .then_inc(self.s_lo, 1)
                    dve.drain()
                    dve.wait_ge(self.s_f, 4 * i + 2)
                    for t in range(2):
                        dve.tensor_tensor(self.s[:, t], shaped(ps[:, 3 + t, 0:H0 * G], (H0, G)),
                                          self.mb[:, bass.ds(i, 1), :].to_broadcast([P, H0, G]), ALU.add)
                    dve.drain()
                    for r in range(KTOP // 8):
                        src = self.s if r == 0 else self.w
                        mx = self.m1 if r == 0 else self.m2
                        for t in range(2):
                            for h in range(H0):
                                dve.max(mx[:, t, h, :], src[:, t, h, :])
                        dve.drain()
                        for t in range(2):
                            for h in range(H0):
                                dve.match_replace(self.w[:, t, h, :], mx[:, t, h, :], src[:, t, h, :], NEG)
                        dve.drain()
                    mx = self.m1[:, :, :, 0:1].to_broadcast([P, 2, H0, G])
                    dve.tensor_tensor(self.s[:], self.s[:], mx, ALU.subtract)
                    dve.tensor_tensor(self.w[:], self.w[:], mx, ALU.subtract)
                    dve.drain().then_inc(self.s_arg, 1)
                    dve.wait_ge(self.s_ex, i + 1)
                    dve.tensor_tensor(self.s[:], self.s[:], self.w[:], ALU.subtract)
                    dve.drain()
                    dve.tensor_reduce(self.den[:], self.s[:], X, ALU.add)
                    dve.drain()
                    dve.reciprocal(self.den[:], self.den[:])
                    dve.drain()
                    for t in range(2):
                        dve.tensor_scalar(self.den[:, t, :], self.den[:, t, :], tmk[:, bass.ds(2 * i + t, 1)], None, ALU.mult)
                    dve.drain()
                    dve.tensor_tensor(self.s[:], self.s[:], self.den[:].unsqueeze(3).to_broadcast([P, 2, H0, G]), ALU.mult)
                    dve.drain()
                    dve.tensor_reduce(self.am[:], self.s[:].rearrange("p t h g -> p t g h"), X, ALU.add)
                    dve.drain().then_inc(self.s_lo, 1)
                    dve.wait_ge(self.s_hi, 3 * i + 2)
                    dve.tensor_tensor(self.amT[0:G, 1, :], ps[0:G, 5, 0:S], self.amT[0:G, 0, :], ALU.subtract)\
                        .then_inc(self.s_lo, 1)
                    dve.wait_ge(self.s_hi, 3 * i + 3)
                    dve.tensor_tensor(xT[:, 1, :, bass.ds(i * S, S)], shaped(ps[:, 6, :], (KD, S)),
                                      xT[:, 0, :, bass.ds(i * S, S)], ALU.subtract).then_inc(self.s_lo, 1)
                    for t in range(2):
                        tt_ = 2 * i + t
                        dve.drain()
                        dve.wait_ge(self.s_ff, tt_ + 1)
                        dve.tensor_scalar(self.xl, xtext[:, tt_, :], mean[:, bass.ds(tt_, 1)], rstd[:, bass.ds(tt_, 1)],
                                          ALU.subtract, ALU.mult)
                        dve.scalar_tensor_tensor(self.f, ps[:, 7 if t == 0 else 0, :], sm[:, 4, 1:2], row(R_FI, 2 * D),
                                                 ALU.mult, ALU.add).then_inc(self.s_fr, 1)
                        dve.drain()
                        dve.tensor_tensor(self.xl, self.xl, row(R_GIN), ALU.mult)
                        dve.drain()
                        dve.tensor_tensor(self.xl, self.xl, row(R_BIN), ALU.add)
                        dve.drain()
                        dve.tensor_tensor(self.xl, self.xl, self.f[:, 0:D], ALU.mult)
                        dve.drain()
                        dve.tensor_tensor(self.xl, self.xl, self.f[:, D:2 * D], ALU.add)
                        dve.drain()
                        dve.tensor_copy(self.uh[:, t, 0, :], self.xl)
                        dve.drain()
                        dve.tensor_tensor(self.uh[:, t, 1, :], self.xl, self.uh[:, t, 0, :], ALU.subtract)\
                            .then_inc(self.s_u, 1)

        class Conv:
            def __init__(self):
                self.s_t = [sem("toeplitz_loaded_0"), sem("toeplitz_loaded_1")]
                self.s_tfree = credit("toeplitz_used", 2)
                self.s_y = sem("conv_full")
                self.s_yfree = credit("conv_bank_free", 2)
                self.s_ff = sem("film_out_full")
                self.s_ffree = credit("film_out_free", 2)
                self.f = xn[:].rearrange("p a b -> p (a b)")[:, 0:2 * D]

            def sp_part(self, sp):
                with sp.Fori(0, D // TG // 2) as i:
                    for par in range(2):
                        g = 2 * i + par
                        sp.wait_ge(self.s_tfree, g + 1)
                        src = bass.AP(tensor=kdram.tensor, offset=g * (TG * KROW * 2),
                                      ap=[[2, P], [KROW * 2, TG], [1, 2 * S]])
                        sp.dma_start(tz[:, par].rearrange("p d l c -> p d (l c)"), src).then_inc(self.s_t[par], 16)

            def pe_part(self):
                with pe.Fori(0, D // TG // 2) as i:
                    for par in range(2):
                        g = 2 * i + par
                        pe.wait_ge(self.s_t[par], 16 * (i + 1))
                        pe.wait_ge(self.s_yfree, g + 1)
                        for k in range(TG):
                            d = g * TG + k
                            o = ps[:, par, k * NT:(k + 1) * NT]

                            def uu(h, a0=0, st=1):
                                return u[:, h, a0::st, bass.ds(d, 1)].rearrange("p t o -> p (t o)")

                            mm3(o, lambda h: tz[:, par, k, 0:P, h], lambda h: uu(h), True, True)
                            for a_, b_ in ((0, 0), (0, 1), (1, 0)):
                                m = pe.matmul(o[:, 1::2], tz[:, par, k, P:2 * P, a_], uu(b_, 0, 2), start=False,
                                              stop=True, skip_group_check=True)
                        m.then_inc(self.s_y, 1)
                        pe.drain().then_inc(self.s_tfree, 1)
                with pe.Fori(0, NT // 2) as i:
                    for par in range(2):
                        t = 2 * i + par
                        pe.wait_ge(self.s_ffree, t + 1)
                        for k in range(KD):
                            m = mm3(ps[:, 2 + par, :], lambda h: xT[:, h, k, bass.ds(t * P, P)],
                                    lambda h: wsp[:, J_X0 % 2, h, 1280 + k * 2 * D:1280 + (k + 1) * 2 * D], k == 0, k == KD - 1)
                        m.then_inc(self.s_ff, 1)
                pe.drain().then_inc(s_wfree, 1)

            def dve_part(self):
                with dve.Fori(0, D // TG // 2) as i:
                    for par in range(2):
                        g = 2 * i + par
                        dve.wait_ge(self.s_y, g + 1)
                        dve.tensor_copy(y[:, :, bass.ds(g * TG, TG)].rearrange("p t d -> p d t"),
                                        shaped(ps[:, par, 0:TG * NT], (TG, NT))).then_inc(self.s_yfree, 1)
                dve.drain()
                f = self.f
                with dve.Fori(0, NT // 2) as i:
                    for par in range(2):
                        t = 2 * i + par
                        dve.wait_ge(self.s_ff, t + 1)
                        dve.scalar_tensor_tensor(f, ps[:, 2 + par, :], sm[:, 4, 1:2], row(R_FO, 2 * D), ALU.mult, ALU.add)\
                            .then_inc(self.s_ffree, 1)
                        dve.drain()
                        dve.tensor_tensor(y[:, t, :], y[:, t, :], f[:, 0:D], ALU.mult)
                        dve.drain()
                        dve.tensor_tensor(y[:, t, :], y[:, t, :], f[:, D:2 * D], ALU.add)
                        dve.drain()
                        dve.tensor_tensor(y[:, t, :], y[:, t, :], xtext[:, t, :], ALU.add)
                        dve.drain()

        s_rows = sem("rows_loaded")
        N_CONST, N_ROWS = 16 * 9, 16
        stage = [0]

        def finish_stage():
            n = stage[0]
            prog["dve"].append(lambda: barrier(dve, 2, n))
            prog["act"].append(lambda: barrier(act, 1, n))
            prog["pe"].append(lambda: barrier(pe, 0, n))
            stage[0] += 1

        def norm(n):
            norm_stage(n, stage[0])
            stage[0] += 1

        kg = KGen()
        prog["dve"].append(kg.dve_part)
        prog["act"].append(kg.act_part)
        prog["pe"].append(kg.pe_part)
        prog["dve"].append(lambda: dve.wait_ge(kg.s_kd, 160))
        finish_stage()
        prog["dve"].append(lambda: dve.wait_ge(s_x, 16))
        prog["pe"].append(lambda: pe.wait_ge(s_cdone, 1))
        prog["act"].append(lambda: act.wait_ge(s_cdone, 1))
        norm(Norm("n0", x, keep=xtext))
        inner_stats = Norm("n0in", xtext)
        prog["dve"].append(inner_stats.dve_stats)
        prog["act"].append(inner_stats.act_stats)
        a0 = Attn0()
        prog["dve"].append(a0.dve_part)
        prog["act"].append(a0.act_part)
        prog["pe"].append(a0.pe_part)
        finish_stage()
        cv = Conv()
        prog["dve"].append(cv.dve_part)
        prog["pe"].append(cv.pe_part)
        finish_stage()
        norm(Norm("n0f", y, affine=(row(R_GF), row(R_BF))))
        no_weight = lambda t, e, j: INV
        mlp_up = lambda w, g, k, j: w[:, k * 1024 + j * P:k * 1024 + (j + 1) * P]
        mlp_down = lambda w, j: w[:, 2048 + j * D:2048 + (j + 1) * D]
        f0 = Ffn("mlp0", J_F0, 0, [P] * 8, ACT.Gelu, mlp_up, mlp_down, False, 0, 0, no_weight, y, single=True)
        prog["dve"].append(f0.dve_part)
        prog["act"].append(f0.act_part)
        prog["pe"].append(f0.pe_part)
        last0 = Norm("n0out", y)

        def out0():
            dve.drain()
            last0.dve_stats()
            with dve.Fori(0, NT) as t:
                last0.normalise(xn[:, 0], t)
                dve.drain()
                dve.tensor_tensor(xn[:, 0], xn[:, 0], row(R_GOUT), ALU.mult)
                dve.drain()
                dve.tensor_tensor(xn[:, 0], xn[:, 0], row(R_BOUT), ALU.add)
                dve.drain()
                dve.scalar_tensor_tensor(x[:, t, :], xn[:, 0], tg[:, 0:1], x[:, t, :], ALU.mult, ALU.add)
                dve.drain()
        prog["dve"].append(out0)
        prog["act"].append(last0.act_stats)
        finish_stage()

        def route(layer):
            r = Route(f"route{layer}", layer)
            prog["dve"].append(r.dve_part)
            prog["act"].append(r.act_part)
            prog["pe"].append(r.pe_part)
            finish_stage()
            return r

        def ffn(f):
            prog["dve"].append(f.dve_part)
            prog["act"].append(f.act_part)
            prog["pe"].append(f.pe_part)

        by_expert = lambda t, e, j: wgt[:, bass.ds(t, 1), bass.ds(e, 1)].rearrange("p a b -> p (a b)")
        s_xz = sem("slots_cleared")
        n0e = Norm("n0e", x, keep=Area(ROUTE_END).f32(NT, D))
        norm(n0e)
        e0 = Dispatched("moe0", J_E0, ACT.Relu, 8, 1, route(0), ROUTE_END)
        prog["pe"].append(lambda: e0.walk(pe.Fori, DispatchedPE(e0)))
        prog["act"].append(lambda: e0.walk(act.Fori, DispatchedACT(e0)))
        prog["dve"].append(lambda: e0.walk(dve.Fori, DispatchedDVE(e0)))
        prog["dve"].append(lambda: DispatchedDVE(e0).combine())
        finish_stage()

        norm(Norm("n1", x))
        attn_stage(Attn("a1", J_X1, J_X1 + 1, 1024, 64, 1, False), stage[0])
        stage[0] += 1
        norm(Norm("n1e", x))
        route(1)
        ffn(Ffn("moe1", J_E1, 4, [P] * 8, ACT.Gelu, mlp_up, mlp_down, False, 72, 9, by_expert, x))
        finish_stage()

        norm(Norm("n2", x))
        attn_stage(Attn("a2", J_X2, J_X2 + 1, 1024, 128, 2, True), stage[0])
        stage[0] += 1
        norm(Norm("n2e", x))
        route(2)
        cols2 = [P] * 5 + [64]
        up2 = lambda w, g, k, j: w[:, g * 1408 + k * 704 + j * P:g * 1408 + k * 704 + j * P + cols2[j]]
        down2 = lambda w, j: w[:, 2816 + j * D:2816 + (j + 1) * D]
        ffn(Ffn("moe2", J_E2, 4, cols2, ACT.Silu, up2, down2, True, None, None, by_expert, x))
        finish_stage()

        norm(Norm("n3", x))
        attn_stage(Attn("a3", J_X3, J_X3, 512, 64, 3, False), stage[0])
        stage[0] += 1
        norm(Norm("n3e", x))
        route(3)
        up3s = lambda w, g, k, j: w[:, g * 1024 + k * 512 + j * P:g * 1024 + k * 512 + (j + 1) * P]
        down3s = lambda w, j: w[:, 2048 + j * D:2048 + (j + 1) * D]
        shared = lambda t, e, j: wgt[:, bass.ds(t, 1), 16:17].rearrange("p a b -> p (a b)")
        ffn(Ffn("shared3", J_SH, 0, [P] * 4, ACT.Silu, up3s, down3s, True, None, None, shared, x, single=True))
        finish_stage()
        up3 = lambda w, g, k, j: w[:, 768 * j + g * D + k * P:768 * j + g * D + (k + 1) * P]
        down3 = lambda w, j: w[:, 768 * j + 512:768 * (j + 1)]
        by_pack = lambda t, e, j: wgt[:, bass.ds(t, 1), bass.ds(4 * e + j, 1)].rearrange("p a b -> p (a b)")
        ffn(Ffn("moe3", J_E3, 2, [P] * 4, ACT.Silu, up3, down3, True, None, None, by_pack, x, each=True))
        finish_stage()

        FULL = [("w", P, 0, 4096)]
        JOBS = [(J_X0, 1, [("wx0", P, 0, 2304), ("wx0c", CP, 2304, 768)]),
                (J_F0, 1, [("wf0", P, 0, 4096)]),
                (J_E0, 8, [("we0", P, 0, 4096)]),
                (J_X1, 1, [("wx1", P, 0, 4096)]),
                (J_X1 + 1, 1, [("wx1c", CP, 0, 4096)]),
                (J_E1, 8, [("we1", P, 0, 4096)]),
                (J_X2, 1, [("wx2", P, 0, 4096)]),
                (J_X2 + 1, 1, [("wx2c", CP, 0, 4096)]),
                (J_E2, 8, [("we2", P, 0, 4096), ("we2r", 64, 4096, 256)]),
                (J_X3, 1, [("wx3", P, 0, 2048), ("wx3c", CP, 2048, 2048)]),
                (J_SH, 1, [("ws3", P, 0, 3072)]),
                (J_E3, 4, [("we3", P, 0, 3072)])]

        landed = {0: 0, 1: 0}
        plan = []
        for j0, n, pieces in JOBS:
            base = dict(landed)
            plan.append((j0, n, pieces, base))
            for j in range(n):
                landed[(j0 + j) % 2] += 16 * len(pieces)

        def job_loop(fori, j0, n, body, middle=None):
            if n == 1:
                body(j0, j0 % 2, 0, 0)
            else:
                if middle is not None:
                    for off in range(2):
                        body(j0 + off, (j0 + off) % 2, off, 0)
                    middle()
                with fori(0 if middle is None else 1, n // 2) as i:
                    for off in range(2):
                        body(2 * i + (j0 + off), (j0 + off) % 2, 2 * i + off, i)

        tmpw = wsp[:, 1].rearrange("p h n -> p (h n)").bitcast(F32)
        ctxr = tmpw[0:CP, 0:KC * GA]
        rwr = tmpw[:, KC * GA:KC * GA + NRC]
        b2r = raw[0:33, 1, :]
        s_tmp = sem("temporaries_loaded")
        s_zero = sem("skip_cleared")

        @block.sync
        def _(sp):
            sp.dma_start(cst[:], a["cst"]).then_inc(s_const, 16)
            sp.dma_start(xT[:].rearrange("p a b c -> p (a b c)")[:, 0:8 * D].bitcast(F32), a["s4"]).then_inc(s_const, 16)
            sp.dma_start(LDT, a["ldt"].partition_broadcast(P)).then_inc(s_const, 16)
            sp.dma_start(sc[:], a["sc"].partition_broadcast(P)).then_inc(s_const, 16)
            sp.dma_start(mk8[:], a["cmask"].partition_broadcast(P)).then_inc(s_const, 16)
            sp.dma_start(tm8[:], a["tmask"]).then_inc(s_const, 16)
            sp.wait_ge(s_zero, 1)
            sp.dma_start(dsk[0:P:16, :], a["dskip"]).then_inc(s_const, 16)
            sp.dma_start(b1c[:], a["b1"]).then_inc(s_const, 16)
            sp.dma_start(brow[:].rearrange("p a b -> p (a b)"), a["brow"].partition_broadcast(P)).then_inc(s_const, 16)
            sp.dma_start(ctxr, a["ctx"]).then_inc(s_tmp, 16)
            sp.dma_start(rwr, a["wr"]).then_inc(s_tmp, 16)
            for r in (0, 32):
                sp.dma_start(b2r[r:r + 1], a["b2"]).then_inc(s_tmp, 16)
            sp.dma_start(x[:], a["x"]).then_inc(s_x, 16)

            def load(job, slot, e, seen, pieces, family):
                if not (isinstance(job, int) and job < 2):
                    sp.wait_ge(s_w, job - 1)
                elif job == 1:
                    sp.wait_ge(s_cdone, 1)
                for name, rows_, at, n in pieces:
                    src = a[name] if not family else a[name][bass.ds(e, 1)].rearrange("e p n -> (e p) n")
                    sp.dma_start(raw[0:rows_, slot, at:at + n], src).then_inc(s_raw[slot], 16)

            for j0, n, pieces, base in plan:
                if j0 == J_E0:
                    kg.store(sp)
                    for s in s_end:
                        sp.wait_ge(s, 1)
                    sp.dma_start(rows[:], a["rows"].partition_broadcast(P)).then_inc(s_rows, 16)
                    cv.sp_part(sp)
                job_loop(sp.Fori, j0, n, lambda j, s, e, seen: load(j, s, e, seen, pieces, n > 1))
            for s in s_end:
                sp.wait_ge(s, stage[0])
            sp.dma_start(out, x[:]).then_inc(s_out, 16)
            sp.wait_ge(s_out, 16)

        @block.gpsimd
        def _(pool):
            start_carrier(pool)
            pool.memset(dsk[:], 0.0).then_inc(s_zero, 1)
            for col, (s, n) in enumerate(credits):
                pool.memset(spare[:, col:col + 1], 0.0).then_inc(s, n)
            pool.memset(ones[:], 1.0)
            pool.memset(eps_t[:], EPS)
            pool.memset(b2s[:].rearrange("p a b -> p (a b)"), 0.0)
            pool.wait_ge(s_const, N_CONST)
            pool.tensor_copy(tri[:], cst[:, C_TRI:C_TRI + P])
            pool.tensor_copy(rev[:], cst[:, C_REV:C_REV + P])
            pool.wait_ge(s_tmp, 64)
            n_step = [0]

            def step(i):
                n_step[0] += 1
                i.then_inc(s_pst, 1)
                pool.wait_ge(s_pst, n_step[0])
            ch = [ctxs[:, h].rearrange("p k n -> p (k n)") for h in range(2)]
            step(pool.tensor_copy(ch[0], ctxr))
            pool.tensor_tensor(ch[1], ctxr, ch[0], ALU.subtract)
            step(pool.tensor_scalar(rwr, rwr, WSCALE, 1.0, ALU.mult, ALU.mult))
            step(pool.tensor_copy(rws[:, 0], rwr))
            pool.tensor_tensor(rws[:, 1], rwr, rws[:, 0], ALU.subtract)
            b2f = b2s[:].rearrange("p a b -> p (a b)")
            for r in (0, 32):
                step(pool.tensor_scalar(b2r[r:r + 1], b2r[r:r + 1], WSCALE, 1.0, ALU.mult, ALU.mult))
                step(pool.tensor_copy(b2f[r:r + 1], b2r[r:r + 1]))
            step(pool.tensor_tensor(b2f[32:33], b2r[32:33], b2f[32:33], ALU.subtract))
            pool.drain().then_inc(s_cdone, 1)
            steps_done = n_step[0]

            for j0, n, pieces, base in plan:
                def split(j, slot, e, seen):
                    pool.wait_ge(s_raw[slot], base[slot] + 16 * len(pieces) * (seen + 1))
                    if not (isinstance(j, int) and j < 2):
                        pool.wait_ge(s_wfree, j - 1)
                    pool.tensor_tensor(spare[:, 63:64], spare[:, 0:1], spare[:, 0:1], ALU.mult)
                    for _, rows_, at, w in pieces:
                        v = raw[0:rows_, slot, at:at + w]
                        hi, lo = (wsp[0:rows_, slot, h, at:at + w] for h in range(2))
                        pool.tensor_scalar(v, v, WSCALE, 1.0, ALU.mult, ALU.mult)
                        pool.drain()
                        pool.tensor_copy(hi, v)
                        pool.drain()
                        pool.tensor_tensor(lo, v, hi, ALU.subtract)
                    pool.drain().then_inc(s_w, 1)
                moe = DispatchedPool(e0) if j0 == J_E0 else None
                job_loop(pool.Fori, j0, n, split, moe and moe.scatter)
                if moe:
                    moe.gather()

        @block.tensor
        def _(_pe):
            start_carrier(pe)
            for part in prog["pe"]:
                part()

        @block.scalar
        def _(_act):
            start_carrier(act)
            for part in prog["act"]:
                part()

        @block.vector
        def _(_dve):
            for part in prog["dve"]:
                part()


def kernel(**inputs):
    import numpy as np
    import concourse.bacc as bacc
    from concourse.bass_utils import run_bass_kernel_spmd as run

    g = {k: np.asarray(v) for k, v in inputs.items()}
    c = np.ascontiguousarray

    def kp(w, rows=P):
        k, n = w.shape
        return w.reshape(k // rows, rows, n).transpose(1, 0, 2).reshape(rows, -1)

    def cat(*parts):
        return c(np.concatenate(parts, axis=-1))

    cst = np.zeros((P, NCST), np.float32)
    r = np.arange(P)
    cst[:, 0:P] = np.eye(P)
    cst[:, C_TRI:C_TRI + P] = r[:, None] < r[None, :]
    cst[:, C_IOTA:C_IOTA + 16] = np.arange(16)
    cst[:, C_K16:C_K16 + 16] = 16 * np.arange(16)
    cst[:, C_MASK:C_MASK + 8] = (r[:, None] // 16) == np.arange(8)
    cst[:, C_REV:C_REV + P] = np.eye(P)[::-1]
    cst[:, C_SPARE:C_SPARE + 2 * NT] = SLOTS + P * np.arange(2 * NT) + r[:, None]
    ph = np.where(r[:, None] < 64, [[0.25, 0.25, 0.5]], [[0.5, 0.0, 0.25]])
    cst[:, C_PH:C_PH + 3] = ph
    cst[:, C_PHR:C_PHR + 3] = ph * -SIN_SCALE
    a = {"cst": cst}
    a["x"] = c(g["x"].reshape(NT, P, D).transpose(1, 0, 2))
    a["ctx"] = c(kp(g["ctx_768"].reshape(GA, DV).T, CP))
    a["s4"] = c(np.tile(np.concatenate([g["L0_xattn_" + n].T for n in ("A_re", "A_im", "C_re", "C_im")], axis=1), (2, 1)))
    a["ldt"] = c(g["L0_xattn_log_dt"])
    a["sc"] = cat(g["g_xattn"], g["g_ffn"], g["L0_xattn_mod_gate"].reshape(1), g["L1_ffn_br"])
    a["cmask"] = c(g["mask_BxS2_bf1"].reshape(GA).view(np.uint8))
    a["tmask"] = c(g["mask_BxS_bf1"].reshape(NT, P).T.view(np.uint8))
    a["dskip"] = c(g["L0_xattn_D_skip"].reshape(D // 8, 8).T)
    a["b1"] = cat(g["L0_xattn_b1"].reshape(8, P).T, g["L0_ffn_b1"].reshape(64, P).T, g["L1_ffn_b1"].reshape(64, P).T)
    a["brow"] = cat(g["L1_xattn_b_out"], g["L2_xattn_bout"], g["L3_xattn_bo"])
    a["wr"] = cat(kp(g["L0_ffn_w_router"]), kp(g["L1_ffn_Wr"]), kp(g["L2_ffn_router_w"].T),
                  kp(np.concatenate([g["L3_ffn_Wg"].T, g["L3_ffn_Wsg"].T], axis=1)))
    a["b2"] = cat(g["L0_xattn_b2"].reshape(1, -1), g["L0_ffn_b2"].reshape(1, -1), g["L1_ffn_b2"].reshape(1, -1))
    L0x = lambda n: g["L0_xattn_" + n]
    a["rows"] = cat(*(L0x(n) for n in ("g_norm_in", "b_norm_in", "g_ffn", "b_ffn", "g_norm_out", "b_norm_out",
                                       "b_film_in", "b_film_out")))
    a["wx0"] = cat(kp(L0x("Wq")), kp(L0x("W_film_in")), kp(L0x("W_film_out")))
    a["wx0c"] = cat(kp(L0x("Wk"), CP), kp(L0x("Wv"), CP))
    a["wf0"] = cat(kp(L0x("W1")), kp(L0x("W2")))
    a["we0"] = c(np.stack([cat(kp(g["L0_ffn_w1"][e]), kp(g["L0_ffn_w2"][e])) for e in range(8)]))
    a["wx1"] = cat(kp(g["L1_xattn_w_q"]), kp(g["L1_xattn_w_out"]))
    a["wx1c"] = cat(kp(g["L1_xattn_w_k"], CP), kp(g["L1_xattn_w_v"], CP))
    a["we1"] = c(np.stack([cat(kp(g["L1_ffn_W1"][e]), kp(g["L1_ffn_W2"][e])) for e in range(8)]))
    a["wx2"] = cat(kp(g["L2_xattn_Wq"]), kp(g["L2_xattn_Wout"]))
    a["wx2c"] = cat(kp(g["L2_xattn_Wk"], CP), kp(g["L2_xattn_Wv"], CP))
    a["we2"] = c(np.stack([cat(kp(g["L2_ffn_gate_w"][e].T), kp(g["L2_ffn_up_w"][e].T),
                               kp(g["L2_ffn_down_w"][e].T[0:640])) for e in range(8)]))
    a["we2r"] = c(np.stack([g["L2_ffn_down_w"][e].T[640:704] for e in range(8)]))
    a["wx3"] = cat(kp(g["L3_xattn_Wq"]), kp(g["L3_xattn_Wo"]))
    a["wx3c"] = cat(kp(g["L3_xattn_Wk"], CP), kp(g["L3_xattn_Wv"], CP))
    a["ws3"] = cat(kp(g["L3_ffn_Ws_gate"].T), kp(g["L3_ffn_Ws_up"].T), kp(g["L3_ffn_Ws_down"].T))
    a["we3"] = c(np.stack([cat(*(v for e in range(4 * p, 4 * p + 4) for v in (
        kp(g["L3_ffn_We_gate"][e].T), kp(g["L3_ffn_We_up"][e].T), g["L3_ffn_We_down"][e].T))) for p in range(4)]))

    nc = bacc.Bacc("TRN2", target_bir_lowering=False, num_devices=1)
    aps = {n: nc.dram_tensor("in_" + n, v.shape, mybir.dt.from_np(v.dtype), kind="ExternalInput").ap()
           for n, v in a.items()}
    o = nc.dram_tensor("out_x", (P, NT, D), F32, kind="ExternalOutput").ap()
    build(nc, aps, o)
    res = run(nc, [{"in_" + n: v for n, v in a.items()}], core_ids=[0])
    return c(res.results[0]["out_x"].transpose(1, 0, 2).reshape(B, S, D))
```

```python
import math
from contextlib import ExitStack

import concourse.bass as bass
from concourse import mybir

F32 = mybir.dt.float32
F16 = mybir.dt.float16
U32 = mybir.dt.uint32
U8 = mybir.dt.uint8
ALU = mybir.AluOpType
ACT = mybir.ActivationFunctionType
X = mybir.AxisListType.X

P = 128
B, S, D = 8, 256, 256
NT = B * S // P
KD = D // P
G, DV = 77, 192
KC, CP = 2, DV // 2
GA = B * G
EPS = 1e-5
WSCALE = 64.0
INV = 1.0 / WSCALE
NEG = -1.0e30

SLOT = 4352
NS4, LAGS = 64, S
TWO_PI = 2.0 * math.pi
SIN_SCALE = -6.2831850
ROUND = 12582912.0
CAPACITY = int(1.5 * B * S * 2 / 8)
CHUNKS = ((384, 384), (384, 384, 384), (384, 384, 128))
SLOTS = 8 * max(sum(c) for c in CHUNKS)
DROPPED = 8 * CAPACITY
KROW = 384

R_GIN, R_BIN, R_GF, R_BF, R_GOUT, R_BOUT = range(6)
R_FI, R_FO, NR_ = 6, 8, 10
NROW = NR_ * D

C_TRI, C_IOTA, C_K16, C_MASK, C_PH, C_PHR, C_REV, C_SPARE, NCST = 128, 256, 272, 288, 296, 300, 304, 432, 464
ARENA = 20656

ROUTERS = [(0, 8), (16, 8), (32, 8), (48, 17)]
NRC = 48 + 34

J_X0, J_F0, J_E0, J_X1, J_E1, J_X2, J_E2, J_X3, J_SH, J_E3 = 0, 1, 2, 10, 12, 20, 22, 30, 31, 32


def build(nc, a, out):
    ctx = ExitStack()
    with ctx:
        def sb(name, shape, dt=F32):
            return ctx.enter_context(nc.sbuf_tensor(name, shape, dt))

        def sem(name):
            return ctx.enter_context(nc.semaphore(name))

        x = sb("x_resid", [P, NT, D])
        xT = sb("xT", [P, 2, KD, B * S], F16)
        raw = sb("w_raw", [P, 2, SLOT])
        wsp = sb("w_split", [P, 2, 2, SLOT], F16)
        ctxs = sb("ctx_split", [CP, 2, KC, GA], F16)
        rws = sb("router_split", [P, 2, NRC], F16)
        b1e = sb("b1_of_expert", [P, 8])
        b1c = sb("b1_cols", [P, 136])
        b2s = sb("b2_split", [33, 17, D], F16)
        ones = sb("ones16", [P, P], F16)
        tri = sb("tri16", [P, P], F16)
        rev = sb("rev16", [P, P], F16)
        cst = sb("consts", [P, NCST])
        ident, iota = cst[:, 0:P], cst[:, C_IOTA:C_IOTA + 16]
        sc = sb("scalars", [P, 17])
        tg = sb("tanh_gates", [P, 8])
        brow = sb("bout_rows", [P, 3, D])
        wgt = sb("expert_weights", [P, NT, 17])
        st6 = sb("bn_stats", [P, NT, 6])
        mean = sb("mean", [P, NT])
        rstd = sb("rstd", [P, NT])
        sm = sb("small", [P, 8, NT])
        xn = sb("xn", [P, 4, D])
        mk8 = sb("ctx_mask_u8", [P, GA], U8)
        tm8 = sb("text_mask_u8", [P, NT], U8)
        dsk = sb("skip", [P, D // 8])
        tmk = sb("text_mask", [P, NT])
        eps_t = sb("eps", [P, 1])
        spare = sb("credit_dummy", [1, 64])
        fits = sb("fits", [1, 4], U32)
        arena = sb("arena", [P, ARENA])

        ps = ctx.enter_context(nc.psum_tensor("ps", [P, 8, 512], F32))
        kdram = nc.dram_tensor("s4_kernel", [D, KROW, 2], F16, kind="Internal").ap()

        xs = nc.dram_tensor("dispatched", [DROPPED + 2 * B * S, D], F32, kind="Internal").ap()
        ys = nc.dram_tensor("expert_rows", [SLOTS, D], F32, kind="Internal").ap()

        class Area:
            def __init__(self, at=0):
                self.at = at

            def f32(self, *dims):
                n = math.prod(dims)
                v = arena[:, self.at:self.at + n]
                self.at += n
                assert self.at <= ARENA, self.at
                return shaped(v, dims)

            def f16(self, *dims):
                n = math.prod(dims)
                v = arena[:, self.at:self.at + n // 2].bitcast(F16)
                self.at += n // 2
                assert self.at <= ARENA, self.at
                return shaped(v, dims)

        def shaped(v, dims):
            if len(dims) == 1:
                return v
            names = "abcde"[:len(dims)]
            return v.rearrange(f"p ({' '.join(names)}) -> p {' '.join(names)}",
                               **{n: d for n, d in zip(names, dims)})

        s_const = sem("const_loaded")
        s_x = sem("x_loaded")
        s_cdone = sem("const_split_ready")
        s_raw = [sem("raw_loaded_0"), sem("raw_loaded_1")]
        s_w = sem("weights_split")
        s_wfree = sem("weights_used")
        s_pst = sem("pool_split_step")
        s_end = [sem(f"stage_end_{e}") for e in ("pe", "act", "dve")]
        s_out = sem("out_stored")
        credits = []

        def credit(name, n):
            s = sem(name)
            credits.append((s, n))
            return s

        block = ctx.enter_context(nc.Block())
        prog = {"pe": [], "act": [], "dve": []}
        pe, act, dve = nc.tensor, nc.scalar, nc.vector

        def barrier(eng, me, stage):
            eng.drain().then_inc(s_end[me], 1)
            for s in s_end:
                eng.wait_ge(s, stage + 1)

        def slot16(job):
            return wsp[:, job % 2]

        def mm3(out_ap, lhs, rhs, start, stop):
            pe.matmul(out_ap, lhs(0), rhs(0), start=start, stop=False)
            pe.matmul(out_ap, lhs(0), rhs(1), start=False, stop=False)
            return pe.matmul(out_ap, lhs(1), rhs(0), start=False, stop=stop)

        def bcast(v, n):
            return v.unsqueeze(1).to_broadcast([v.shape[0], n, v.shape[1]])

        def nothing(*args):
            pass

        carrier = {id(e): e.alloc_register("wait_carrier") for e in (pe, act, nc.gpsimd)}

        def settled(eng):
            eng.reg_add(carrier[id(eng)], carrier[id(eng)], 1)

        def start_carrier(eng):
            eng.reg_mov(carrier[id(eng)], 0)

        class Norm:
            stat_runs = 0
            tile_runs = 0
            var, std = sem("norm_var_ready"), sem("norm_std_ready")
            xn, full, hi = sem("norm_tile_ready"), sem("norm_tile_transposed"), sem("norm_hi_ready")
            free = credit("norm_bank_free", 4)

            def __init__(self, name, src, keep=None, affine=None):
                self.src, self.keep, self.affine = src, keep, affine
                self.rs = Norm.stat_runs
                Norm.stat_runs += 1
                self.rt = None

            def dve_stats(self):
                with dve.Fori(0, NT) as t:
                    dve.bn_stats(st6[:, t, :], self.src[:, t, :])
                dve.drain()
                dve.tensor_tensor(mean[:], st6[:, :, 1], st6[:, :, 4], ALU.add)
                dve.tensor_tensor(sm[:, 0], st6[:, :, 1], st6[:, :, 4], ALU.subtract)
                dve.tensor_tensor(sm[:, 1], st6[:, :, 2], st6[:, :, 5], ALU.add)
                dve.drain()
                dve.tensor_scalar(mean[:], mean[:], 0.5, None, ALU.mult)
                dve.tensor_tensor(sm[:, 0], sm[:, 0], sm[:, 0], ALU.mult)
                dve.tensor_scalar(sm[:, 1], sm[:, 1], 1.0 / D, None, ALU.mult)
                dve.drain()
                dve.scalar_tensor_tensor(sm[:, 2], sm[:, 0], 0.25, sm[:, 1], ALU.mult, ALU.add)\
                    .then_inc(self.var, 1)
                dve.wait_ge(self.std, self.rs + 1)
                dve.reciprocal(rstd[:], sm[:, 3])
                dve.drain()

            def act_stats(self):
                act.wait_ge(self.var, self.rs + 1)
                act.activation(sm[:, 3], sm[:, 2], ACT.Sqrt, bias=eps_t[:, 0:1]).then_inc(self.std, 1)

            def normalise(self, dst, t):
                return dve.tensor_scalar(dst, self.src[:, t, :], mean[:, bass.ds(t, 1)],
                                         rstd[:, bass.ds(t, 1)], ALU.subtract, ALU.mult)

            def dve_low(self, i):
                for k in range(4):
                    t = 4 * i + k
                    dve.wait_ge(self.hi, self.rt + t + 1)
                    dve.tensor_tensor(xT[:, 1, :, bass.ds(t * P, P)], ps[:, k, 0:D].rearrange("p (c n) -> p c n", c=KD),
                                      xT[:, 0, :, bass.ds(t * P, P)], ALU.subtract).then_inc(self.free, 1)

            def dve_kept(self, i):
                for k in range(4):
                    self.normalise(self.keep[:, 4 * i + k, :], 4 * i + k).then_inc(self.xn, 1)

            def dve_tiles(self):
                if self.keep is not None:
                    self.dve_kept(0)
                    with dve.Fori(0, NT // 4 - 1) as i:
                        self.dve_kept(i + 1)
                        self.dve_low(i)
                    self.dve_low(NT // 4 - 1)
                    return
                g, b = self.affine
                with dve.Fori(0, NT // 4) as i:
                    for k in range(4):
                        self.normalise(xn[:, k], 4 * i + k)
                    dve.drain()
                    dve.tensor_tensor(xn[:], xn[:], bcast(g, 4), ALU.mult)
                    dve.drain()
                    for k in range(4):
                        dve.tensor_tensor(xn[:, k], xn[:, k], b, ALU.add).then_inc(self.xn, 1)
                    self.dve_low(i)

            def pe_tile(self, t, k, src):
                pe.wait_ge(self.xn, self.rt + t + 1)
                pe.wait_ge(self.free, self.rt + t + 1)
                for c in range(KD):
                    m = pe.transpose(ps[:, k, c * P:(c + 1) * P], src[:, c * P:(c + 1) * P], ident)
                m.then_inc(self.full, 1)

            def pe_tiles(self):
                if self.keep is not None:
                    for t in range(NT):
                        self.pe_tile(t, t % 4, self.keep[:, t, :])
                    return
                with pe.Fori(0, NT // 4) as i:
                    for k in range(4):
                        self.pe_tile(4 * i + k, k, xn[:, k])

            def act_tiles(self):
                with act.Fori(0, NT // 4) as i:
                    for k in range(4):
                        t = 4 * i + k
                        act.wait_ge(self.full, self.rt + t + 1)
                        settled(act)
                        act.activation(xT[:, 0, :, bass.ds(t * P, P)], ps[:, k, 0:D].rearrange("p (c n) -> p c n", c=KD),
                                       ACT.Copy).then_inc(self.hi, 1)

        def norm_stage(n, stage):
            n.rt = Norm.tile_runs * NT
            Norm.tile_runs += 1
            prog["dve"] += [n.dve_stats, n.dve_tiles, lambda: barrier(dve, 2, stage)]
            prog["act"] += [n.act_stats, n.act_tiles, lambda: barrier(act, 1, stage)]
            prog["pe"] += [n.pe_tiles, lambda: barrier(pe, 0, stage)]

        ROUTE_END = 2560

        route_sems = [sem("route_" + n) for n in ("logits_ready", "exp_arg_ready", "exp_ready", "chosen_ready",
                                                  "positions_ready", "slots_ready")]

        class Route:
            def __init__(self, name, layer):
                self.layer = layer
                self.col, self.E = ROUTERS[layer]
                self.cap = sum(CHUNKS[layer]) if layer < 3 else None
                self.full, self.arg, self.ex, self.sel, self.pos, self.s_ix = route_sems
                E = self.E
                ar = Area()
                self.L = ar.f32(NT, 17)
                self.mx = ar.f32(NT, 8)
                self.ix = ar.f32(NT, 8)
                self.ixf = ar.f32(NT, 2)
                self.io = ar.f32(16)
                self.e = ar.f32(NT, 17)
                self.s = ar.f32(NT, 16)
                self.t = ar.f32(NT, 16)
                self.h = ar.f16(NT, 16)
                self.den = ar.f32(NT)
                if layer < 3:
                    self.oh = ar.f32(NT, 2, 8)
                    self.pr = ar.f32(NT, 2, 8)
                    self.slot = ar.f32(NT, 2)
                    self.kept = ar.f32(NT, 2)
                    self.to, self.fro = (ar.f32(NT, 2).bitcast(U32) for _ in range(2))
                    self.w2 = ar.f32(NT, 2)
                    assert ar.at <= ROUTE_END

            def slots(self):
                pos = ps[:, 1, 0:NT * 8].rearrange("p (t e) -> p t e", t=NT).unsqueeze(2).to_broadcast([P, NT, 2, 8])
                w = wgt[:, :, 0:8].unsqueeze(2).to_broadcast([P, NT, 2, 8])
                io = iota[:, 0:8].unsqueeze(1).unsqueeze(1).to_broadcast([P, NT, 2, 8])
                spare_row = cst[:, C_SPARE:C_SPARE + 2 * NT].rearrange("p (t k) -> p t k", k=2)
                dve.tensor_tensor(self.oh, io, self.ixf[:].unsqueeze(3).to_broadcast([P, NT, 2, 8]), ALU.is_equal)
                dve.drain()
                dve.tensor_tensor(self.pr, self.oh, pos, ALU.mult)
                dve.tensor_tensor(self.oh, self.oh, w, ALU.mult)
                dve.drain()
                dve.tensor_reduce(self.slot, self.pr, X, ALU.add)
                dve.tensor_reduce(self.w2, self.oh, X, ALU.add)
                dve.drain()
                dve.tensor_scalar(self.kept, self.slot, float(self.cap), None, ALU.is_lt)
                dve.drain()
                dve.scalar_tensor_tensor(self.slot, self.ixf, float(self.cap), self.slot, ALU.mult, ALU.add)
                if self.layer > 0:
                    total = ps[:, 1, NT * 8:NT * 8 + 8]
                    dve.tensor_reduce(self.den[:, 0:1], total, X, ALU.max)
                    dve.tensor_reduce(self.den[:, 1:2], total, X, ALU.add)
                    dve.drain()
                    dve.tensor_scalar(self.den[:, 2:3], self.den[:, 0:1], float(self.cap) + 0.5, None, ALU.is_lt)
                    dve.tensor_scalar(self.den[:, 3:4], self.den[:, 1:2], 2.0 * B * S + 0.5, None, ALU.is_lt)
                    dve.drain()
                    dve.tensor_tensor(self.den[:, 4:5], self.den[:, 2:3], self.den[:, 3:4], ALU.mult)
                    dve.drain()
                    dve.tensor_copy(fits[:, self.layer:self.layer + 1], self.den[0:1, 4:5])
                dve.drain()
                dve.tensor_tensor(self.pr[:, :, :, 0], self.slot, spare_row, ALU.subtract)
                dve.tensor_tensor(self.pr[:, :, :, 1], self.slot, self.kept, ALU.mult)
                dve.drain()
                dve.tensor_tensor(self.pr[:, :, :, 0], self.pr[:, :, :, 0], self.kept, ALU.mult)
                dve.tensor_copy(self.fro, self.pr[:, :, :, 1])
                dve.drain()
                dve.tensor_tensor(self.pr[:, :, :, 0], self.pr[:, :, :, 0], spare_row, ALU.add)
                dve.drain()
                dve.tensor_copy(self.to, self.pr[:, :, :, 0])
                dve.drain().then_inc(self.s_ix, 1)

            def pe_part(self):
                E, c0 = self.E, self.col
                with pe.Fori(0, NT) as t:
                    for c in range(KD):
                        m = mm3(ps[:, 0, bass.ds(t * E, E)], lambda h: xT[:, h, c, bass.ds(t * P, P)],
                                lambda h: rws[:, h, c0 + c * E:c0 + (c + 1) * E], c == 0, c == KD - 1)
                    m.then_inc(self.full, 1)
                if self.layer < 3:
                    pe.wait_ge(self.sel, self.layer + 1)
                    pe.matmul(ps[:, 1, 0:NT * 8], tri[:], self.h[:, :, 0:8], start=True, stop=True)
                    for t in range(NT - 1):
                        rest = NT - 1 - t
                        src = self.h[:, t:t + 1, 0:8].to_broadcast([P, rest, 8])
                        m = pe.matmul(ps[:, 1, (t + 1) * 8:NT * 8], ones[:], src, start=False,
                                      stop=True, skip_group_check=True)
                    for t in range(NT):
                        m = pe.matmul(ps[:, 1, NT * 8:NT * 8 + 8], ones[:], self.h[:, t, 0:8], start=t == 0,
                                      stop=t == NT - 1)
                    m.then_inc(self.pos, 1)

            def act_part(self):
                ne = 16 if self.layer == 3 else 8
                act.wait_ge(self.arg, self.layer + 1)
                act.activation(self.e[:, :, 0:self.E], self.e[:, :, 0:self.E], ACT.Exp).then_inc(self.ex, 1)

            def dve_part(self):
                E, layer = self.E, self.layer
                ne = 16 if layer == 3 else 8
                L, e = self.L, self.e
                dve.wait_ge(self.full, NT * (layer + 1))
                dve.tensor_scalar(L[:, :, 0:E], ps[:, 0, 0:NT * E].rearrange("p (t e) -> p t e", t=NT), INV, None, ALU.mult)
                dve.drain()
                if layer == 1:
                    dve.tensor_tensor(L[:, :, 0:E], L[:, :, 0:E], bcast(sc[:, 9:17], NT), ALU.add)
                    dve.drain()
                for t in range(NT):
                    dve.max(self.mx[:, t, :], L[:, t, 0:ne])
                dve.drain()
                m1 = self.mx[:, :, 0:1].to_broadcast([P, NT, ne])
                m2 = self.mx[:, :, 1:2].to_broadcast([P, NT, ne])
                dve.tensor_tensor(e[:, :, 0:ne], L[:, :, 0:ne], m1, ALU.subtract)
                if layer == 3:
                    dve.tensor_scalar(e[:, :, 16:17], L[:, :, 16:17], -1.0, None, ALU.mult)
                dve.drain().then_inc(self.arg, 1)
                s, t2 = self.s[:, :, 0:ne], self.t[:, :, 0:ne]
                for t in range(NT):
                    dve.max_index(self.ix[:, t, :].bitcast(U32), self.mx[:, t, :], L[:, t, 0:ne])
                dve.drain()
                dve.tensor_copy(self.ixf[:], self.ix[:, :, 0:2].bitcast(U32))
                dve.drain()
                if layer == 1:
                    dve.tensor_tensor(s, L[:, :, 0:ne], m2, ALU.is_ge)
                else:
                    io = bcast(iota[:, 0:ne], NT)
                    dve.tensor_tensor(s, io, self.ixf[:, :, 0:1].to_broadcast([P, NT, ne]), ALU.is_equal)
                    dve.tensor_tensor(t2, io, self.ixf[:, :, 1:2].to_broadcast([P, NT, ne]), ALU.is_equal)
                    dve.drain()
                    dve.tensor_tensor(s, s, t2, ALU.add)
                dve.drain()
                if layer < 3:
                    dve.tensor_copy(self.h[:, :, 0:8], s).then_inc(self.sel, 1)
                dve.drain()
                dve.wait_ge(self.ex, layer + 1)
                den = self.den[:]
                if layer == 2:
                    dve.tensor_reduce(den, e[:, :, 0:ne], X, ALU.add)
                    dve.drain()
                dve.tensor_tensor(s, s, e[:, :, 0:ne], ALU.mult)
                dve.drain()
                if layer != 2:
                    dve.tensor_reduce(den, s, X, ALU.add)
                    dve.drain()
                dve.reciprocal(den, den)
                dve.drain()
                dve.tensor_scalar(den, den, tg[:, 4 + layer:5 + layer], INV, ALU.mult, ALU.mult)
                dve.drain()
                dve.tensor_tensor(wgt[:, :, 0:ne], s, den.unsqueeze(2).to_broadcast([P, NT, ne]), ALU.mult)
                if layer < 3:
                    dve.drain()
                    dve.wait_ge(self.pos, layer + 1)
                if layer == 0:
                    dve.tensor_scalar(t2, ps[:, 1, 0:NT * 8].rearrange("p (t e) -> p t e", t=NT), float(CAPACITY), None, ALU.is_lt)
                    dve.drain()
                    dve.tensor_tensor(wgt[:, :, 0:8], wgt[:, :, 0:8], t2, ALU.mult)
                    dve.drain()
                if layer < 3:
                    self.slots()
                if layer == 3:
                    dve.tensor_scalar(e[:, :, 16:17], e[:, :, 16:17], 1.0, None, ALU.add)
                    dve.drain()
                    dve.reciprocal(e[:, :, 16:17], e[:, :, 16:17])
                    dve.drain()
                    dve.tensor_scalar(wgt[:, :, 16:17], e[:, :, 16:17], tg[:, 7:8], INV, ALU.mult, ALU.mult)
                dve.drain()

        TOK = 512
        NCH = B * S // TOK
        Q = TOK // P

        class Ffn:

            def __init__(self, name, job, pairs, cols, act_fn, up, down, gated, bias1, b2_row,
                         weight, dst, each=False, area=0, single=False):
                self.name, self.job, self.pairs, self.single = name, job, pairs, single
                self.cols, self.fn, self.up, self.down = cols, act_fn, up, down
                self.gated, self.bias1, self.b2_row = gated, bias1, b2_row
                self.weight, self.dst, self.each = weight, dst, each
                self.nh = len(cols)
                self.R = 2 if gated else 4
                self.lag = 1 if each else 2
                ar = Area(area)
                self.hf = ar.f32(self.R, TOK)
                self.hh = ar.f16(self.R, 2, TOK)
                self.s_up = sem(name + "_up_full")
                self.s_act = credit(name + "_act_done", self.R)
                self.s_upfree = credit(name + "_gate_product_done", self.R)
                self.s_hhi = sem(name + "_hi_ready")
                self.s_h = credit(name + "_hidden_ready", self.R)
                self.s_hfree = credit(name + "_down_done", self.R)
                self.s_yfree = credit(name + "_y_free", 2 if each else 1)

            def bank(self, j):
                return 2 * (j % 2) if self.gated else j % 4

            def schedule(self, fori, unit_up, unit_down, begin, end):
                nh, lag = self.nh, self.lag

                def steps(i0, off, cont_in, cont_out):
                    if not cont_in:
                        begin(i0, off)
                        for j in range(lag):
                            unit_up(i0, off, 0, j)
                    with fori(0, NCH - 1) as c:
                        for j in range(nh):
                            nx = j + lag
                            unit_up(i0, off, c, nx) if nx < nh else unit_up(i0, off, c + 1, nx - nh)
                            unit_down(i0, off, c, j)
                    for j in range(nh):
                        nx = j + lag
                        if nx < nh:
                            unit_up(i0, off, NCH - 1, nx)
                        elif cont_out:
                            if nx == nh:
                                begin(i0, off + 1)
                            unit_up(i0, off + 1, 0, nx - nh)
                        unit_down(i0, off, NCH - 1, j)
                    end(i0, off)

                if self.single:
                    steps(0, 0, False, False)
                else:
                    with fori(0, self.pairs) as i:
                        steps(2 * i, 0, False, True)
                        steps(2 * i, 1, True, False)

            def unit(self, i0, off, c, j):
                return ((i0 + off) * NCH + c) * self.nh + j

            def pe_part(self):
                def begin(i0, off):
                    pe.wait_ge(s_w, self.job + i0 + off + 1)

                def unit_up(i0, off, c, j):
                    w = wsp[:, (self.job + off) % 2]
                    n = self.unit(i0, off, c, j)
                    m = self.cols[j]
                    bk = self.bank(j)
                    pe.wait_ge(self.s_upfree if self.gated else self.s_act, n + 1)
                    if self.gated and m < P:
                        pe.matmul(ps[0:m, bk, 0:1], w[:, 0, 0:m], w[:, 0, 0:1], start=True, stop=True)
                    for g in range(2 if self.gated else 1):
                        for k in range(KD):
                            last = mm3(ps[0:m, bk + g, :],
                                       lambda h: self.up(w[:, h], g, k, j),
                                       lambda h: xT[:, h, k, bass.ds(c * TOK, TOK)], k == 0, k == KD - 1)
                    last.then_inc(self.s_up, 1)

                def unit_down(i0, off, c, j):
                    w = wsp[:, (self.job + off) % 2]
                    n = self.unit(i0, off, c, j)
                    step = (i0 + off) * NCH + c
                    m = self.cols[j]
                    r = j % self.R
                    pe.wait_ge(self.s_h, n + 1 + self.R)
                    first = self.each or j == 0
                    final = self.each or j == self.nh - 1
                    if first:
                        pe.wait_ge(self.s_yfree, (n if self.each else step) + 1)
                    for q in range(Q):
                        if self.each:
                            o = ps[:, 4 + 2 * (j % 2) + q // 2, (q % 2) * D:(q % 2 + 1) * D]
                        else:
                            o = ps[:, 4 + q, 0:D]
                        if first and self.b2_row is not None:
                            pe.matmul(o, ones[0:33, :], b2s[:, self.b2_row + i0 + off, :], start=True, stop=False)
                        last = mm3(o, lambda h: self.hh[0:m, r, h, q * P:(q + 1) * P],
                                   lambda h: self.down(w[0:m, h], j),
                                   first and self.b2_row is None, final)
                    last.then_inc(self.s_hfree, 1)

                def end(i0, off):
                    pe.drain().then_inc(s_wfree, 1)

                self.schedule(pe.Fori, unit_up, unit_down, begin, end)

            def act_part(self):
                def begin(i0, off):
                    if self.bias1 is not None:
                        act.drain()
                        act.copy(b1e[:], b1c[:, bass.ds(self.bias1 + (i0 + off) * self.nh, self.nh)])
                        act.drain()

                def unit_up(i0, off, c, j):
                    n = self.unit(i0, off, c, j)
                    m, r, bk = self.cols[j], j % self.R, self.bank(j)
                    act.wait_ge(self.s_up, n + 1)
                    act.wait_ge(self.s_h, n + 1)
                    settled(act)
                    kw = {}
                    if self.bias1 is not None:
                        kw["bias"] = b1e[:, j:j + 1]
                    act.activation(self.hf[0:m, r, :], ps[0:m, bk, :], self.fn, scale=INV, **kw)\
                        .then_inc(self.s_act, 1)

                self.schedule(act.Fori, unit_up, nothing, begin, nothing)

            def dve_part(self):
                def unit_up(i0, off, c, j):
                    n = self.unit(i0, off, c, j)
                    m, r, bk = self.cols[j], j % self.R, self.bank(j)
                    hf = self.hf[0:m, r, :]
                    dve.wait_ge(self.s_act, n + 1 + self.R)
                    if self.gated:
                        dve.scalar_tensor_tensor(hf, ps[0:m, bk + 1, :], INV, hf, ALU.mult, ALU.mult)\
                            .then_inc(self.s_upfree, 1)
                        dve.wait_ge(self.s_upfree, n + 1 + self.R)
                    dve.wait_ge(self.s_hfree, n + 1)
                    dve.tensor_copy(self.hh[0:m, r, 0, :], hf).then_inc(self.s_hhi, 1)
                    dve.wait_ge(self.s_hhi, n + 1)
                    dve.tensor_tensor(self.hh[0:m, r, 1, :], hf, self.hh[0:m, r, 0, :], ALU.subtract)\
                        .then_inc(self.s_h, 1)

                def unit_down(i0, off, c, j):
                    if not (self.each or j == self.nh - 1):
                        return
                    n = self.unit(i0, off, c, j)
                    dve.drain()
                    dve.wait_ge(self.s_hfree, n + 1 + self.R)
                    for q in range(Q):
                        t = c * Q + q
                        if self.each:
                            y = ps[:, 4 + 2 * (j % 2) + q // 2, (q % 2) * D:(q % 2 + 1) * D]
                        else:
                            y = ps[:, 4 + q, 0:D]
                        i = dve.scalar_tensor_tensor(self.dst[:, t, :], y, self.weight(t, i0 + off, j),
                                                     self.dst[:, t, :], ALU.mult, ALU.add)
                    i.then_inc(self.s_yfree, 1)

                self.schedule(dve.Fori, unit_up, unit_down, nothing, nothing)

        class Dispatched:
            ROWS, NQ, CR, LAG = 384, 3, 4, 2

            def __init__(self, name, job, cols, act_fn, up, down, gated, bias1, b2_row, route, at, before=None):
                self.name, self.job, self.cols, self.fn, self.up, self.down = name, job, cols, act_fn, up, down
                self.gated, self.bias1, self.b2_row, self.route = gated, bias1, b2_row, route
                self.NH, self.R = len(cols), 2 if gated else 4
                self.sizes = CHUNKS[route.layer] * 2
                self.NC = len(self.sizes) // 2
                self.CH = 8 * self.NC
                ar = Area(at)
                self.rows = ar.f32(NT, D)
                self.hf = ar.f32(self.R, self.ROWS)
                self.hh = ar.f16(self.R, 2, self.ROWS)
                back = Area(at)
                self.yg = back.f32(2 * NT, D)
                ar.at = max(ar.at, back.at)
                self.xe = ar.f16(2, 2, KD, self.ROWS)
                self.xin = ar.f32(2, self.NQ, D)
                self.ysb = ar.f32(2, self.NQ, D)
                if before is None:
                    self.s_up = sem(name + "_up_full")
                    self.s_act = credit(name + "_act_done", self.CR)
                    self.s_hhi = sem(name + "_hi_ready")
                    self.s_h = credit(name + "_hidden_ready", self.CR)
                    self.s_hfree = credit(name + "_down_done", self.CR)
                    self.s_y = credit(name + "_y_copied", 1)
                    self.s_in = [sem(name + f"_rows_loaded_{c}") for c in range(2)]
                    self.s_tf = sem(name + "_rows_transposed")
                    self.s_th = sem(name + "_xe_hi")
                    self.s_tl = credit(name + "_xe_lo", 1)
                    self.s_st = [credit(name + f"_rows_stored_{c}", 16) for c in range(2)]
                    self.s_sc = sem(name + "_dispatched")
                    self.s_ga = [sem(name + f"_gathered_{c}") for c in range(2)]
                    self.units = self.chunks = self.tiles = self.runs = 0
                else:
                    self.s_up, self.s_act, self.s_hhi, self.s_h = \
                        before.s_up, before.s_act, before.s_hhi, before.s_h
                    self.s_hfree, self.s_y, self.s_in, self.s_tf = \
                        before.s_hfree, before.s_y, before.s_in, before.s_tf
                    self.s_th, self.s_tl, self.s_st, self.s_sc = \
                        before.s_th, before.s_tl, before.s_st, before.s_sc
                    self.s_ga = before.s_ga
                    self.units = before.units + before.CH * before.NH
                    self.chunks = before.chunks + before.CH
                    self.tiles = before.tiles + 4 * sum(before.sizes) // P
                    self.runs = before.runs + 1
                self.s_upfree = credit(name + "_gate_product_done", self.R) if gated else None

            def bank(self, j):
                return 2 * (j % 2) if self.gated else j % 4

            def walk(self, fori, eng):
                NC, NH = self.NC, self.NH

                def body(i, last):
                    for k in range(2 * NC):
                        nxt = (i, k + 1) if k + 1 < 2 * NC else (i + 1, 0)
                        fin = last and k == 2 * NC - 1
                        if k + 2 < 2 * NC or not last:
                            eng.load(*((i, k + 2) if k + 2 < 2 * NC else (i + 1, k + 2 - 2 * NC)))
                        for j in range(NH):
                            nx = j + self.LAG
                            if nx < NH:
                                eng.up(i, k, nx)
                            elif not fin:
                                if nx == NH and nxt[1] % NC == 0:
                                    eng.begin(*nxt)
                                eng.up(*nxt, nx - NH)
                            eng.down(i, k, j)
                            q = self.turn_at(j)
                            if q is not None and q < self.sizes[nxt[1]] // P and not fin:
                                eng.turn(*nxt, q)
                        if k % NC == NC - 1:
                            eng.end()
                eng.begin(0, 0)
                for k in range(2):
                    eng.load(0, k)
                for q in range(self.sizes[0] // P):
                    eng.turn(0, 0, q)
                for j in range(self.LAG):
                    eng.up(0, 0, j)
                with fori(0, 3) as i:
                    body(i, False)
                body(3, True)

            def turn_at(self, j):
                q = j // 2 if self.NH > 6 else j
                return q if (j % 2 == 0 or self.NH <= 6) and q < self.NQ else None

            def chunk(self, i, k):
                return 2 * self.NC * i + k

            def tile(self, i, k, q):
                return sum(self.sizes) // P * i + sum(self.sizes[:k]) // P + q + self.tiles

            def span(self, i, k):
                return bass.ds(sum(self.sizes) * i + sum(self.sizes[:k]), self.sizes[k])

            def unit(self, i, k, j):
                return self.NH * self.chunk(i, k) + j + self.units

            def in_slot(self, i, k):
                return self.NC * i + k // 2 + self.chunks // 2

            def expert(self, i, k):
                return 2 * i + k // self.NC

            def weights(self, k):
                return wsp[:, (self.job + k // self.NC) % 2]

        class DispatchedPE:
            def __init__(self, F):
                self.F = F

            def begin(self, i, k):
                pe.wait_ge(s_w, self.F.job + self.F.expert(i, k) + 1)

            def load(self, i, k):
                pass

            def turn(self, i, k, q):
                F = self.F
                tile = F.tile(i, k, q)
                if q == 0:
                    pe.wait_ge(F.s_in[k % 2], 16 * (F.in_slot(i, k) + 1))
                pe.wait_ge(F.s_tl, tile + 1)
                for d in range(KD):
                    m = pe.transpose(ps[:, 7, d * P:(d + 1) * P], F.xin[:, k % 2, q, d * P:(d + 1) * P], ident)
                m.then_inc(F.s_tf, 1)

            def up(self, i, k, j):
                F = self.F
                n, m, bk = F.unit(i, k, j), F.cols[j], F.bank(j)
                w = F.weights(k)
                if j == 0:
                    pe.wait_ge(F.s_tl, F.tile(i, k, F.sizes[k] // P) + 1)
                if F.gated:
                    pe.wait_ge(F.s_upfree, n - F.units + 1)
                else:
                    pe.wait_ge(F.s_act, n + 1 + F.CR - F.R)
                for g in range(2 if F.gated else 1):
                    for d in range(KD):
                        last = mm3(ps[0:m, bk + g, 0:F.sizes[k]], lambda h: F.up(w[:, h], g, d, j),
                                   lambda h: F.xe[:, k % 2, h, d, 0:F.sizes[k]], d == 0, d == KD - 1)
                last.then_inc(F.s_up, 1)

            def down(self, i, k, j):
                F = self.F
                m, w = F.cols[j], F.weights(k)
                if j == 0:
                    pe.wait_ge(F.s_y, F.chunk(i, k) + F.chunks + 1)
                pe.wait_ge(F.s_h, F.unit(i, k, j) + 1 + F.CR)
                for q in range(F.sizes[k] // P):
                    o = ps[:, 4 + q, 0:D]
                    last = mm3(o, lambda h: F.hh[0:m, j % F.R, h, q * P:(q + 1) * P],
                               lambda h: F.down(w[0:m, h], j), j == 0, j == F.NH - 1)
                    if j == 0 and F.b2_row is not None:
                        last = pe.matmul(o, ones[0:33, :], b2s[:, F.b2_row + F.expert(i, k), :], start=False, stop=False)
                last.then_inc(F.s_hfree, 1)

            def end(self):
                pe.drain().then_inc(s_wfree, 1)

        class DispatchedACT:
            def __init__(self, F):
                self.F = F

            def begin(self, i, k):
                F = self.F
                if F.bias1 is not None:
                    act.drain()
                    act.copy(b1e[:], b1c[:, bass.ds(F.bias1 + F.expert(i, k) * F.NH, F.NH)])
                    act.drain()

            def load(self, i, k):
                F = self.F
                n = F.chunk(i, k)
                if isinstance(n, int) and n < 2:
                    act.wait_ge(F.s_sc, 16 * 2 * NT * (F.runs + 1))
                else:
                    act.wait_ge(F.s_tf, F.tile(i, k, 0) - F.sizes[(k - 1) % (2 * F.NC)] // P)
                act.dma_start(F.xin[:, k % 2, 0:F.sizes[k] // P], xs[F.span(i, k)].rearrange("(q p) d -> p q d", p=P))\
                    .then_inc(F.s_in[k % 2], 16)

            def turn(self, i, k, q):
                F = self.F
                act.wait_ge(F.s_tf, F.tile(i, k, q) + 1)
                act.activation(F.xe[:, k % 2, 0, :, q * P:(q + 1) * P], shaped(ps[:, 7, 0:D], (KD, P)), ACT.Copy)\
                    .then_inc(F.s_th, 1)

            def up(self, i, k, j):
                F = self.F
                n, m, bk = F.unit(i, k, j), F.cols[j], F.bank(j)
                act.wait_ge(F.s_up, n + 1)
                act.wait_ge(F.s_h, n + 1 + F.CR - F.R)
                kw = {} if F.bias1 is None else {"bias": b1e[:, j:j + 1]}
                w = F.sizes[k]
                act.activation(F.hf[0:m, j % F.R, 0:w], ps[0:m, bk, 0:w], F.fn, scale=INV, **kw).then_inc(F.s_act, 1)

            def down(self, i, k, j):
                F = self.F
                n = F.chunk(i, k)
                if j == F.NH - 1:
                    act.wait_ge(F.s_y, n + F.chunks + 2)
                    act.dma_start(ys[F.span(i, k)].rearrange("(q p) d -> p q d", p=P), F.ysb[:, k % 2, 0:F.sizes[k] // P])\
                        .then_inc(F.s_st[k % 2], 16)

            def end(self):
                pass

        class DispatchedDVE:
            def __init__(self, F):
                self.F = F

            def begin(self, i, k):
                pass

            def load(self, i, k):
                pass

            def turn(self, i, k, q):
                F = self.F
                dve.wait_ge(F.s_th, F.tile(i, k, q) + 1)
                dve.tensor_tensor(F.xe[:, k % 2, 1, :, q * P:(q + 1) * P], shaped(ps[:, 7, 0:D], (KD, P)),
                                  F.xe[:, k % 2, 0, :, q * P:(q + 1) * P], ALU.subtract).then_inc(F.s_tl, 1)

            def up(self, i, k, j):
                F = self.F
                n, m, r, w = F.unit(i, k, j), F.cols[j], j % F.R, F.sizes[k]
                hf = F.hf[0:m, r, 0:w]
                dve.wait_ge(F.s_act, n + 1 + F.CR)
                if F.gated:
                    dve.scalar_tensor_tensor(hf, ps[0:m, F.bank(j) + 1, 0:w], INV, hf, ALU.mult, ALU.mult)\
                        .then_inc(F.s_upfree, 1)
                    dve.wait_ge(F.s_upfree, n - F.units + 1 + F.R)
                dve.wait_ge(F.s_hfree, n + 1 + F.CR - F.R)
                dve.tensor_copy(F.hh[0:m, r, 0, 0:w], hf).then_inc(F.s_hhi, 1)
                dve.wait_ge(F.s_hhi, n + 1)
                dve.tensor_tensor(F.hh[0:m, r, 1, 0:w], hf, F.hh[0:m, r, 0, 0:w], ALU.subtract).then_inc(F.s_h, 1)

            def down(self, i, k, j):
                F = self.F
                if j == F.NH - 1:
                    dve.wait_ge(F.s_hfree, F.unit(i, k, j) + 1 + F.CR)
                    dve.wait_ge(F.s_st[k % 2], 16 * F.in_slot(i, k) + 16)
                    nq = F.sizes[k] // P
                    dve.tensor_copy(F.ysb[:, k % 2, 0:nq], ps[:, 4:4 + nq, 0:D]).then_inc(F.s_y, 1)

            def end(self):
                pass

            def combine(self):
                F = self.F
                for half in range(2):
                    dve.wait_ge(F.s_ga[half], 16 * NT * (F.runs + 1))
                    for k in range(2):
                        for t in range(half * NT // 2, (half + 1) * NT // 2):
                            dve.scalar_tensor_tensor(x[:, t, :], F.yg[:, 2 * t + k, :], F.route.w2[:, t, k:k + 1], x[:, t, :],
                                                     ALU.mult, ALU.add)
                        dve.drain()

        class DispatchedPool:
            def __init__(self, F, pool):
                self.F, self.pool = F, pool

            def if_fits(self, body):
                F, pool = self.F, self.pool
                if F.route.layer == 0:
                    return body()
                pool.wait_ge(F.route.s_ix, F.route.layer + 1)
                with pool.If(fits_of(pool, F.route.layer)):
                    body()

            def scatter(self):
                F, pool = self.F, self.pool
                pool.wait_ge(F.route.s_ix, F.route.layer + 1)
                pool.wait_ge(s_xz, 16)
                to = F.route.to.rearrange("p t k -> p (t k)")
                for n in range(2 * NT):
                    pool.indirect_dma_start(xs, bass.IndirectOffsetOnAxis(ap=to[:, n:n + 1], axis=0),
                                            F.rows[:, n // 2, :], None).then_inc(F.s_sc, 16)

            def gather(self):
                F, pool = self.F, self.pool
                for c in range(2):
                    pool.wait_ge(F.s_st[c], 16 * (1 + (F.chunks + F.CH) // 2))
                fro = F.route.fro.rearrange("p t k -> p (t k)")
                for n in range(2 * NT):
                    pool.indirect_dma_start(F.yg[:, n, :], None, ys[0:8 * F.route.cap],
                                            bass.IndirectOffsetOnAxis(ap=fro[:, n:n + 1], axis=0))\
                        .then_inc(F.s_ga[n // NT], 16)

        def fits_of(eng, layer):
            return eng.value_load(fits[0:1, layer:layer + 1], min_val=0, max_val=1)

        class Attn:
            def __init__(self, name, jobq, jobk, inner, dh, layer, merged):
                self.name, self.jobq, self.jobk = name, jobq, jobk
                self.inner, self.dh, self.layer, self.merged = inner, dh, layer, merged
                self.NC = inner // P
                self.hpc = P // dh
                self.H = inner // dh
                self.scale = dh ** -0.5
                ar = Area()
                self.q = ar.f16(2, self.NC, S)
                self.o = ar.f16(2, self.NC, S)
                if merged:
                    self.k = ar.f16(2, self.NC, GA)
                    self.v = ar.f16(2, 5, inner)
                    self.pr = ar.f32(2, 2, GA)
                    self.pT = ar.f16(2, 2, 5, S)
                    self.G = self.H
                    self.tuses = 3
                    self.kc = [P] * 4 + [GA - 4 * P]
                else:
                    self.k = ar.f16(2, self.NC, 2 * G)
                    self.v = ar.f16(2, inner)
                    self.pr = ar.f32(2, 2, 4, G)
                    self.pT = ar.f16(2, 2, 4, S)
                    self.G = self.NC // 2
                    self.tuses = 2
                self.mx = ar.f32(2, 2, 4)
                self.sm = ar.f32(2, 2, 4)
                n = name
                self.s_pf = sem(n + "_proj_full")
                self.s_ph = sem(n + "_proj_hi")
                self.s_pfree = credit(n + "_proj_free", 2)
                self.s_sf = sem(n + "_scores_full")
                self.car, self.cex = (0, 2) if merged else (4, 0)
                self.s_ar = sem(n + "_exp_arg") if merged else credit(n + "_exp_arg", 4)
                self.s_ex = credit(n + "_exp_done", 2) if merged else sem(n + "_exp_done")
                self.s_p = sem(n + "_probs_ready")
                self.s_tf = sem(n + "_trans_full")
                self.s_th = sem(n + "_trans_hi")
                self.s_tfree = credit(n + "_trans_free", 2)
                self.s_z = sem(n + "_zero_ready")
                self.plan()

            def events(self, T):
                G_, last = self.G, B * self.G
                b, g = divmod(T, G_)
                ev = []
                if 0 <= T - 1 < last and self.merged:
                    ev.append(("norm",) + divmod(T - 1, G_))
                if T < last:
                    ev.append(("scores", b, g))
                if 0 <= T - 1 < last and self.merged:
                    ev.append(("trans",) + divmod(T - 1, G_))
                if T >= 3 and T % G_ == 2 % G_:
                    ev += [("out", (T - 3) // G_, 0), ("out", (T - 3) // G_, 1)]
                if 0 <= T - 2 < last:
                    pb, pg = divmod(T - 2, G_)
                    ev.append(("pvhalf" if self.merged and pg % 2 == 0 else "pv", pb, pg))
                    if not self.merged and pg % 2 == 1 and pb + 1 < B:
                        ev.append(("v", pb + 1, pg // 2))
                if 0 <= T - 1 < last and not self.merged:
                    ev.append(("norm",) + divmod(T - 1, G_))
                if T < last and b + 1 < B:
                    if not self.merged:
                        ev.append(("q", b + 1, g))
                        if g % 2 == 1:
                            ev.append(("k", b + 1, g // 2))
                    elif g % 2 == 1:
                        ev.append(("q", b + 1, g // 2))
                if 0 <= T - 1 < last:
                    if not self.merged:
                        ev.append(("trans",) + divmod(T - 1, G_))
                    ev.append(("trans_end",) + divmod(T - 1, G_))
                return ev

            def plan(self):
                G_ = self.G
                if self.merged:
                    self.first = [("kv", 0, e) for e in range(2 * self.NC + 10)]
                else:
                    self.first = [("k", 0, e) for e in range(self.NC // 4)] + \
                                 [("v", 0, e) for e in range(self.inner // 512)]
                self.first += [("q", 0, e) for e in range(self.NC // 2)]
                self.tail = [e for T in range(B * G_, B * G_ + 3) for e in self.events(T)]
                bodies = [[e for T in range(b * G_, (b + 1) * G_) for e in self.events(T)] for b in range(B)]
                rel = [[(k, b - n, g) for k, b, g in body] for n, body in enumerate(bodies)]
                self.bodies = bodies
                self.h = next(h for h in range(B) if rel[h] == rel[B - 2])
                assert all(r == rel[self.h] for r in rel[self.h:B - 1])
                self.use, self.high = {}, {}
                for k, b, g in self.first + [e for x_ in bodies for e in x_] + self.tail:
                    if k in ("kv", "k", "v", "q", "out") or k == "pvhalf" or (k == "pv" and not self.merged):
                        key = (k, b, g) if k != "pvhalf" else ("pv", b, g + 1)
                        self.use[key] = len(self.use)
                        if k != "out":
                            self.high[key] = len(self.high)
                self.su = self.use["pv", 3, 1] - self.use["pv", 2, 1]
                self.sh = self.high["pv", 3, 1] - self.high["pv", 2, 1]
                assert self.su % 2 == 0

            def walk(self, fori, eng):
                for e in self.first:
                    eng.event(*e, 0)
                for body in self.bodies[:self.h]:
                    for e in body:
                        eng.event(*e, 0)
                with fori(0, B - 1 - self.h) as i:
                    for e in self.bodies[self.h]:
                        eng.event(*e, i)
                for e in self.bodies[B - 1] + self.tail:
                    eng.event(*e, 0)

            def parts(self, k):
                return range(self.tuses - 1) if k == "trans" else range(self.tuses - 1, self.tuses)

            def u(self, key, i):
                return self.use[key] + self.su * i

            def bank67(self, key):
                return 6 + self.use[key] % 2

            def entry(self, k, b, e, i):
                if k == "q":
                    return self.q_entries(b + i)[e]
                kv = self.kv_entries(b + i)
                return kv[e] if k in ("kv", "k") else kv[self.NC // 4 + e]

            def wq(self, h, k, c):
                w = wsp[:, self.jobq % 2, h]
                return w[:, k * self.inner + c * P:k * self.inner + (c + 1) * P]

            def wo(self, h, c):
                at = KD * self.inner + c * D
                return wsp[:, self.jobq % 2, h, at:at + D]

            def koff(self):
                return 2048 if self.jobk == self.jobq else 0

            def wk(self, h, k, c):
                at = self.koff() + k * self.inner + c * P
                return wsp[0:CP, self.jobk % 2, h, at:at + P]

            def wv(self, h, k, c0, n):
                at = self.koff() + KC * self.inner + k * self.inner + c0
                return wsp[0:CP, self.jobk % 2, h, at:at + n]

            def kv_entries(self, i):
                r = []
                if self.merged:
                    for c in range(self.NC):
                        for half in range(2):
                            n0 = half * (GA // 2)

                            def fill(bk, c=c, n0=n0):
                                for k in range(KC):
                                    m = mm3(ps[:, bk, 0:GA // 2], lambda h: self.wk(h, k, c),
                                            lambda h: ctxs[:, h, k, n0:n0 + GA // 2], k == 0, k == KC - 1)
                                return m
                            r.append((fill, [(lambda bk: ps[:, bk, 0:GA // 2],
                                              lambda h, c=c, n0=n0: self.k[:, h, c, n0:n0 + GA // 2], INV)]))
                    for kc, rows in enumerate(self.kc):
                        for half in range(2):
                            def fill(bk, kc=kc, rows=rows, half=half):
                                for k in range(KC):
                                    m = mm3(ps[0:rows, bk, :], lambda h: ctxs[:, h, k, kc * P:kc * P + rows],
                                            lambda h: self.wv(h, k, half * 512, 512), k == 0, k == KC - 1)
                                return m
                            r.append((fill, [(lambda bk, rows=rows: ps[0:rows, bk, :],
                                              lambda h, kc=kc, rows=rows, half=half:
                                              self.v[0:rows, h, kc, half * 512:(half + 1) * 512], INV)]))
                    return r
                for c0 in range(0, self.NC, 4):
                    def fill(bk, c0=c0):
                        for c in range(4):
                            for k in range(KC):
                                m = mm3(ps[:, bk, c * G:(c + 1) * G], lambda h: self.wk(h, k, c0 + c),
                                        lambda h: ctxs[:, h, k, bass.ds(i * G, G)], k == 0, k == KC - 1)
                        return m
                    dr = []
                    for b in range(self.hpc):
                        r0 = b * self.dh
                        dr.append((lambda bk, r0=r0: ps[r0:r0 + self.dh, bk, 0:4 * G].rearrange("p (c g) -> p c g", c=4),
                                   lambda h, r0=r0, b=b, c0=c0: self.k[r0:r0 + self.dh, h, c0:c0 + 4, b * G:(b + 1) * G], INV))
                    r.append((fill, dr))
                for half in range(self.inner // 512):
                    def fill(bk, half=half):
                        for k in range(KC):
                            m = mm3(ps[0:G, bk, :], lambda h: ctxs[:, h, k, bass.ds(i * G, G)],
                                    lambda h: self.wv(h, k, half * 512, 512), k == 0, k == KC - 1)
                        return m
                    r.append((fill, [(lambda bk: ps[0:G, bk, :],
                                      lambda h, half=half: self.v[0:G, h, half * 512:(half + 1) * 512], INV)]))
                return r

            def q_entries(self, i):
                r = []
                for c0 in range(0, self.NC, 2):
                    def fill(bk, c0=c0):
                        for c in range(2):
                            for k in range(KD):
                                m = mm3(ps[:, bk, c * S:(c + 1) * S], lambda h: self.wq(h, k, c0 + c),
                                        lambda h: xT[:, h, k, bass.ds(i * S, S)], k == 0, k == KD - 1)
                        return m
                    r.append((fill, [(lambda bk: ps[:, bk, :],
                                      lambda h, c0=c0: self.q[:, h, c0:c0 + 2, :].rearrange("p c n -> p (c n)"), INV)]))
                return r

        class AttnPE:
            def __init__(self, A):
                self.A = A

            def event(self, k, b, g, i):
                A = self.A
                T = b * A.G + g + i * A.G
                if k in ("kv", "k", "v", "q"):
                    pe.wait_ge(A.s_pfree, A.u((k, b, g), i) + 1)
                    A.entry(k, b, g, i)[0](A.bank67((k, b, g))).then_inc(A.s_pf, 1)
                elif k == "scores":
                    need = A.use["q", b, g // 2 if A.merged else g]
                    if not A.merged:
                        need = max(need, A.use["k", b, g // 2])
                    pe.wait_ge(A.s_pfree, need + A.su * i + 3)
                    self.scores(T, g)
                elif k in ("trans", "trans_end"):
                    self.trans(T, g, A.parts(k))
                elif k in ("pvhalf", "pv"):
                    key = ("pv", b, g + (k == "pvhalf"))
                    pe.wait_ge(A.s_tfree, (T + 1) * A.tuses + 2)
                    if k == "pvhalf" or not A.merged:
                        pe.wait_ge(A.s_pfree, A.u(key, i) + 1)
                    if not A.merged and g % 2 == 0:
                        pe.wait_ge(A.s_pfree, A.u(("v", b, g // 2), i) + 3)
                    self.pv(g, A.bank67(key), k)
                elif k == "out":
                    key = ("out", b, g)
                    pe.wait_ge(A.s_pfree, A.u(key, i) + 1)
                    if g == 0:
                        pe.wait_ge(A.s_pfree, A.u(("pv", b, A.G - 1), i) + 3)
                    for c in range(A.NC):
                        m = mm3(ps[:, A.bank67(key), 0:D], lambda h: A.o[:, h, c, g * P:(g + 1) * P],
                                lambda h: A.wo(h, c), c == 0, c == A.NC - 1)
                    m.then_inc(A.s_pf, 1)

            def scores(self, T, g):
                A = self.A
                for t in range(2):
                    pe.wait_ge(A.s_ex if A.merged else A.s_ar, 2 * T + t + 1)
                    if A.merged:
                        for half in range(2):
                            n0 = half * (GA // 2)
                            m = mm3(ps[:, 2 * t + half, 0:GA // 2],
                                    lambda h: A.q[:, h, g, t * P:(t + 1) * P],
                                    lambda h: A.k[:, h, g, n0:n0 + GA // 2], True, True)
                    else:
                        for c in range(2):
                            m = mm3(ps[:, 2 * (g % 2) + t, c * 2 * G:(c + 1) * 2 * G],
                                    lambda h: A.q[:, h, 2 * g + c, t * P:(t + 1) * P],
                                    lambda h: A.k[:, h, 2 * g + c, :], True, True)
                    m.then_inc(A.s_sf, 1)

            def trans(self, T, g, parts):
                A = self.A
                if 0 in parts:
                    pe.wait_ge(A.s_p, 2 * T + 2)
                for tu in parts:
                    pe.wait_ge(A.s_tfree, T * A.tuses + tu + 1)
                    bk = 4 + A.tbank(g, tu)
                    if A.merged:
                        for kc in range(2 * tu, min(2 * tu + 2, 5)):
                            rows = A.kc[kc]
                            for t in range(2):
                                at = (kc % 2) * S + t * P
                                m = pe.transpose(ps[0:rows, bk, at:at + P], A.pr[:, g % 2, t, kc * P:kc * P + rows], ident)
                    else:
                        for hd in range(2 * tu, 2 * tu + 2):
                            for t in range(2):
                                at = (hd % 2) * S + t * P
                                m = pe.transpose(ps[0:G, bk, at:at + P], A.pr[:, g % 2, t, hd, :], ident)
                    m.then_inc(A.s_tf, 1)

            def pv(self, g, bk, k):
                A = self.A
                if A.merged:
                    at = 0 if k == "pvhalf" else S
                    for kc in range(5):
                        rows = A.kc[kc]
                        m = mm3(ps[:, bk, at:at + S], lambda h: A.v[0:rows, h, kc, g * P:(g + 1) * P],
                                lambda h: A.pT[0:rows, g % 2, h, kc, :], kc == 0, kc == 4)
                else:
                    for c in range(2):
                        for b in range(2):
                            hd = 2 * c + b
                            col = (4 * g + hd) * A.dh
                            m = mm3(ps[b * 64:(b + 1) * 64, bk, c * S:(c + 1) * S],
                                    lambda h: A.v[0:G, h, col:col + A.dh],
                                    lambda h: A.pT[0:G, g % 2, h, hd, :], True, True)
                if k == "pv":
                    m.then_inc(A.s_pf, 1)

        class AttnACT:
            def __init__(self, A):
                self.A = A

            def event(self, k, b, g, i):
                A = self.A
                T = b * A.G + g + i * A.G
                if k in ("kv", "k", "v", "q", "pv"):
                    key = (k, b, g)
                    act.wait_ge(A.s_pf, A.u(key, i) + 1)
                    for view, dst, scale in A.entry(k, b, g, i)[1] if k != "pv" else [A.odrain(g)]:
                        m = act.activation(dst(0), view(A.bank67(key)), ACT.Copy, scale=scale)
                    m.then_inc(A.s_ph, 1)
                elif k == "scores":
                    for t in range(2):
                        act.wait_ge(A.s_ar, 2 * T + t + 1 + A.car)
                        if A.merged:
                            act.activation(A.pr[:, g % 2, t, :].rearrange("p (a n) -> p a n", a=2),
                                           ps[:, 2 * t:2 * t + 2, 0:GA // 2], ACT.Exp,
                                           scale=1.5 * A.scale, bias=A.mx[:, g % 2, t, 1:2],
                                           accum_out=A.sm[:, g % 2, t, 0:1])
                            act.drain().then_inc(A.s_ex, 1)
                        else:
                            v = A.pr[:, g % 2, t, :, :]
                            act.activation(v, v, ACT.Exp, scale=A.scale).then_inc(A.s_ex, 1)
                elif k in ("trans", "trans_end"):
                    for tu in A.parts(k):
                        act.wait_ge(A.s_tf, T * A.tuses + tu + 1)
                        bk = 4 + A.tbank(g, tu)
                        act.activation(A.tdst(g, tu, 0), A.tsrc(bk, tu), ACT.Copy).then_inc(A.s_th, 1)

        class AttnDVE:
            def __init__(self, A):
                self.A = A

            def event(self, k, b, g, i):
                A = self.A
                T = b * A.G + g + i * A.G
                if k in ("kv", "k", "v", "q", "pv"):
                    key = (k, b, g)
                    dve.wait_ge(A.s_ph, A.high[key] + A.sh * i + 1)
                    for view, dst, scale in A.entry(k, b, g, i)[1] if k != "pv" else [A.odrain(g)]:
                        m = dve.scalar_tensor_tensor(dst(1), view(A.bank67(key)), scale, dst(0), ALU.mult, ALU.subtract)
                    m.then_inc(A.s_pfree, 1)
                elif k == "norm":
                    self.norm(T, g % 2)
                elif k == "scores":
                    self.maxima(T, g, g % 2)
                elif k in ("trans", "trans_end"):
                    for tu in A.parts(k):
                        dve.wait_ge(A.s_th, T * A.tuses + tu + 1)
                        bk = 4 + A.tbank(g, tu)
                        dve.tensor_tensor(A.tdst(g, tu, 1), A.tsrc(bk, tu), A.tdst(g, tu, 0), ALU.subtract)\
                            .then_inc(A.s_tfree, 1)
                elif k == "out":
                    dve.wait_ge(A.s_pf, A.u((k, b, g), i) + 1)
                    xo = x[:, 2 * (b + i) + g, :]
                    dve.scalar_tensor_tensor(xo, ps[:, A.bank67((k, b, g)), 0:D], sm[:, 4, 0:1], xo, ALU.mult, ALU.add)\
                        .then_inc(A.s_pfree, 1)

            def maxima(self, T, g, r):
                A = self.A
                for t in range(2):
                    dve.wait_ge(A.s_sf, 2 * T + t + 1)
                    if A.merged:
                        src = ps[:, 2 * t:2 * t + 2, 0:GA // 2]
                        dve.tensor_reduce(A.mx[:, r, t, 0:1], src, mybir.AxisListType.XY, ALU.max)
                    else:
                        src = ps[:, 2 * (g % 2) + t, 0:4 * G].rearrange("p (h k) -> p h k", h=4)
                        dve.tensor_reduce(A.mx[:, r, t, :], src, X, ALU.max)
                    dve.drain()
                    if A.merged:
                        dve.tensor_scalar(A.mx[:, r, t, 1:2], A.mx[:, r, t, 0:1], -1.5 * A.scale, None, ALU.mult)\
                            .then_inc(A.s_ar, 1)
                    else:
                        dve.tensor_tensor(A.pr[:, r, t, :, :], src,
                                          A.mx[:, r, t, :].unsqueeze(2).to_broadcast([P, 4, G]), ALU.subtract)\
                            .then_inc(A.s_ar, 1)

            def norm(self, T, r):
                A = self.A
                n = 2 * T + 2 + A.cex
                dve.wait_ge(A.s_ex, n)
                if A.merged:
                    dve.reciprocal(A.sm[:, r, :, 1:2], A.sm[:, r, :, 0:1])
                    dve.drain()
                    for t in range(2):
                        dve.tensor_scalar(A.pr[:, r, t, :], A.pr[:, r, t, :], A.sm[:, r, t, 1:2], None, ALU.mult)\
                            .then_inc(A.s_p, 1)
                else:
                    dve.tensor_reduce(A.sm[:, r, :, :], A.pr[:, r, :, :, :], X, ALU.add)
                    dve.drain()
                    dve.reciprocal(A.sm[:, r, :, :], A.sm[:, r, :, :])
                    dve.drain()
                    dve.tensor_tensor(A.pr[:, r].rearrange("p t h k -> p (t h) k"), A.pr[:, r].rearrange("p t h k -> p (t h) k"),
                                      A.sm[:, r].rearrange("p t h -> p (t h)").unsqueeze(2).to_broadcast([P, 8, G]),
                                      ALU.mult).then_inc(A.s_p, 2)

        def tbank(A):
            return lambda g, tu: (g * A.tuses + tu) % 2

        def tdst(A):
            def f(g, tu, h):
                if A.merged:
                    if tu == 2:
                        return A.pT[0:A.kc[4], g % 2, h, 4, :]
                    return A.pT[:, g % 2, h, 2 * tu:2 * tu + 2, :].rearrange("p c n -> p (c n)")
                return A.pT[0:G, g % 2, h, 2 * tu:2 * tu + 2, :].rearrange("p c n -> p (c n)")
            return f

        def tsrc(A):
            def f(bk, tu):
                if A.merged:
                    return ps[0:A.kc[4], bk, 0:S] if tu == 2 else ps[:, bk, :]
                return ps[0:G, bk, :]
            return f

        def odrain(A):
            def f(g):
                c0 = g - 1 if A.merged else 2 * g
                return (lambda bk: ps[:, bk, :],
                        lambda h: A.o[:, h, c0:c0 + 2, :].rearrange("p c n -> p (c n)"), 1.0)
            return f

        def attn_stage(A, stage):
            A.tbank, A.tdst, A.tsrc, A.odrain = tbank(A), tdst(A), tsrc(A), odrain(A)

            def pe_part():
                for j in sorted({A.jobq, A.jobk}):
                    pe.wait_ge(s_w, j + 1)
                if not A.merged:
                    pe.wait_ge(A.s_z, 1)
                A.walk(pe.Fori, AttnPE(A))
                pe.drain().then_inc(s_wfree, len({A.jobq, A.jobk}))
                barrier(pe, 0, stage)

            def act_part():
                if not A.merged:
                    act.wait_ge(A.s_z, 1)
                A.walk(act.Fori, AttnACT(A))
                barrier(act, 1, stage)

            def dve_part():
                if not A.merged:
                    dve.memset(A.k[:, :, :, :].rearrange("p h c n -> p (h c n)"), 0.0)
                dve.tensor_scalar(sm[:, 4, 0:1], tg[:, A.layer:A.layer + 1], INV, None, ALU.mult)
                dve.tensor_scalar(brow[:, A.layer - 1, :], brow[:, A.layer - 1, :], tg[:, A.layer:A.layer + 1], None, ALU.mult)
                dve.drain().then_inc(A.s_z, 1)
                with dve.Fori(0, NT) as t:
                    dve.tensor_tensor(x[:, t, :], x[:, t, :], brow[:, A.layer - 1, :], ALU.add)
                dve.drain()
                A.walk(dve.Fori, AttnDVE(A))
                barrier(dve, 2, stage)
            prog["pe"].append(pe_part)
            prog["act"].append(act_part)
            prog["dve"].append(dve_part)

        def small(n):
            return xT[:].rearrange("p a b c -> p (a b c)")[:, 2 * D * n:2 * D * (n + 1)].bitcast(F32)

        ARE, AIM, CRE, CIM, LDT = (small(n) for n in range(5))
        DT, IMC, T1, T2, T3, DCR, DCI, RE, T4, T5, T6 = (small(n) for n in range(5, 16))

        class KGen:
            def __init__(self):
                ar = Area()
                self.y = ar.f32(D, 16)
                self.e1 = ar.f32(D, 16)
                self.e2 = ar.f32(D, 16)
                self.v = ar.f32(D, 16)
                self.w = ar.f32(D, 16)
                self.kk = self.v[:, 0:32, :]
                self.kp = shaped(self.w.rearrange("p a b -> p (a b)")[:, 0:512].bitcast(F16), (32, 16, 2))
                self.zero = self.w.rearrange("p a b -> p (a b)")[:, 1024:1280].bitcast(F16)
                self.s_d = sem("kgen_dve")
                self.s_a = sem("kgen_act")
                self.s_t = sem("kgen_tables_ready")
                self.s_k = sem("kgen_sums_ready")
                self.s_st = sem("kgen_rows_ready")
                self.s_kd = sem("kernel_in_dram")

            ACTS = [("T1", "T1", "tanh", 1.0 / 16), ("T1", "T1", "tanh", 0.5), ("T2", "T2", "sin", 0),
                    ("T3", "T3", "sin", 0)]

            def act_part(self):
                n = [0]

                def step(dst, src, fn, **kw):
                    n[0] += 1
                    act.wait_ge(self.s_d, n[0])
                    act.activation(dst, src, fn, **kw)
                    act.drain().then_inc(self.s_a, 1)

                act.wait_ge(s_const, N_CONST)
                act.activation(tg[:], sc[:, 0:8], ACT.Tanh)
                step(T1, LDT, ACT.Tanh, scale=1.0 / 16)
                step(T1, RE, ACT.Tanh, scale=0.5)
                step(T2, T2, ACT.Sin, scale=SIN_SCALE)
                step(T3, T3, ACT.Sin, scale=SIN_SCALE)
                step(self.v, self.v, ACT.Sin, scale=SIN_SCALE, bias=cst[:, C_PHR:C_PHR + 1])
                step(self.w, self.w, ACT.Exp)
                step(self.v, self.v, ACT.Sin, scale=SIN_SCALE, bias=cst[:, C_PHR + 1:C_PHR + 2])
                step(self.w, self.w, ACT.Sin, scale=SIN_SCALE, bias=cst[:, C_PHR + 2:C_PHR + 3])
                step(self.w, self.w, ACT.Exp)

            def dve_part(self):
                n = [0]

                def tt(o, a_, b_, op):
                    dve.tensor_tensor(o, a_, b_, op)
                    dve.drain()

                def ts(o, a_, s1, s2, op0, op1):
                    dve.tensor_scalar(o, a_, s1, s2, op0, op1) if s2 is not None else dve.tensor_scalar(o, a_, s1, None, op0)
                    dve.drain()

                def ask(count=1):
                    dve.drain().then_inc(self.s_d, count)
                    n[0] += count
                    dve.wait_ge(self.s_a, n[0])

                def wrap(dst, y, ph):
                    ts(dst, y, ph, ROUND, ALU.add, ALU.add)
                    dve.scalar_tensor_tensor(dst, dst, ROUND, y, ALU.subtract, ALU.subtract)
                    dve.drain()

                dve.wait_ge(s_const, N_CONST)
                ask()
                ts(T2, T1, -1.0, 1.0, ALU.mult, ALU.add)
                ts(T3, T1, 1.0, None, ALU.add, None)
                dve.reciprocal(T2, T2)
                dve.drain()
                tt(T2, T2, T3, ALU.mult)
                for _ in range(3):
                    tt(T2, T2, T2, ALU.mult)
                tt(RE, T2, ARE, ALU.mult)
                tt(IMC, T2, AIM, ALU.mult)
                ts(IMC, IMC, 1.0 / TWO_PI, None, ALU.mult, None)
                ask()
                ts(T2, IMC, 0.5, None, ALU.mult, None)
                wrap(T4, T2, 0.0)
                wrap(T3, IMC, 0.0)
                dve.tensor_copy(T2, T4)
                ask(2)
                ts(T4, T1, -1.0, 1.0, ALU.mult, ALU.add)
                dve.reciprocal(T4, T4)
                dve.drain()
                tt(T1, T1, T4, ALU.mult)
                ts(T1, T1, 2.0, None, ALU.mult, None)
                tt(T2, T2, T2, ALU.mult)
                ts(T2, T2, 2.0, None, ALU.mult, None)
                ts(T4, T2, -1.0, 1.0, ALU.mult, ALU.add)
                tt(T4, T4, T1, ALU.mult)
                tt(T4, T4, T2, ALU.subtract)
                dve.scalar_tensor_tensor(T5, T1, 1.0, T3, ALU.add, ALU.mult)
                dve.drain()
                tt(T1, ARE, ARE, ALU.mult)
                tt(T2, AIM, AIM, ALU.mult)
                tt(T1, T1, T2, ALU.add)
                dve.reciprocal(T1, T1)
                dve.drain()
                ts(T1, T1, 2.0, None, ALU.mult, None)
                tt(T2, T4, ARE, ALU.mult)
                tt(T3, T5, AIM, ALU.mult)
                tt(T2, T2, T3, ALU.add)
                tt(T2, T2, T1, ALU.mult)
                tt(T3, T5, ARE, ALU.mult)
                tt(T6, T4, AIM, ALU.mult)
                tt(T3, T3, T6, ALU.subtract)
                tt(T3, T3, T1, ALU.mult)
                tt(DCR, CRE, T2, ALU.mult)
                tt(T6, CIM, T3, ALU.mult)
                tt(DCR, DCR, T6, ALU.subtract)
                tt(DCI, CRE, T3, ALU.mult)
                tt(T6, CIM, T2, ALU.mult)
                tt(DCI, DCI, T6, ALU.add)

                def over_k(o, v, at):
                    tt(o, v.unsqueeze(2).to_broadcast([P, D, 16]), bcast(cst[:, at:at + 16], D), ALU.mult)

                over_k(self.y, IMC, C_IOTA)
                wrap(self.v, self.y, cst[:, C_PH:C_PH + 1])
                over_k(self.w, RE, C_IOTA)
                ask(2)
                tt(self.e1, self.v, self.w, ALU.mult)
                over_k(self.y, IMC, C_K16)
                wrap(self.v, self.y, cst[:, C_PH + 1:C_PH + 2])
                wrap(self.w, self.y, cst[:, C_PH + 2:C_PH + 3])
                ask(2)
                tt(self.v, self.v, DCR.unsqueeze(2).to_broadcast([P, D, 16]), ALU.mult)
                tt(self.w, self.w, DCI.unsqueeze(2).to_broadcast([P, D, 16]), ALU.mult)
                tt(self.v, self.v, self.w, ALU.add)
                over_k(self.w, RE, C_K16)
                ask()
                dve.tensor_tensor(self.e2, self.v, self.w, ALU.mult)
                dve.drain().then_inc(self.s_t, 1)
                for bk in range(8):
                    dve.wait_ge(self.s_k, bk + 1)
                    m = self.y.rearrange("p a b -> p (a b)")[:, 512 * (bk % 4):512 * (bk % 4 + 1)]
                    m4 = shaped(m, (4, 8, 16))
                    mask = cst[:, C_MASK:C_MASK + 8].unsqueeze(1).unsqueeze(3).to_broadcast([P, 4, 8, 16])
                    dve.tensor_tensor(m4, shaped(ps[:, bk, :], (4, 8, 16)), mask, ALU.mult)
                    dve.drain()
                    dve.tensor_reduce(self.kk[:, 4 * bk:4 * bk + 4, :], m4.rearrange("p g d b -> p g b d"), X, ALU.add)
                dve.memset(self.zero, 0.0)
                dve.drain()
                dve.tensor_tensor(self.kk[:, :, 0], self.kk[:, :, 0], dsk[:], ALU.add)
                dve.drain()
                dve.tensor_copy(self.kp[:, :, :, 0], self.kk)
                dve.drain()
                dve.tensor_tensor(self.kp[:, :, :, 1], self.kk, self.kp[:, :, :, 0], ALU.subtract)
                dve.drain().then_inc(self.s_st, 1)

            def pe_part(self):
                pe.wait_ge(self.s_t, 1)
                for g in range(D // 8):
                    l = self.e2[:, 8 * g:8 * g + 8, :].rearrange("p d a -> p (d a)")
                    r = self.e1[:, 8 * g:8 * g + 8, :].rearrange("p d a -> p (d a)")
                    m = pe.matmul(ps[:, g // 4, (g % 4) * P:(g % 4 + 1) * P], l, r, start=True, stop=True)
                    if g % 4 == 3:
                        m.then_inc(self.s_k, 1)

            def store(self, sp):
                sp.wait_ge(self.s_st, 1)
                for half in range(2):
                    sp.dma_start(kdram[half * P:(half + 1) * P, 0:127, :].rearrange("d j c -> d (j c)"),
                                 self.zero[:, 0:254]).then_inc(self.s_kd, 16)
                for e in range(8):
                    sp.dma_start(kdram[:, 127:127 + S, :].rearrange("(g e) (a b) c -> e a g (b c)", e=8, b=16)[e],
                                 self.kp[16 * e:16 * e + 16].rearrange("p g b c -> p g (b c)")).then_inc(self.s_kd, 16)
                sp.dma_start(xs[0:SLOTS].rearrange("(p n) d -> p n d", p=P),
                             self.zero.bitcast(F32).unsqueeze(1).to_broadcast([P, SLOTS // P, D])).then_inc(s_xz, 16)
                sp.wait_ge(self.s_kd, 160)

        L0 = Area()
        xtext = L0.f32(NT, D)
        u = L0.f16(2, NT, D)
        ystart = L0.at
        y = L0.f32(NT, D)
        rows = L0.f32(NROW)
        TG, TR = 4, 4
        tz = L0.f16(TR, TG, S, 2)
        H0, DH0, KTOP = 4, 32, 32

        def row(n, w=D):
            return rows[:, n * D:n * D + w]

        class Attn0:
            def __init__(self):
                ar = Area(ystart)
                self.q = ar.f16(2, S)
                self.k = ar.f16(2, H0 * G)
                self.v = ar.f16(2, D)
                self.s = ar.f32(2, H0, G)
                self.w = ar.f32(2, H0, G)
                self.m1 = ar.f32(2, H0, 8)
                self.m2 = ar.f32(2, H0, 8)
                self.den = ar.f32(2, H0)
                self.am = ar.f32(2, G)
                self.amT = ar.f16(2, S)
                self.f = xn[:, 0:2, :].rearrange("p a b -> p (a b)")
                self.xl = xn[:, 2, :]
                self.uh = ar.f16(2, 2, D)
                self.mb = ar.f32(B, G)
                assert ar.at <= ystart + NT * D
                self.s_z = sem("a0_zero_ready")
                self.s_f = sem("a0_pe_done")
                self.s_hi = sem("a0_hi_done")
                self.s_lo = sem("a0_dve_done")
                self.s_arg = sem("a0_exp_arg")
                self.s_ex = sem("a0_exp_done")
                self.s_ff = sem("a0_film_full")
                self.s_fr = credit("a0_film_free", 2)
                self.s_u = sem("a0_u_ready")
                self.s_r = sem("a0_u_reversed")
                self.s_uc = credit("a0_u_copied", 2)

            def w0(self, at, n, rows_=P):
                return lambda h: wsp[0:rows_, J_X0 % 2, h, at:at + n]

            def pe_part(self):
                pe.wait_ge(s_w, J_X0 + 1)
                pe.wait_ge(self.s_z, 1)
                self.walk(pe.Fori, self.pe_batch, self.pe_film)

            def walk(self, fori, batch, film):
                batch(0, None)
                with fori(0, B - 1) as i:
                    batch(i + 1, lambda t: film(i, t))
                for t in range(2):
                    film(B - 1, t)

            def pe_batch(self, i, film):
                def cx(k):
                    return lambda h: ctxs[:, h, k, bass.ds(i * G, G)]
                pe.wait_ge(self.s_fr, 2 * i + 2 if film is None else 2 * i)
                pe.wait_ge(self.s_uc, 2 * i + 2 if film is None else 2 * i)
                for k in range(KC):
                    mm3(ps[:, 0, 0:G], self.w0(2304 + k * P, P, CP), cx(k), k == 0, k == KC - 1)
                for k in range(KC):
                    mm3(ps[0:G, 1, 0:D], cx(k), self.w0(2304 + 256 + k * D, D, CP), k == 0, k == KC - 1)
                for k in range(KD):
                    m = mm3(ps[:, 2, 0:S], self.w0(k * P, P), lambda h: xT[:, h, k, bass.ds(i * S, S)],
                            k == 0, k == KD - 1)
                m.then_inc(self.s_f, 1)
                pe.wait_ge(self.s_lo, 4 * i + 1)
                for t in range(2):
                    m = mm3(ps[:, 3 + t, 0:H0 * G], lambda h: self.q[:, h, t * P:(t + 1) * P],
                            lambda h: self.k[:, h, :], True, True)
                m.then_inc(self.s_f, 1)
                if film:
                    for t in range(2):
                        film(t)
                pe.wait_ge(self.s_lo, 4 * i + 2)
                for t in range(2):
                    m = pe.transpose(ps[0:G, 5, t * P:(t + 1) * P], self.am[:, t, :], ident)
                m.then_inc(self.s_f, 1)
                pe.wait_ge(self.s_lo, 4 * i + 3)
                for c in range(KD):
                    m = mm3(ps[:, 6, c * S:(c + 1) * S], lambda h: self.v[0:G, h, c * P:(c + 1) * P],
                            lambda h: self.amT[0:G, h, :], True, True)
                m.then_inc(self.s_f, 1)

            def pe_film(self, i, t):
                pe.wait_ge(self.s_lo, 4 * i + 4)
                pe.wait_ge(self.s_fr, 2 * i + t + 1)
                for k in range(KD):
                    m = mm3(ps[:, 7 if t == 0 else 0, :], lambda h: xT[:, h, k, bass.ds(i * S + t * P, P)],
                            self.w0(256 + k * 2 * D, 2 * D), k == 0, k == KD - 1)
                m.then_inc(self.s_ff, 1)
                pe.wait_ge(self.s_u, 2 * i + t + 1)
                pe.wait_ge(self.s_uc, 2 * i + t + 1)
                pe.matmul(ps[:, 1 + t, :], rev[:], self.uh[:, t].rearrange("p h d -> p (h d)"),
                          start=True, stop=True).then_inc(self.s_r, 1)

            def kblocks(self, h):
                return [(self.k[DH0 * b:DH0 * (b + 1), h, b * G:(b + 1) * G], ps[DH0 * b:DH0 * (b + 1), 0, 0:G])
                        for b in range(H0)]

            def act_part(self):
                act.wait_ge(self.s_z, 1)
                self.walk(act.Fori, self.act_batch, self.act_film)

            def act_batch(self, i, film):
                act.wait_ge(self.s_f, 4 * i + 1)
                for o, v in self.kblocks(0):
                    act.activation(o, v, ACT.Copy, scale=INV)
                act.activation(self.v[0:G, 0, :], ps[0:G, 1, 0:D], ACT.Copy, scale=INV)
                act.activation(self.q[:, 0, :], ps[:, 2, 0:S], ACT.Copy, scale=INV).then_inc(self.s_hi, 1)
                if film:
                    for t in range(2):
                        film(t)
                act.wait_ge(self.s_arg, i + 1)
                act.activation(self.s[:], self.s[:], ACT.Exp, scale=DH0 ** -0.5)
                act.activation(self.w[:], self.w[:], ACT.Exp, scale=DH0 ** -0.5).then_inc(self.s_ex, 1)
                act.wait_ge(self.s_f, 4 * i + 3)
                act.activation(self.amT[0:G, 0, :], ps[0:G, 5, 0:S], ACT.Copy).then_inc(self.s_hi, 1)
                act.wait_ge(self.s_f, 4 * i + 4)
                settled(act)
                act.activation(xT[:, 0, :, bass.ds(i * S, S)], shaped(ps[:, 6, :], (KD, S)), ACT.Copy)\
                    .then_inc(self.s_hi, 1)

            def act_film(self, i, t):
                act.wait_ge(self.s_r, 2 * i + t + 1)
                settled(act)
                act.activation(u[:, :, 2 * i + t, :], shaped(ps[:, 1 + t, :], (2, D)), ACT.Copy)\
                    .then_inc(self.s_uc, 1)

            def dve_part(self):
                dve.wait_ge(s_rows, N_ROWS)
                dve.tensor_copy(self.mb[:].rearrange("p a b -> p (a b)"), mk8[:])
                dve.tensor_copy(tmk[:], tm8[:])
                dve.memset(self.k[:].rearrange("p a b -> p (a b)"), 0.0)
                dve.drain()
                dve.tensor_scalar(self.mb[:], self.mb[:], -NEG, NEG, ALU.mult, ALU.add)
                dve.tensor_scalar(tmk[:], tmk[:], 1.0 / H0, None, ALU.mult)
                dve.tensor_scalar(row(R_FI, 4 * D), row(R_FI, 4 * D), sc[:, 8:9], None, ALU.mult)
                dve.drain()
                dve.tensor_scalar(row(R_FI), row(R_FI), 1.0, None, ALU.add)
                dve.tensor_scalar(row(R_FO), row(R_FO), 1.0, None, ALU.add)
                dve.tensor_scalar(sm[:, 4, 1:2], sc[:, 8:9], INV, None, ALU.mult)
                dve.drain().then_inc(self.s_z, 1)
                self.walk(dve.Fori, self.dve_batch, self.dve_film)

            def dve_batch(self, i, film):
                dve.wait_ge(self.s_hi, 3 * i + 1)
                for (o, v), (oh, _) in zip(self.kblocks(1), self.kblocks(0)):
                    dve.scalar_tensor_tensor(o, v, INV, oh, ALU.mult, ALU.subtract)
                dve.scalar_tensor_tensor(self.v[0:G, 1, :], ps[0:G, 1, 0:D], INV, self.v[0:G, 0, :], ALU.mult, ALU.subtract)
                dve.scalar_tensor_tensor(self.q[:, 1, :], ps[:, 2, 0:S], INV, self.q[:, 0, :], ALU.mult, ALU.subtract)\
                    .then_inc(self.s_lo, 1)
                dve.drain()
                dve.wait_ge(self.s_f, 4 * i + 2)
                for t in range(2):
                    dve.tensor_tensor(self.s[:, t], shaped(ps[:, 3 + t, 0:H0 * G], (H0, G)),
                                      self.mb[:, bass.ds(i, 1), :].to_broadcast([P, H0, G]), ALU.add)
                dve.drain()
                for r in range(KTOP // 8):
                    src = self.s if r == 0 else self.w
                    mx = self.m1 if r == 0 else self.m2
                    for t in range(2):
                        for h in range(H0):
                            dve.max(mx[:, t, h, :], src[:, t, h, :])
                    dve.drain()
                    for t in range(2):
                        for h in range(H0):
                            dve.match_replace(self.w[:, t, h, :], mx[:, t, h, :], src[:, t, h, :], NEG)
                    dve.drain()
                    if film and r < 2:
                        film(r)
                mx = self.m1[:, :, :, 0:1].to_broadcast([P, 2, H0, G])
                dve.tensor_tensor(self.s[:], self.s[:], mx, ALU.subtract)
                dve.tensor_tensor(self.w[:], self.w[:], mx, ALU.subtract)
                dve.drain().then_inc(self.s_arg, 1)
                dve.wait_ge(self.s_ex, i + 1)
                dve.tensor_tensor(self.s[:], self.s[:], self.w[:], ALU.subtract)
                dve.drain()
                dve.tensor_reduce(self.den[:], self.s[:], X, ALU.add)
                dve.drain()
                dve.reciprocal(self.den[:], self.den[:])
                dve.drain()
                for t in range(2):
                    dve.tensor_scalar(self.den[:, t, :], self.den[:, t, :], tmk[:, bass.ds(2 * i + t, 1)], None, ALU.mult)
                dve.drain()
                dve.tensor_tensor(self.s[:], self.s[:], self.den[:].unsqueeze(3).to_broadcast([P, 2, H0, G]), ALU.mult)
                dve.drain()
                dve.tensor_reduce(self.am[:], self.s[:].rearrange("p t h g -> p t g h"), X, ALU.add)
                dve.drain().then_inc(self.s_lo, 1)
                dve.wait_ge(self.s_hi, 3 * i + 2)
                dve.tensor_tensor(self.amT[0:G, 1, :], ps[0:G, 5, 0:S], self.amT[0:G, 0, :], ALU.subtract)\
                    .then_inc(self.s_lo, 1)
                dve.wait_ge(self.s_hi, 3 * i + 3)
                dve.tensor_tensor(xT[:, 1, :, bass.ds(i * S, S)], shaped(ps[:, 6, :], (KD, S)),
                                  xT[:, 0, :, bass.ds(i * S, S)], ALU.subtract).then_inc(self.s_lo, 1)

            def dve_film(self, i, t):
                tt_ = 2 * i + t
                dve.drain()
                dve.wait_ge(self.s_ff, tt_ + 1)
                dve.tensor_scalar(self.xl, xtext[:, tt_, :], mean[:, bass.ds(tt_, 1)], rstd[:, bass.ds(tt_, 1)],
                                  ALU.subtract, ALU.mult)
                dve.scalar_tensor_tensor(self.f, ps[:, 7 if t == 0 else 0, :], sm[:, 4, 1:2], row(R_FI, 2 * D),
                                         ALU.mult, ALU.add).then_inc(self.s_fr, 1)
                dve.drain()
                dve.tensor_tensor(self.xl, self.xl, row(R_GIN), ALU.mult)
                dve.drain()
                dve.tensor_tensor(self.xl, self.xl, row(R_BIN), ALU.add)
                dve.drain()
                dve.tensor_tensor(self.xl, self.xl, self.f[:, 0:D], ALU.mult)
                dve.drain()
                dve.tensor_tensor(self.xl, self.xl, self.f[:, D:2 * D], ALU.add)
                dve.drain()
                dve.tensor_copy(self.uh[:, t, 0, :], self.xl)
                dve.drain()
                dve.tensor_tensor(self.uh[:, t, 1, :], self.xl, self.uh[:, t, 0, :], ALU.subtract)\
                    .then_inc(self.s_u, 1)

        class Conv:
            def __init__(self):
                self.s_t = [sem(f"toeplitz_loaded_{r}") for r in range(TR)]
                self.s_tfree = credit("toeplitz_used", TR)
                self.s_y = sem("conv_full")
                self.s_yfree = credit("conv_bank_free", TR)
                self.s_ff = sem("film_out_full")
                self.s_ffree = credit("film_out_free", 2)
                self.f = xn[:].rearrange("p a b -> p (a b)")[:, 0:2 * D]

            def sp_part(self, sp):
                with sp.Fori(0, D // TG // TR) as i:
                    for par in range(TR):
                        g = TR * i + par
                        sp.wait_ge(self.s_tfree, g + 1)
                        src = bass.AP(tensor=kdram.tensor, offset=g * (TG * KROW * 2),
                                      ap=[[2, P], [KROW * 2, TG], [1, 2 * S]])
                        sp.dma_start(tz[:, par].rearrange("p d l c -> p d (l c)"), src).then_inc(self.s_t[par], 16)

            def pe_part(self):
                with pe.Fori(0, D // TG // TR) as i:
                    for par in range(TR):
                        g = TR * i + par
                        pe.wait_ge(self.s_t[par], 16 * (i + 1))
                        pe.wait_ge(self.s_yfree, g + 1)
                        for k in range(TG):
                            d = g * TG + k
                            o = ps[:, par, k * NT:(k + 1) * NT]

                            def uu(h, a0=0, st=1):
                                return u[:, h, a0::st, bass.ds(d, 1)].rearrange("p t o -> p (t o)")

                            mm3(o, lambda h: tz[:, par, k, 0:P, h], lambda h: uu(h), True, True)
                            for a_, b_ in ((0, 0), (0, 1), (1, 0)):
                                m = pe.matmul(o[:, 1::2], tz[:, par, k, P:2 * P, a_], uu(b_, 0, 2), start=False,
                                              stop=True, skip_group_check=True)
                        m.then_inc(self.s_y, 1)
                        pe.drain().then_inc(self.s_tfree, 1)
                with pe.Fori(0, NT // 2) as i:
                    for par in range(2):
                        t = 2 * i + par
                        pe.wait_ge(self.s_ffree, t + 1)
                        for k in range(KD):
                            m = mm3(ps[:, 4 + par, :], lambda h: xT[:, h, k, bass.ds(t * P, P)],
                                    lambda h: wsp[:, J_X0 % 2, h, 1280 + k * 2 * D:1280 + (k + 1) * 2 * D], k == 0, k == KD - 1)
                        m.then_inc(self.s_ff, 1)
                pe.drain().then_inc(s_wfree, 1)

            def dve_part(self):
                with dve.Fori(0, D // TG // TR) as i:
                    for par in range(TR):
                        g = TR * i + par
                        dve.wait_ge(self.s_y, g + 1)
                        dve.tensor_copy(y[:, :, bass.ds(g * TG, TG)].rearrange("p t d -> p d t"),
                                        shaped(ps[:, par, 0:TG * NT], (TG, NT))).then_inc(self.s_yfree, 1)
                dve.drain()
                f = self.f
                with dve.Fori(0, NT // 2) as i:
                    for par in range(2):
                        t = 2 * i + par
                        dve.wait_ge(self.s_ff, t + 1)
                        dve.scalar_tensor_tensor(f, ps[:, 4 + par, :], sm[:, 4, 1:2], row(R_FO, 2 * D), ALU.mult, ALU.add)\
                            .then_inc(self.s_ffree, 1)
                        dve.drain()
                        dve.tensor_tensor(y[:, t, :], y[:, t, :], f[:, 0:D], ALU.mult)
                        dve.drain()
                        dve.tensor_tensor(y[:, t, :], y[:, t, :], f[:, D:2 * D], ALU.add)
                        dve.drain()
                        dve.tensor_tensor(y[:, t, :], y[:, t, :], xtext[:, t, :], ALU.add)
                        dve.drain()

        s_rows = sem("rows_loaded")
        N_CONST, N_ROWS = 16 * 9, 16
        stage = [0]

        def finish_stage():
            n = stage[0]
            prog["dve"].append(lambda: barrier(dve, 2, n))
            prog["act"].append(lambda: barrier(act, 1, n))
            prog["pe"].append(lambda: barrier(pe, 0, n))
            stage[0] += 1

        def norm(n):
            norm_stage(n, stage[0])
            stage[0] += 1

        kg = KGen()
        prog["dve"].append(kg.dve_part)
        prog["act"].append(kg.act_part)
        prog["pe"].append(kg.pe_part)
        prog["dve"].append(lambda: dve.wait_ge(kg.s_kd, 160))
        finish_stage()
        prog["dve"].append(lambda: dve.wait_ge(s_x, 16))
        prog["pe"].append(lambda: pe.wait_ge(s_cdone, 1))
        prog["act"].append(lambda: act.wait_ge(s_cdone, 1))
        norm(Norm("n0", x, keep=xtext))
        inner_stats = Norm("n0in", xtext)
        prog["dve"].append(inner_stats.dve_stats)
        prog["act"].append(inner_stats.act_stats)
        a0 = Attn0()
        prog["dve"].append(a0.dve_part)
        prog["act"].append(a0.act_part)
        prog["pe"].append(a0.pe_part)
        finish_stage()
        cv = Conv()
        prog["dve"].append(cv.dve_part)
        prog["pe"].append(cv.pe_part)
        finish_stage()
        norm(Norm("n0f", y, affine=(row(R_GF), row(R_BF))))
        no_weight = lambda t, e, j: INV
        mlp_up = lambda w, g, k, j: w[:, k * 1024 + j * P:k * 1024 + (j + 1) * P]
        mlp_down = lambda w, j: w[:, 2048 + j * D:2048 + (j + 1) * D]
        f0 = Ffn("mlp0", J_F0, 0, [P] * 8, ACT.Gelu, mlp_up, mlp_down, False, 0, 0, no_weight, y, single=True)
        prog["dve"].append(f0.dve_part)
        prog["act"].append(f0.act_part)
        prog["pe"].append(f0.pe_part)
        last0 = Norm("n0out", y)

        def out0():
            dve.drain()
            last0.dve_stats()
            with dve.Fori(0, NT) as t:
                last0.normalise(xn[:, 0], t)
                dve.drain()
                dve.tensor_tensor(xn[:, 0], xn[:, 0], row(R_GOUT), ALU.mult)
                dve.drain()
                dve.tensor_tensor(xn[:, 0], xn[:, 0], row(R_BOUT), ALU.add)
                dve.drain()
                dve.scalar_tensor_tensor(x[:, t, :], xn[:, 0], tg[:, 0:1], x[:, t, :], ALU.mult, ALU.add)
                dve.drain()
        prog["dve"].append(out0)
        prog["act"].append(last0.act_stats)
        finish_stage()

        def route(layer):
            r = Route(f"route{layer}", layer)
            prog["dve"].append(r.dve_part)
            prog["act"].append(r.act_part)
            prog["pe"].append(r.pe_part)
            finish_stage()
            return r

        def experts(F, dense=None):
            def dve_part():
                F.walk(dve.Fori, DispatchedDVE(F))
                DispatchedDVE(F).combine()

            def either(eng, sparse, full):
                if dense is None:
                    return sparse()
                with eng.If(fits_of(eng, F.route.layer)):
                    sparse()
                with eng.Else():
                    full()
            prog["dve"].append(lambda: either(dve, dve_part, dense and dense.dve_part))
            prog["act"].append(lambda: either(act, lambda: F.walk(act.Fori, DispatchedACT(F)), dense and dense.act_part))
            prog["pe"].append(lambda: either(pe, lambda: F.walk(pe.Fori, DispatchedPE(F)), dense and dense.pe_part))

        def ffn(f):
            prog["dve"].append(f.dve_part)
            prog["act"].append(f.act_part)
            prog["pe"].append(f.pe_part)

        by_expert = lambda t, e, j: wgt[:, bass.ds(t, 1), bass.ds(e, 1)].rearrange("p a b -> p (a b)")
        s_xz = sem("slots_cleared")
        norm(Norm("n0e", x, keep=Area(ROUTE_END).f32(NT, D)))
        e0 = Dispatched("moe0", J_E0, [P] * 8, ACT.Relu, mlp_up, mlp_down, False, 8, 1, route(0), ROUTE_END)
        experts(e0)
        finish_stage()

        norm(Norm("n1", x, keep=Area(ROUTE_END).f32(NT, D)))
        attn_stage(Attn("a1", J_X1, J_X1 + 1, 1024, 64, 1, False), stage[0])
        stage[0] += 1
        norm(Norm("n1e", x, keep=Area(ROUTE_END).f32(NT, D)))
        e1 = Dispatched("moe1", J_E1, [P] * 8, ACT.Gelu, mlp_up, mlp_down, False, 72, 9, route(1), ROUTE_END)
        experts(e1, Ffn("dense1", J_E1, 4, [P] * 8, ACT.Gelu, mlp_up, mlp_down, False, 72, 9, by_expert, x))
        finish_stage()

        norm(Norm("n2", x, keep=Area(ROUTE_END).f32(NT, D)))
        attn_stage(Attn("a2", J_X2, J_X2 + 1, 1024, 128, 2, True), stage[0])
        stage[0] += 1
        norm(Norm("n2e", x, keep=Area(ROUTE_END).f32(NT, D)))
        cols2 = [P] * 5 + [64]
        up2 = lambda w, g, k, j: w[:, g * 1408 + k * 704 + j * P:g * 1408 + k * 704 + j * P + cols2[j]]
        down2 = lambda w, j: w[:, 2816 + j * D:2816 + (j + 1) * D]
        e2 = Dispatched("moe2", J_E2, cols2, ACT.Silu, up2, down2, True, None, None, route(2), ROUTE_END, before=e0)
        experts(e2, Ffn("dense2", J_E2, 4, cols2, ACT.Silu, up2, down2, True, None, None, by_expert, x))
        finish_stage()

        norm(Norm("n3", x, keep=Area(ROUTE_END).f32(NT, D)))
        attn_stage(Attn("a3", J_X3, J_X3, 512, 64, 3, False), stage[0])
        stage[0] += 1
        norm(Norm("n3e", x, keep=Area(ROUTE_END).f32(NT, D)))
        route(3)
        up3s = lambda w, g, k, j: w[:, g * 1024 + k * 512 + j * P:g * 1024 + k * 512 + (j + 1) * P]
        down3s = lambda w, j: w[:, 2048 + j * D:2048 + (j + 1) * D]
        shared = lambda t, e, j: wgt[:, bass.ds(t, 1), 16:17].rearrange("p a b -> p (a b)")
        ffn(Ffn("shared3", J_SH, 0, [P] * 4, ACT.Silu, up3s, down3s, True, None, None, shared, x, single=True))
        finish_stage()
        up3 = lambda w, g, k, j: w[:, 768 * j + g * D + k * P:768 * j + g * D + (k + 1) * P]
        down3 = lambda w, j: w[:, 768 * j + 512:768 * (j + 1)]
        by_pack = lambda t, e, j: wgt[:, bass.ds(t, 1), bass.ds(4 * e + j, 1)].rearrange("p a b -> p (a b)")
        ffn(Ffn("moe3", J_E3, 2, [P] * 4, ACT.Silu, up3, down3, True, None, None, by_pack, x, each=True))
        finish_stage()

        FULL = [("w", P, 0, 4096)]
        JOBS = [(J_X0, 1, [("wx0", P, 0, 2304), ("wx0c", CP, 2304, 768)]),
                (J_F0, 1, [("wf0", P, 0, 4096)]),
                (J_E0, 8, [("we0", P, 0, 4096)]),
                (J_X1, 1, [("wx1", P, 0, 4096)]),
                (J_X1 + 1, 1, [("wx1c", CP, 0, 4096)]),
                (J_E1, 8, [("we1", P, 0, 4096)]),
                (J_X2, 1, [("wx2", P, 0, 4096)]),
                (J_X2 + 1, 1, [("wx2c", CP, 0, 4096)]),
                (J_E2, 8, [("we2", P, 0, 4096), ("we2r", 64, 4096, 256)]),
                (J_X3, 1, [("wx3", P, 0, 2048), ("wx3c", CP, 2048, 2048)]),
                (J_SH, 1, [("ws3", P, 0, 3072)]),
                (J_E3, 4, [("we3", P, 0, 3072)])]

        landed = {0: 0, 1: 0}
        plan = []
        for j0, n, pieces in JOBS:
            base = dict(landed)
            plan.append((j0, n, pieces, base))
            for j in range(n):
                landed[(j0 + j) % 2] += 16 * len(pieces)

        def job_loop(fori, j0, n, body, middle=None):
            if n == 1:
                body(j0, j0 % 2, 0, 0)
            else:
                if middle is not None:
                    for off in range(2):
                        body(j0 + off, (j0 + off) % 2, off, 0)
                    middle()
                with fori(0 if middle is None else 1, n // 2) as i:
                    for off in range(2):
                        body(2 * i + (j0 + off), (j0 + off) % 2, 2 * i + off, i)

        tmpw = wsp[:, 1].rearrange("p h n -> p (h n)").bitcast(F32)
        ctxr = tmpw[0:CP, 0:KC * GA]
        rwr = tmpw[:, KC * GA:KC * GA + NRC]
        b2r = raw[0:33, 1, :]
        s_tmp = sem("temporaries_loaded")
        s_zero = sem("skip_cleared")

        @block.sync
        def _(sp):
            sp.dma_start(cst[:], a["cst"]).then_inc(s_const, 16)
            sp.dma_start(xT[:].rearrange("p a b c -> p (a b c)")[:, 0:8 * D].bitcast(F32), a["s4"]).then_inc(s_const, 16)
            sp.dma_start(LDT, a["ldt"].partition_broadcast(P)).then_inc(s_const, 16)
            sp.dma_start(sc[:], a["sc"].partition_broadcast(P)).then_inc(s_const, 16)
            sp.dma_start(mk8[:], a["cmask"].partition_broadcast(P)).then_inc(s_const, 16)
            sp.dma_start(tm8[:], a["tmask"]).then_inc(s_const, 16)
            sp.wait_ge(s_zero, 1)
            sp.dma_start(dsk[0:P:16, :], a["dskip"]).then_inc(s_const, 16)
            sp.dma_start(b1c[:], a["b1"]).then_inc(s_const, 16)
            sp.dma_start(brow[:].rearrange("p a b -> p (a b)"), a["brow"].partition_broadcast(P)).then_inc(s_const, 16)
            sp.dma_start(ctxr, a["ctx"]).then_inc(s_tmp, 16)
            sp.dma_start(rwr, a["wr"]).then_inc(s_tmp, 16)
            for r in (0, 32):
                sp.dma_start(b2r[r:r + 1], a["b2"]).then_inc(s_tmp, 16)
            sp.dma_start(x[:], a["x"]).then_inc(s_x, 16)

            def load(job, slot, e, seen, pieces, family):
                if not (isinstance(job, int) and job < 2):
                    sp.wait_ge(s_w, job - 1)
                elif job == 1:
                    sp.wait_ge(s_cdone, 1)
                for name, rows_, at, n in pieces:
                    src = a[name] if not family else a[name][bass.ds(e, 1)].rearrange("e p n -> (e p) n")
                    sp.dma_start(raw[0:rows_, slot, at:at + n], src).then_inc(s_raw[slot], 16)

            for j0, n, pieces, base in plan:
                if j0 == J_E0:
                    kg.store(sp)
                    for s in s_end:
                        sp.wait_ge(s, 1)
                    sp.dma_start(rows[:], a["rows"].partition_broadcast(P)).then_inc(s_rows, 16)
                    cv.sp_part(sp)
                job_loop(sp.Fori, j0, n, lambda j, s, e, seen: load(j, s, e, seen, pieces, n > 1))
            for s in s_end:
                sp.wait_ge(s, stage[0])
            sp.dma_start(out, x[:]).then_inc(s_out, 16)
            sp.wait_ge(s_out, 16)

        @block.gpsimd
        def _(pool):
            start_carrier(pool)
            pool.memset(dsk[:], 0.0).then_inc(s_zero, 1)
            for col, (s, n) in enumerate(credits):
                pool.memset(spare[:, col:col + 1], 0.0).then_inc(s, n)
            pool.memset(ones[:], 1.0)
            pool.memset(eps_t[:], EPS)
            pool.memset(b2s[:].rearrange("p a b -> p (a b)"), 0.0)
            pool.wait_ge(s_const, N_CONST)
            pool.tensor_copy(tri[:], cst[:, C_TRI:C_TRI + P])
            pool.tensor_copy(rev[:], cst[:, C_REV:C_REV + P])
            pool.wait_ge(s_tmp, 64)
            n_step = [0]

            def step(i):
                n_step[0] += 1
                i.then_inc(s_pst, 1)
                pool.wait_ge(s_pst, n_step[0])
            ch = [ctxs[:, h].rearrange("p k n -> p (k n)") for h in range(2)]
            step(pool.tensor_copy(ch[0], ctxr))
            pool.tensor_tensor(ch[1], ctxr, ch[0], ALU.subtract)
            step(pool.tensor_scalar(rwr, rwr, WSCALE, 1.0, ALU.mult, ALU.mult))
            step(pool.tensor_copy(rws[:, 0], rwr))
            pool.tensor_tensor(rws[:, 1], rwr, rws[:, 0], ALU.subtract)
            b2f = b2s[:].rearrange("p a b -> p (a b)")
            for r in (0, 32):
                step(pool.tensor_scalar(b2r[r:r + 1], b2r[r:r + 1], WSCALE, 1.0, ALU.mult, ALU.mult))
                step(pool.tensor_copy(b2f[r:r + 1], b2r[r:r + 1]))
            step(pool.tensor_tensor(b2f[32:33], b2r[32:33], b2f[32:33], ALU.subtract))
            pool.drain().then_inc(s_cdone, 1)
            steps_done = n_step[0]

            for j0, n, pieces, base in plan:
                def split(j, slot, e, seen):
                    pool.wait_ge(s_raw[slot], base[slot] + 16 * len(pieces) * (seen + 1))
                    if not (isinstance(j, int) and j < 2):
                        pool.wait_ge(s_wfree, j - 1)
                    pool.tensor_tensor(spare[:, 63:64], spare[:, 0:1], spare[:, 0:1], ALU.mult)
                    for _, rows_, at, w in pieces:
                        v = raw[0:rows_, slot, at:at + w]
                        hi, lo = (wsp[0:rows_, slot, h, at:at + w] for h in range(2))
                        pool.tensor_scalar(v, v, WSCALE, 1.0, ALU.mult, ALU.mult)
                        pool.drain()
                        pool.tensor_copy(hi, v)
                        pool.drain()
                        pool.tensor_tensor(lo, v, hi, ALU.subtract)
                    pool.drain().then_inc(s_w, 1)
                moe = {J_E0: e0, J_E1: e1, J_E2: e2}.get(j0)
                moe = moe and DispatchedPool(moe, pool)
                job_loop(pool.Fori, j0, n, split, moe and (lambda: moe.if_fits(moe.scatter)))
                if moe:
                    moe.if_fits(moe.gather)

        @block.tensor
        def _(_pe):
            start_carrier(pe)
            for part in prog["pe"]:
                part()

        @block.scalar
        def _(_act):
            start_carrier(act)
            for part in prog["act"]:
                part()

        @block.vector
        def _(_dve):
            for part in prog["dve"]:
                part()


def kernel(**inputs):
    import numpy as np
    import concourse.bacc as bacc
    from concourse.bass_utils import run_bass_kernel_spmd as run

    g = {k: np.asarray(v) for k, v in inputs.items()}
    c = np.ascontiguousarray

    def kp(w, rows=P):
        k, n = w.shape
        return w.reshape(k // rows, rows, n).transpose(1, 0, 2).reshape(rows, -1)

    def cat(*parts):
        return c(np.concatenate(parts, axis=-1))

    cst = np.zeros((P, NCST), np.float32)
    r = np.arange(P)
    cst[:, 0:P] = np.eye(P)
    cst[:, C_TRI:C_TRI + P] = r[:, None] < r[None, :]
    cst[:, C_IOTA:C_IOTA + 16] = np.arange(16)
    cst[:, C_K16:C_K16 + 16] = 16 * np.arange(16)
    cst[:, C_MASK:C_MASK + 8] = (r[:, None] // 16) == np.arange(8)
    cst[:, C_REV:C_REV + P] = np.eye(P)[::-1]
    cst[:, C_SPARE:C_SPARE + 2 * NT] = DROPPED + P * np.arange(2 * NT) + r[:, None]
    ph = np.where(r[:, None] < 64, [[0.25, 0.25, 0.5]], [[0.5, 0.0, 0.25]])
    cst[:, C_PH:C_PH + 3] = ph
    cst[:, C_PHR:C_PHR + 3] = ph * -SIN_SCALE
    a = {"cst": cst}
    a["x"] = c(g["x"].reshape(NT, P, D).transpose(1, 0, 2))
    a["ctx"] = c(kp(g["ctx_768"].reshape(GA, DV).T, CP))
    a["s4"] = c(np.tile(np.concatenate([g["L0_xattn_" + n].T for n in ("A_re", "A_im", "C_re", "C_im")], axis=1), (2, 1)))
    a["ldt"] = c(g["L0_xattn_log_dt"])
    a["sc"] = cat(g["g_xattn"], g["g_ffn"], g["L0_xattn_mod_gate"].reshape(1), g["L1_ffn_br"])
    a["cmask"] = c(g["mask_BxS2_bf1"].reshape(GA).view(np.uint8))
    a["tmask"] = c(g["mask_BxS_bf1"].reshape(NT, P).T.view(np.uint8))
    a["dskip"] = c(g["L0_xattn_D_skip"].reshape(D // 8, 8).T)
    a["b1"] = cat(g["L0_xattn_b1"].reshape(8, P).T, g["L0_ffn_b1"].reshape(64, P).T, g["L1_ffn_b1"].reshape(64, P).T)
    a["brow"] = cat(g["L1_xattn_b_out"], g["L2_xattn_bout"], g["L3_xattn_bo"])
    a["wr"] = cat(kp(g["L0_ffn_w_router"]), kp(g["L1_ffn_Wr"]), kp(g["L2_ffn_router_w"].T),
                  kp(np.concatenate([g["L3_ffn_Wg"].T, g["L3_ffn_Wsg"].T], axis=1)))
    a["b2"] = cat(g["L0_xattn_b2"].reshape(1, -1), g["L0_ffn_b2"].reshape(1, -1), g["L1_ffn_b2"].reshape(1, -1))
    L0x = lambda n: g["L0_xattn_" + n]
    a["rows"] = cat(*(L0x(n) for n in ("g_norm_in", "b_norm_in", "g_ffn", "b_ffn", "g_norm_out", "b_norm_out",
                                       "b_film_in", "b_film_out")))
    a["wx0"] = cat(kp(L0x("Wq")), kp(L0x("W_film_in")), kp(L0x("W_film_out")))
    a["wx0c"] = cat(kp(L0x("Wk"), CP), kp(L0x("Wv"), CP))
    a["wf0"] = cat(kp(L0x("W1")), kp(L0x("W2")))
    a["we0"] = c(np.stack([cat(kp(g["L0_ffn_w1"][e]), kp(g["L0_ffn_w2"][e])) for e in range(8)]))
    a["wx1"] = cat(kp(g["L1_xattn_w_q"]), kp(g["L1_xattn_w_out"]))
    a["wx1c"] = cat(kp(g["L1_xattn_w_k"], CP), kp(g["L1_xattn_w_v"], CP))
    a["we1"] = c(np.stack([cat(kp(g["L1_ffn_W1"][e]), kp(g["L1_ffn_W2"][e])) for e in range(8)]))
    a["wx2"] = cat(kp(g["L2_xattn_Wq"]), kp(g["L2_xattn_Wout"]))
    a["wx2c"] = cat(kp(g["L2_xattn_Wk"], CP), kp(g["L2_xattn_Wv"], CP))
    a["we2"] = c(np.stack([cat(kp(g["L2_ffn_gate_w"][e].T), kp(g["L2_ffn_up_w"][e].T),
                               kp(g["L2_ffn_down_w"][e].T[0:640])) for e in range(8)]))
    a["we2r"] = c(np.stack([g["L2_ffn_down_w"][e].T[640:704] for e in range(8)]))
    a["wx3"] = cat(kp(g["L3_xattn_Wq"]), kp(g["L3_xattn_Wo"]))
    a["wx3c"] = cat(kp(g["L3_xattn_Wk"], CP), kp(g["L3_xattn_Wv"], CP))
    a["ws3"] = cat(kp(g["L3_ffn_Ws_gate"].T), kp(g["L3_ffn_Ws_up"].T), kp(g["L3_ffn_Ws_down"].T))
    a["we3"] = c(np.stack([cat(*(v for e in range(4 * p, 4 * p + 4) for v in (
        kp(g["L3_ffn_We_gate"][e].T), kp(g["L3_ffn_We_up"][e].T), g["L3_ffn_We_down"][e].T))) for p in range(4)]))

    nc = bacc.Bacc("TRN2", target_bir_lowering=False, num_devices=1)
    aps = {n: nc.dram_tensor("in_" + n, v.shape, mybir.dt.from_np(v.dtype), kind="ExternalInput").ap()
           for n, v in a.items()}
    o = nc.dram_tensor("out_x", (P, NT, D), F32, kind="ExternalOutput").ap()
    build(nc, aps, o)
    res = run(nc, [{"in_" + n: v for n, v in a.items()}], core_ids=[0])
    return c(res.results[0]["out_x"].transpose(1, 0, 2).reshape(B, S, D))
```
